# Optimizing a Trainium2 kernel written in Bass

```python
import numpy as np
import jax
import jax.numpy as jnp

def _softmax(x, axis=-1):
    return jax.nn.softmax(x, axis=axis)

def _gelu(x):
    return jax.nn.gelu(x, approximate=True)

def _silu(x):
    return jax.nn.silu(x)

def _sigmoid(x):
    return jax.nn.sigmoid(x)

def _layernorm(x, axis=-1, eps=1e-05):
    m = jnp.mean(x, axis=axis, keepdims=True)
    v = jnp.var(x, axis=axis, keepdims=True)
    return (x - m) / jnp.sqrt(v + eps)

def _scatter_add(tgt, idx, src, axis=0):
    return tgt.at[idx].add(src)

def _segment_sum(src, seg, n):
    return jax.ops.segment_sum(src, seg, n)
kernel_name = 'mk_gnn_preln_d4_gnn_r64_dde08f'

def setup_inputs(seed: int=0):
    np.random.seed(seed)
    _w = jnp.asarray

    def _rec_inputs():
        import jax
        import jax.numpy as jnp
        _gk = jax.random.key(seed)
        x = -0.0003713 + 1 * jax.random.normal(jax.random.fold_in(_gk, 1), (100000, 128), jnp.float32)
        src = jax.random.randint(jax.random.fold_in(_gk, 2), (50000,), 0, 100000, jnp.int32)
        dst = jax.random.randint(jax.random.fold_in(_gk, 3), (50000,), 0, 100000, jnp.int32)
        _o = jnp.argsort(dst, stable=True)
        src = src[_o]
        dst = dst[_o]
        edge_attr_64 = -8.16379e-05 + 0.999858 * jax.random.normal(jax.random.fold_in(_gk, 12), (50000, 64), jnp.float32)
        edge_type_64 = jax.random.randint(jax.random.fold_in(_gk, 14), (50000,), 0, 64, jnp.int32)
        edge_weight = 6.14103e-05 + 0.0999867 * jax.random.normal(jax.random.fold_in(_gk, 15), (50000,), jnp.float32)
        return (x, src, dst, edge_attr_64, edge_type_64, edge_weight)
    x, src, dst, edge_attr_64, edge_type_64, edge_weight = _rec_inputs()

    def _L0_gnn_setup():
        import jax, jax.numpy as jnp
        import numpy as np
        N_NODES = 100000
        N_EDGES = 25000
        IN_FEATS = 128
        OUT_FEATS = 128
        EDGE_HIDDEN = 64
        key = jax.random.key(seed)
        ks = jax.random.split(key, 7)
        h = jax.random.normal(ks[0], (N_NODES, IN_FEATS), dtype=jnp.float32)
        edge_feat = jax.random.normal(ks[1], (N_EDGES, EDGE_HIDDEN), dtype=jnp.float32)
        src = jax.random.randint(ks[2], (N_EDGES,), 0, N_NODES)
        dst = jax.random.randint(ks[3], (N_EDGES,), 0, N_NODES)
        stdv = 1.0 / np.sqrt(OUT_FEATS)
        stdv_e = 1.0 / np.sqrt(IN_FEATS)
        weight = jax.random.uniform(ks[4], (IN_FEATS, OUT_FEATS), minval=-stdv, maxval=stdv, dtype=jnp.float32)
        weight_edge = jax.random.uniform(ks[5], (EDGE_HIDDEN, IN_FEATS), minval=-stdv_e, maxval=stdv_e, dtype=jnp.float32)
        bias = jax.random.uniform(ks[6], (OUT_FEATS,), minval=-stdv, maxval=stdv, dtype=jnp.float32)
        return {'h': h, 'edge_feat': edge_feat, 'src': src, 'dst': dst, 'num_nodes': N_NODES, 'weight': weight, 'weight_edge': weight_edge, 'bias': bias}
    _L0_gnn_all = _L0_gnn_setup()
    _L0_gnn_in = {k: v for k, v in _L0_gnn_all.items() if k in ('weight', 'weight_edge', 'bias')}
    del _L0_gnn_all

    def _L1_gnn_setup():
        import jax, jax.numpy as jnp
        import numpy as np
        N = 100000
        E_RAND = 50000
        F_IN = 128
        D = 64
        SUBHEADS = 2
        ALPHA = 0.2
        key = jax.random.key(seed)
        ks = jax.random.split(key, 8)
        x = jax.random.normal(ks[0], (N, F_IN), jnp.float32)
        src = jax.random.randint(ks[1], (E_RAND,), 0, N)
        dst = jax.random.randint(ks[2], (E_RAND,), 0, N)
        loops = jnp.arange(N)
        edge_index = jnp.stack([jnp.concatenate([src, loops]), jnp.concatenate([dst, loops])])
        xav = lambda k, shp, fan: jax.random.normal(k, shp, jnp.float32) * np.float32(1.414 * np.sqrt(2.0 / fan))
        W = xav(ks[3], (SUBHEADS, F_IN, D), F_IN + D)
        b = jnp.zeros((SUBHEADS, D), jnp.float32)
        fc = xav(ks[4], (SUBHEADS, D, 1), D + 1)
        bf = jnp.zeros((SUBHEADS,), jnp.float32)
        a_src = xav(ks[5], (SUBHEADS, D), D + 1)
        a_dst = xav(ks[6], (SUBHEADS, D), D + 1)
        return dict(x=x, edge_index=edge_index, W=W, b=b, fc=fc, bf=bf, a_src=a_src, a_dst=a_dst)
    _L1_gnn_all = _L1_gnn_setup()
    _L1_gnn_in = {k: v for k, v in _L1_gnn_all.items() if k in ('W', 'b', 'fc', 'bf', 'a_src', 'a_dst')}
    del _L1_gnn_all

    def _L2_gnn_setup():
        import jax, jax.numpy as jnp
        import numpy as np
        N, E, H, R = (3125, 9375, 128, 64)
        key = jax.random.key(seed)
        ks = jax.random.split(key, 10)
        s = 1.0 / np.sqrt(H)
        return {'node_states': jax.random.normal(ks[0], (N, H), dtype=jnp.float32), 'edge_index': jax.random.randint(ks[1], (2, E), 0, N, dtype=jnp.int32), 'edge_type_ids': jax.random.randint(ks[2], (E,), 0, R, dtype=jnp.int32), 'W_self': jax.random.uniform(ks[3], (H, H), jnp.float32, -s, s), 'b_self': jax.random.uniform(ks[4], (H,), jnp.float32, -s, s), 'W_msg': jax.random.uniform(ks[5], (H, H), jnp.float32, -s, s), 'b_msg': jax.random.uniform(ks[6], (H,), jnp.float32, -s, s), 'rel_emb': jax.random.normal(ks[7], (R, H), dtype=jnp.float32), 'gamma': jnp.ones((H,), jnp.float32), 'beta': jnp.zeros((H,), jnp.float32)}
    _L2_gnn_all = _L2_gnn_setup()
    _L2_gnn_in = {k: v for k, v in _L2_gnn_all.items() if k in ('W_self', 'b_self', 'W_msg', 'b_msg', 'rel_emb', 'gamma', 'beta')}
    del _L2_gnn_all

    def _L3_gnn_setup():
        import jax, jax.numpy as jnp
        import numpy as np
        N = 50000
        E = 12500
        C = 128
        H = 8
        HD = C // H
        key = jax.random.key(seed)
        ks = jax.random.split(key, 8)
        s = 1.0 / np.sqrt(C)
        x = jax.random.normal(ks[0], (N, C), jnp.float32)
        edge_index = jax.random.randint(ks[1], (2, E), 0, N, jnp.int32)
        edge_weight = jax.random.normal(ks[2], (E,), jnp.float32) * 0.1
        Wq = jax.random.normal(ks[3], (C, C), jnp.float32) * s
        Wk = jax.random.normal(ks[4], (C, C), jnp.float32) * s
        Wv = jax.random.normal(ks[5], (C, C), jnp.float32) * s
        Wd = jax.random.normal(ks[6], (H, 1), jnp.float32)
        Wo = jax.random.normal(ks[7], (C, C), jnp.float32) * s
        return {'x': x, 'edge_index': edge_index, 'edge_weight': edge_weight, 'Wq': Wq, 'bq': jnp.zeros((C,), jnp.float32), 'Wk': Wk, 'bk': jnp.zeros((C,), jnp.float32), 'Wv': Wv, 'bv': jnp.zeros((C,), jnp.float32), 'Wd': Wd, 'bd': jnp.zeros((H,), jnp.float32), 'Wo': Wo, 'bo': jnp.zeros((C,), jnp.float32)}
    _L3_gnn_all = _L3_gnn_setup()
    _L3_gnn_in = {k: v for k, v in _L3_gnn_all.items() if k in ('Wq', 'bq', 'Wk', 'bk', 'Wv', 'bv', 'Wd', 'bd', 'Wo', 'bo')}
    del _L3_gnn_all
    return {'x': x, 'src': src, 'dst': dst, 'edge_attr_64': edge_attr_64, 'edge_type_64': edge_type_64, 'edge_weight': edge_weight, 'L0_gnn_weight': _L0_gnn_in['weight'], 'L0_gnn_weight_edge': _L0_gnn_in['weight_edge'], 'L0_gnn_bias': _L0_gnn_in['bias'], 'L1_gnn_W': _L1_gnn_in['W'], 'L1_gnn_b': _L1_gnn_in['b'], 'L1_gnn_fc': _L1_gnn_in['fc'], 'L1_gnn_bf': _L1_gnn_in['bf'], 'L1_gnn_a_src': _L1_gnn_in['a_src'], 'L1_gnn_a_dst': _L1_gnn_in['a_dst'], 'L2_gnn_W_self': _L2_gnn_in['W_self'], 'L2_gnn_b_self': _L2_gnn_in['b_self'], 'L2_gnn_W_msg': _L2_gnn_in['W_msg'], 'L2_gnn_b_msg': _L2_gnn_in['b_msg'], 'L2_gnn_rel_emb': _L2_gnn_in['rel_emb'], 'L2_gnn_gamma': _L2_gnn_in['gamma'], 'L2_gnn_beta': _L2_gnn_in['beta'], 'L3_gnn_Wq': _L3_gnn_in['Wq'], 'L3_gnn_bq': _L3_gnn_in['bq'], 'L3_gnn_Wk': _L3_gnn_in['Wk'], 'L3_gnn_bk': _L3_gnn_in['bk'], 'L3_gnn_Wv': _L3_gnn_in['Wv'], 'L3_gnn_bv': _L3_gnn_in['bv'], 'L3_gnn_Wd': _L3_gnn_in['Wd'], 'L3_gnn_bd': _L3_gnn_in['bd'], 'L3_gnn_Wo': _L3_gnn_in['Wo'], 'L3_gnn_bo': _L3_gnn_in['bo']}

def reference(x, src, dst, edge_attr_64, edge_type_64, edge_weight, L0_gnn_weight, L0_gnn_weight_edge, L0_gnn_bias, L1_gnn_W, L1_gnn_b, L1_gnn_fc, L1_gnn_bf, L1_gnn_a_src, L1_gnn_a_dst, L2_gnn_W_self, L2_gnn_b_self, L2_gnn_W_msg, L2_gnn_b_msg, L2_gnn_rel_emb, L2_gnn_gamma, L2_gnn_beta, L3_gnn_Wq, L3_gnn_bq, L3_gnn_Wk, L3_gnn_bk, L3_gnn_Wv, L3_gnn_bv, L3_gnn_Wd, L3_gnn_bd, L3_gnn_Wo, L3_gnn_bo):
    import jax
    import jax.numpy as jnp

    def _L0_gnn_ref(h, edge_feat, src, dst, num_nodes, weight, weight_edge, bias):
        import jax, jax.numpy as jnp
        import numpy as np
        N_NODES = 100000
        N_EDGES = 25000
        IN_FEATS = 128
        OUT_FEATS = 128
        EDGE_HIDDEN = 64
        eh = edge_feat @ weight_edge
        m = eh + h[src]
        agg = jax.ops.segment_sum(m, dst, num_segments=num_nodes)
        deg = jax.ops.segment_sum(jnp.ones((dst.shape[0],), dtype=h.dtype), dst, num_segments=num_nodes)
        norm = jnp.clip(deg, 1.0, None) ** (-0.5)
        agg = agg * norm[:, None]
        out = agg @ weight + bias
        return jax.nn.relu(out)

    def _L1_gnn_ref(x, edge_index, W, b, fc, bf, a_src, a_dst):
        import jax, jax.numpy as jnp
        import numpy as np
        N = 100000
        E_RAND = 50000
        F_IN = 128
        D = 64
        SUBHEADS = 2
        ALPHA = 0.2
        row, col = (edge_index[0], edge_index[1])
        n = x.shape[0]
        outs = []
        for i in range(SUBHEADS):
            h = x @ W[i]
            s_r = h @ a_src[i]
            s_c = h @ a_dst[i]
            e = jax.nn.leaky_relu(s_r[row] + s_c[col], ALPHA)
            m = jax.ops.segment_max(e, row, num_segments=n)
            ee = jnp.exp(e - m[row])
            denom = jax.ops.segment_sum(ee, row, num_segments=n)
            att = ee / denom[row]
            rs = jax.ops.segment_sum(att, row, num_segments=n)
            val = att / jnp.where(rs == 0, 1.0, rs)[row]
            vh = h
            for _ in range(i + 1):
                vh = jax.ops.segment_sum(val[:, None] * vh[col], row, num_segments=n)
            vh = jnp.where(jnp.isnan(vh), 0.0, vh)
            vh = vh + b[i]
            g = jax.nn.sigmoid(vh @ fc[i] + bf[i])
            vh = jnp.maximum(vh, 0.0) + g * jnp.minimum(vh, 0.0)
            vh = jax.nn.leaky_relu(vh, ALPHA)
            outs.append(vh)
        return jnp.concatenate(outs, axis=1)

    def _L2_gnn_ref(node_states, edge_index, edge_type_ids, W_self, b_self, W_msg, b_msg, rel_emb, gamma, beta):
        import jax, jax.numpy as jnp
        import numpy as np
        N, E, H, R = (3125, 9375, 128, 64)
        src, dst = (edge_index[0], edge_index[1])
        rel_ids = jnp.clip(edge_type_ids, 0, rel_emb.shape[0] - 1)
        msg = (node_states[src] + rel_emb[rel_ids]) @ W_msg.T + b_msg
        agg = jax.ops.segment_sum(msg, dst, num_segments=node_states.shape[0])
        deg = jax.ops.segment_sum(jnp.ones((msg.shape[0],), msg.dtype), dst, num_segments=node_states.shape[0])
        agg = agg / jnp.maximum(deg, 1.0)[:, None]
        updated = node_states @ W_self.T + b_self + agg
        updated = jax.nn.gelu(updated, approximate=False)
        x = updated + node_states
        mu = jnp.mean(x, axis=-1, keepdims=True)
        var = jnp.var(x, axis=-1, keepdims=True)
        return (x - mu) * jax.lax.rsqrt(var + 1e-05) * gamma + beta

    def _L3_gnn_ref(x, edge_index, edge_weight, Wq, bq, Wk, bk, Wv, bv, Wd, bd, Wo, bo):
        import jax, jax.numpy as jnp
        import numpy as np
        N = 50000
        E = 12500
        C = 128
        H = 8
        HD = C // H
        row, col = (edge_index[0], edge_index[1])
        n = x.shape[0]
        q = (x @ Wq.T + bq).reshape(n, H, HD)
        k = (x @ Wk.T + bk).reshape(n, H, HD)
        v = (x @ Wv.T + bv).reshape(n, H, HD)
        scores = jnp.einsum('ehd,ehd->eh', q[row], k[col]) / np.sqrt(HD)
        scores = scores + edge_weight[:, None]
        dmean = jnp.mean(x[col] - x[row], axis=-1, keepdims=True)
        scores = scores + dmean @ Wd.T + bd
        attn = jax.nn.softmax(scores, axis=0)
        msgs = (v[col] * attn[:, :, None]).reshape(-1, H * HD)
        out = jnp.zeros((n, H * HD), x.dtype).at[row].add(msgs)
        return out @ Wo.T + bo
    edge_index = jnp.stack([src, dst])
    h = jnp.maximum(_layernorm(x, axis=-1), 0.0)
    x = x + _L0_gnn_ref(h, edge_attr_64, src, dst, 100000, L0_gnn_weight, L0_gnn_weight_edge, L0_gnn_bias)
    h = jnp.maximum(_layernorm(x, axis=-1), 0.0)
    x = x + _L1_gnn_ref(h, edge_index, L1_gnn_W, L1_gnn_b, L1_gnn_fc, L1_gnn_bf, L1_gnn_a_src, L1_gnn_a_dst)
    h = jnp.maximum(_layernorm(x, axis=-1), 0.0)
    x = x + _L2_gnn_ref(h, edge_index, edge_type_64, L2_gnn_W_self, L2_gnn_b_self, L2_gnn_W_msg, L2_gnn_b_msg, L2_gnn_rel_emb, L2_gnn_gamma, L2_gnn_beta)
    h = jnp.maximum(_layernorm(x, axis=-1), 0.0)
    x = x + _L3_gnn_ref(h, edge_index, edge_weight, L3_gnn_Wq, L3_gnn_bq, L3_gnn_Wk, L3_gnn_bk, L3_gnn_Wv, L3_gnn_bv, L3_gnn_Wd, L3_gnn_bd, L3_gnn_Wo, L3_gnn_bo)
    return x

_drawn_inputs = setup_inputs


def setup_inputs(seed=0):
    import zlib

    import numpy as np

    out = dict(_drawn_inputs(seed))
    spreads = {'L1_gnn_b': (0.0, 0.1),
     'L1_gnn_bf': (0.0, 2.0),
     'L2_gnn_gamma': (1.0, 0.2),
     'L2_gnn_beta': (0.0, 0.1),
     'L3_gnn_bq': (0.0, 0.8),
     'L3_gnn_bk': (0.0, 2.0),
     'L3_gnn_bv': (0.0, 2.0),
     'L3_gnn_bd': (0.0, 0.1),
     'L3_gnn_bo': (0.0, 0.1)}
    factors = {'edge_weight': 30.544,
     'L1_gnn_fc': 2.84,
     'L2_gnn_b_msg': 3.733,
     'L3_gnn_Wq': 8.0,
     'L3_gnn_Wk': 8.0,
     'L3_gnn_Wv': 8.0,
     'L3_gnn_Wd': 64.0,
     'L3_gnn_Wo': 8.0}
    for name, (base, spread) in spreads.items():
        noise = np.random.default_rng([zlib.crc32(name.encode()), seed]).standard_normal(out[name].shape)
        drawn = base * np.exp(spread * noise) if base else spread * noise
        out[name] = jnp.asarray(drawn.astype(out[name].dtype))
    for name, factor in factors.items():
        out[name] = (out[name] * factor).astype(out[name].dtype)
    return out
```

```python
import numpy as np
from contextlib import ExitStack

import concourse.bass as bass
from concourse import mybir

F32 = mybir.dt.float32
I32 = mybir.dt.int32
BF16 = mybir.dt.bfloat16
ALU = mybir.AluOpType
ACT = mybir.ActivationFunctionType
AX = mybir.AxisListType

P = 128
N = 100000
E = 50000
C = 128
D = 64
HEADS = 8
HD = C // HEADS
U = 8
NB = -(-E // (P * U))
T = NB * U
EP = P * T
FULL = E // T
REST = E - FULL * T
SKIP = 1 << 20
BIG = 1e30
EPS = 1e-5
ZEROS = 2500
LO = 512
HI = 256
ALPHA = 0.2
FLAGS = 5
CONT, FIRST, RSQRT, RDEG, TYPE = range(FLAGS)
assert NB % 2 == 1 and FULL == P - 1


class Step:

    def __init__(self, k, par):
        self.k, self.par, self.blk = k, par, 2 * k + par

    def ago(self, n):
        at = self.par - n
        return Step(self.k + at // 2, at % 2)

    def within(self, blocks):
        return not isinstance(self.blk, int) or 0 <= self.blk < blocks


def sweep(eng, body, blocks=NB, lag=0):
    body(Step(0, 0))
    body(Step(0, 1))
    pairs_end = (blocks - 3) // 2
    with eng.Fori(1, pairs_end) as k:
        body(Step(k, 0))
        body(Step(k, 1))
    for blk in range(2 * pairs_end, blocks + lag):
        body(Step(blk // 2, blk % 2))


def wait(eng, sem, value):
    if not isinstance(value, int) or value > 0:
        eng.wait_ge(sem, value)


def settle(eng, sem):
    eng.sem_inc(sem, 1)


class Chain:

    def __init__(self, sem, per):
        self.sem, self.per = sem, per

    def at(self, step):
        self.base, self.n = step.blk * self.per, 0

    def base_of(self, step):
        return step.blk * self.per

    def done(self, instruction):
        instruction.then_inc(self.sem, 1)
        self.n += 1
        assert self.n <= self.per
        return self.base + self.n

    def end(self, step):
        return (step.blk + 1) * self.per


class Line:

    def __init__(self, eng, sem):
        self.eng, self.sem, self.n = eng, sem, 0

    def __call__(self, instruction):
        self.n += 1
        instruction.then_inc(self.sem, 1)
        self.eng.wait_ge(self.sem, self.n)


def middle(vector, n):
    return vector.unsqueeze(1).to_broadcast([vector.shape[0], n, vector.shape[1]])


def inner(vector, n):
    return vector.unsqueeze(2).to_broadcast([vector.shape[0], vector.shape[1], n])


class Kernel:
    pass


def build(nc, A, out):
    K = Kernel()
    K.nc, K.A, K.out = nc, A, out
    with ExitStack() as keep:
        K.keep = keep
        declare(K)
        phases = (setup_tables, sort_by_src, order_tables, layer0, attention_inputs, attention_weights,
                  attention_hop1, attention_hop2, layer2, layer2_nodes, scores, score_softmax, layer3)
        for phase in phases:
            phase(K)


def dram(K, name, shape, dt=F32):
    return K.nc.dram_tensor(name, shape, dt).ap()


def kept(K, name, shape, dt=F32):
    return K.keep.enter_context(K.nc.sbuf_tensor(name, shape, dt))


class Phase:

    def __init__(self, K, name):
        self.K, self.name = K, name

    def __enter__(self):
        self.stack = ExitStack()
        self.sems = []
        return self

    def __exit__(self, *error):
        self.stack.close()
        self.K.nc.clear_and_free_semaphores(self.sems)
        self.K.nc.all_engine_barrier()

    def sb(self, name, shape, dt=F32):
        return self.stack.enter_context(self.K.nc.sbuf_tensor(f"{self.name}_{name}", shape, dt))

    def ps(self, name, shape, dt=F32):
        return self.stack.enter_context(self.K.nc.psum_tensor(f"{self.name}_{name}", shape, dt))

    def sem(self, name):
        self.sems.append(self.K.nc.alloc_semaphore(f"{self.name}_{name}"))
        return self.sems[-1]

    def block(self):
        return self.stack.enter_context(self.K.nc.Block())


def declare(K):
    K.X = dram(K, "node_states", (N + EP, C))
    K.HOP = dram(K, "hop1_rows", (N, D))
    K.AGG = dram(K, "relation_rows", (N, C))
    K.PASS1 = dram(K, "sorted_by_low_digit", (EP, 4), I32)
    K.BY_SRC = dram(K, "edges_by_src", (EP + 2, 4), I32)
    K.BY_DST = dram(K, "edges_by_dst", (EP + 2, 4), I32)
    K.EDGE = dram(K, "edge_features", (EP, D))
    K.H0 = dram(K, "col_rows_head0", (EP, D))
    K.H1 = dram(K, "col_rows_head1", (EP, D))
    K.V = dram(K, "value_rows", (EP, C))
    K.ROW = dram(K, "row_states", (EP, C))

    K.ident = kept(K, "ident", [P, P])
    K.ones = kept(K, "ones", [P, P])
    K.zeros = kept(K, "zeros", [P, ZEROS])
    K.eps = kept(K, "eps", [P, 1])
    K.below = kept(K, "below", [P, P])
    K.above = kept(K, "above", [P, P])
    K.iota64 = kept(K, "iota64", [P, D])
    K.w0 = kept(K, "w0", [P, C])
    K.w0e = kept(K, "w0e", [D, C])
    K.w1 = kept(K, "w1", [P, 2 * D + 2])
    K.w1r = kept(K, "w1r", [P, 2])
    K.wmsg = kept(K, "wmsg", [P, C])
    K.wrel = kept(K, "wrel", [D, C])
    K.wself = kept(K, "wself", [P, C])
    K.wq = kept(K, "wq", [P, C + 1])
    K.wkv = kept(K, "wkv", [P, 2 * C + 1])
    K.wo = kept(K, "wo", [P, C])
    K.vec = {n: kept(K, f"v_{n}", [P, size]) for n, size in VECTORS}
    K.relu_b0 = kept(K, "relu_b0", [P, C])
    K.c1 = kept(K, "c1", [P, C])
    K.order = {}
    for o in ("s", "d"):
        K.order[o] = {
            "near": kept(K, f"near_{o}", [P, T], I32),
            "far": kept(K, f"far_{o}", [P, T], I32),
            "put": kept(K, f"put_{o}", [P, T], I32),
            "add": kept(K, f"add_{o}", [P, T], I32),
            "put_first": kept(K, f"put_first_{o}", [P, 1], I32),
            "add_first": kept(K, f"add_first_{o}", [P, 1], I32),
            "flags": kept(K, f"flags_{o}", [P, T, FLAGS]),
            "scale_first": kept(K, f"scale_first_{o}", [P, 2]),
            "to_later": kept(K, f"to_later_{o}", [P, P]),
            "from_earlier": kept(K, f"from_earlier_{o}", [P, P]),
            "last_seg": kept(K, f"last_seg_{o}", [P, T]),
            "next_cont": kept(K, f"next_cont_{o}", [P, T]),
            "real": kept(K, f"real_{o}", [P, T]),
            "weight": kept(K, f"weight_{o}", [P, T]),
        }
    K.score = kept(K, "score", [P, T, HEADS])
    K.mean_diff = kept(K, "mean_diff", [P, T])
    K.att = [kept(K, f"att{i}", [P, T]) for i in range(2)]


VECTORS = [("L0_gnn_bias", C), ("L1_gnn_b", C), ("L1_gnn_fc", C), ("L1_gnn_bf", 2),
           ("L1_gnn_a_src", C), ("L1_gnn_a_dst", C), ("L2_gnn_b_self", C), ("L2_gnn_b_msg", C),
           ("L2_gnn_gamma", C), ("L2_gnn_beta", C), ("L3_gnn_bq", C), ("L3_gnn_bk", C),
           ("L3_gnn_bv", C), ("L3_gnn_Wd", HEADS), ("L3_gnn_bd", HEADS), ("L3_gnn_bo", C)]
VECTOR_DIMS = {"L1_gnn_b": "a b -> (a b)", "L1_gnn_fc": "a b c -> (a b c)",
               "L1_gnn_a_src": "a b -> (a b)", "L1_gnn_a_dst": "a b -> (a b)",
               "L3_gnn_Wd": "a b -> (a b)"}


def setup_tables(K):
    nc, A = K.nc, K.A
    chunk = 11
    per = N // P
    chunks = per // chunk
    tail = N - P * per
    assert chunks * chunk == per and tail <= P and chunks % 2 == 1
    with Phase(K, "setup") as ph:
        names = ["weight", "weight_edge", "W_self", "W_msg", "rel_emb", "Wq", "Wk", "Wv", "Wo"]
        raw = {n: ph.sb(n, [P, C]) for n in names}
        weT = ph.sb("weT", [P, D])
        relT = ph.sb("relT", [P, D])
        prod = ph.sb("prod", [P, C])
        xc = ph.sb("xc", [P, 2, chunk, C])
        xt = ph.sb("xt", [tail, C])
        t1 = ph.sb("t1", [P, C])
        t2 = ph.sb("t2", [P, C])
        t3 = ph.sb("t3", [P, 2])
        t4 = ph.sb("t4", [P, 2])
        pT = ph.ps("pT", [P, 512])
        loaded, weights_loaded, consts, dve_step, pe_step, act_step = (ph.sem(n) for n in (
            "vectors_loaded", "weights_loaded", "consts", "dve_step", "pe_step", "act_step"))
        zeroed = ph.sem("zeroed")
        x_in = [ph.sem("x_in0"), ph.sem("x_in1")]
        x_out = [ph.sem("x_out0"), ph.sem("x_out1")]
        x_added, tail_in, b0_ready = ph.sem("x_added"), ph.sem("tail_in"), ph.sem("b0_ready")
        bias = K.vec["L0_gnn_bias"]
        xv = A["x"][0:P * per, :].rearrange("(p r) d -> p r d", p=P)
        Xv = K.X[0:P * per, :].rearrange("(p r) d -> p r d", p=P)
        w1 = A["L1_gnn_W"]
        n_vec = len(VECTORS)
        n_w = 2 + 7 + 2
        block = ph.block()

        @block.sync
        def _(sp):
            for n, size in VECTORS:
                v = A[n].rearrange(VECTOR_DIMS[n]) if n in VECTOR_DIMS else A[n]
                sp.dma_start(K.vec[n][:, :], v.partition_broadcast(P)).then_inc(loaded, 16)
            sp.dma_start(raw["weight_edge"][0:D, :], A["L0_gnn_weight_edge"]).then_inc(weights_loaded, 16)
            sp.dma_start(raw["rel_emb"][0:D, :], A["L2_gnn_rel_emb"]).then_inc(weights_loaded, 16)
            sp.dma_start(K.w0[:, :], A["L0_gnn_weight"]).then_inc(weights_loaded, 16)
            for n in ("W_self", "W_msg"):
                sp.dma_start(raw[n][:, :], A[f"L2_gnn_{n}"]).then_inc(weights_loaded, 16)
            for n in ("Wq", "Wk", "Wv", "Wo"):
                sp.dma_start(raw[n][:, :], A[f"L3_gnn_{n}"]).then_inc(weights_loaded, 16)
            for i in range(2):
                sp.dma_start(K.w1[:, i * D:(i + 1) * D], w1[i, :, :]).then_inc(weights_loaded, 16)

            def load_x(b):
                wait(sp, x_out[b.par], 16 * b.k)
                sp.dma_start(xc[:, b.par, :, :], xv[:, bass.ds(b.blk * chunk, chunk), :])\
                    .then_inc(x_in[b.par], 16)

            sweep(sp, load_x, chunks)
            sp.dma_start(xt[:, :], A["x"][P * per:N, :]).then_inc(tail_in, 16)

        @block.scalar
        def _(act):
            act.wait_ge(consts, 1)
            z = K.zeros
            for table, size in ((K.HOP[:, :], N * D), (K.AGG[:, :], N * C), (K.X[N:N + EP, :], EP * C)):
                width = next(w for w in (ZEROS, 14 * C) if size // P % w == 0)
                flat = table.rearrange("n d -> (n d)").rearrange("(p a b) -> p a b", p=P, b=width)
                act.dma_start(flat, middle(z[:, 0:width], size // P // width)).then_inc(zeroed, 16)
            pads = K.EDGE[E:EP, :].rearrange("(p a) d -> p (a d)", p=16)
            act.dma_start(K.EDGE[0:E, :].rearrange("(p a) d -> p (a d)", p=80),
                          A["edge_attr_64"].rearrange("(p a) d -> p (a d)", p=80)).then_inc(zeroed, 16)
            act.dma_start(pads, z[0:16, 0:(EP - E) * D // 16]).then_inc(zeroed, 16)

            def store_x(b):
                wait(act, x_added, b.blk + 1)
                act.dma_start(Xv[:, bass.ds(b.blk * chunk, chunk), :], xc[:, b.par, :, :])\
                    .then_inc(x_out[b.par], 16)

            sweep(act, store_x, chunks)
            act.wait_ge(x_added, chunks + 1)
            act.dma_start(K.X[P * per:N, :], xt[:, :]).then_inc(zeroed, 16)
            act.wait_ge(dve_step, SETUP_SIGMOID)
            act.activation(t4[:, :], t3[:, :], ACT.Sigmoid).then_inc(act_step, 1)
            for sem, n in ((zeroed, 6), (x_out[0], chunks // 2 + 1), (x_out[1], chunks // 2)):
                act.wait_ge(sem, 16 * n)

        @block.gpsimd
        def _(pool):
            pool.memset(K.zeros[:, :], 0.0).then_inc(consts, 1)
            pool.memset(K.ones[:, :], 1.0).then_inc(consts, 1)
            pool.memset(K.eps[:, :], EPS).then_inc(consts, 1)
            pool.wait_ge(consts, 3)
            pool.affine_select(out=K.ident[:, :], in_=K.zeros[:, 0:P], compare_op=ALU.not_equal, fill=1.0,
                               base=0, pattern=[[-1, P]], channel_multiplier=1).then_inc(consts, 1)
            pool.affine_select(out=K.below[:, :], in_=K.ones[:, :], compare_op=ALU.is_gt, fill=0.0,
                               base=0, pattern=[[1, P]], channel_multiplier=-1).then_inc(consts, 1)
            pool.affine_select(out=K.above[:, :], in_=K.ones[:, :], compare_op=ALU.is_gt, fill=0.0,
                               base=0, pattern=[[-1, P]], channel_multiplier=1).then_inc(consts, 1)
            pool.iota(K.iota64[:, :], pattern=[[1, D]], base=0, channel_multiplier=0,
                      allow_small_or_imprecise_dtypes=True).then_inc(consts, 1)
            pool.wait_ge(b0_ready, 1)

            def add_bias(b):
                wait(pool, x_in[b.par], 16 * (b.k + 1))
                pool.tensor_tensor(xc[:, b.par, :, :], xc[:, b.par, :, :],
                                   middle(K.relu_b0[:, :], chunk), ALU.add).then_inc(x_added, 1)

            sweep(pool, add_bias, chunks)
            pool.wait_ge(tail_in, 16)
            pool.tensor_tensor(xt[:, :], xt[:, :], K.relu_b0[0:tail, :], ALU.add).then_inc(x_added, 1)

        turns = [(raw["weight_edge"], D, weT[:, :]),
                 (raw["rel_emb"], D, relT[:, :]),
                 (raw["W_self"], P, K.wself[:, :]), (raw["W_msg"], P, K.wmsg[:, :]),
                 (raw["Wq"], P, K.wq[:, 0:C]), (raw["Wk"], P, K.wkv[:, 0:C]),
                 (raw["Wv"], P, K.wkv[:, C:2 * C]), (raw["Wo"], P, K.wo[:, :])]
        products = [(weT, K.w0, K.w0e), (relT, K.wmsg, K.wrel)]

        @block.tensor
        def _(pe):
            pe.wait_ge(consts, 7)
            pe.wait_ge(weights_loaded, 16 * n_w)
            for n, (source, rows, _) in enumerate(turns):
                wait(pe, b0_ready, 1 + n if n else 0)
                nc.tensor.transpose(pT[:, 0:rows], source[0:rows, :], K.ident[0:rows, 0:rows])\
                    .then_inc(pe_step, 1)
            for n, (lhs, rhs, _) in enumerate(products):
                pe.wait_ge(b0_ready, 1 + len(turns) + n)
                nc.tensor.matmul(pT[0:D, 0:C], lhs[:, :], rhs[:, :],
                                 start=True, stop=True).then_inc(pe_step, 1)

        @block.vector
        def _(dve):
            line = Line(dve, dve_step)
            dve.wait_ge(loaded, 16 * n_vec)
            dve.tensor_scalar(K.relu_b0[:, :], bias[:, :], 0.0, None, ALU.max).then_inc(b0_ready, 1)
            line(dve.memset(K.wq[:, C:C + 1], 1.0 / C))
            line(dve.memset(K.wkv[:, 2 * C:2 * C + 1], 1.0 / C))
            for n, (_, rows, target) in enumerate(turns):
                dve.wait_ge(pe_step, n + 1)
                dve.tensor_copy(target, pT[:, 0:rows]).then_inc(b0_ready, 1)
            for n, (_, _, target) in enumerate(products):
                dve.wait_ge(pe_step, len(turns) + n + 1)
                dve.tensor_copy(target[:, :], pT[0:D, 0:C]).then_inc(b0_ready, 1)
            for a, target in ((K.vec["L1_gnn_a_dst"], K.w1[:, 2 * D:2 * D + 2]),
                              (K.vec["L1_gnn_a_src"], K.w1r[:, :])):
                line(dve.tensor_tensor(prod[:, :], K.w1[:, 0:C], a[:, :], ALU.mult))
                line(dve.tensor_reduce(target, prod[:, :].rearrange("p (h d) -> p h d", h=2), AX.X, ALU.add))
            b1, fc, bf = K.vec["L1_gnn_b"], K.vec["L1_gnn_fc"], K.vec["L1_gnn_bf"]
            line(dve.tensor_tensor(t1[:, :], b1[:, :], fc[:, :], ALU.mult))
            line(dve.tensor_reduce(t3[:, :], t1[:, :].rearrange("p (h d) -> p h d", h=2), AX.X, ALU.add))
            line(dve.tensor_tensor(t3[:, :], t3[:, :], bf[:, :], ALU.add))
            assert line.n == SETUP_SIGMOID, line.n
            line(dve.tensor_scalar(t1[:, :], b1[:, :], 0.0, None, ALU.min))
            dve.wait_ge(act_step, 1)
            half = lambda t: t[:, :].rearrange("p (h d) -> p h d", h=2)
            line(dve.tensor_tensor(half(t2), half(t1), inner(t4[:, :], D), ALU.mult))
            line(dve.scalar_tensor_tensor(t1[:, :], b1[:, :], 0.0, t2[:, :], ALU.max, ALU.add))
            line(dve.scalar_tensor_tensor(K.c1[:, :], t1[:, :], ALPHA, t1[:, :], ALU.mult, ALU.max))


SETUP_SIGMOID = 9



def sort_by_src(K):
    nc, A = K.nc, K.A
    GROUP = 4
    groups = T // GROUP
    assert groups <= P and U == 2 * GROUP
    with Phase(K, "sort") as ph:
        load = [ph.sb(f"load{n}", [P, T, 4], I32) for n in range(2)]
        digit_i = ph.sb("digit_i", [P, T], I32)
        digit = ph.sb("digit", [P, T])
        rank = ph.sb("rank", [P, 2, U])
        iota = ph.sb("iota", [P, LO], BF16)
        onehot = ph.sb("onehot", [P, U, LO], BF16)
        junk = ph.sb("junk", [P, 4, LO], BF16)
        tri = ph.sb("tri", [P, P], BF16)
        ones = ph.sb("ones", [P, P], BF16)
        ident = ph.sb("ident", [P, P], BF16)
        pick = ph.sb("pick", [P, 2 * P], BF16)
        counts = ph.sb("counts", [P, LO])
        firsts = ph.sb("firsts", [P, LO])
        begins = ph.sb("begins", [P, LO])
        begins_i = ph.sb("begins_i", [P, 2, LO], I32)
        begins_hi = ph.sb("begins_hi", [P, LO], BF16)
        begins_lo = ph.sb("begins_lo", [P, LO], BF16)
        scan_ones = ph.sb("scan_ones", [P, LO])
        place_i = ph.sb("place_i", [P, 3, U], I32)
        place = ph.sb("place", [P, 2, U], I32)
        stage = ph.sb("stage", [P, 2, U, 4], I32)
        edge_row = ph.sb("edge_row", [2, 4], I32)
        totals = ph.ps("totals", [P, LO])
        before = ph.ps("before", [P, LO])
        running = ph.ps("running", [P, 4, LO])

        loaded, consts, line_sem = ph.sem("loaded"), ph.sem("consts"), ph.sem("dve_line")
        pads_set, by_dst, reloaded = ph.sem("pads_set"), ph.sem("by_dst"), ph.sem("reloaded")
        settled, pe_settled = ph.sem("pool_settled"), ph.sem("pe_settled")
        passes = [{n: ph.sem(f"{n}{w}") for n in ("hist_hot", "counted", "copied", "before", "begun",
                                                    "hot", "summed", "ranked", "places", "small")}
                  | {"sent": [ph.sem(f"sent{w}_{i}") for i in range(2)]} for w in (LO, HI)]
        block = ph.block()

        @block.sync
        def _(sp):
            sp.wait_ge(pads_set, 2)
            with nc.allow_non_contiguous_dma(reason="four fields of an edge side by side"):
                for n, name in enumerate(("src", "dst", "edge_type_64", "edge_weight")):
                    a = A[name].bitcast(I32) if name == "edge_weight" else A[name]
                    sp.dma_start(load[0][0:FULL, :, n:n + 1],
                                 a[0:FULL * T].rearrange("(p t a) -> p t a", t=T, a=1)).then_inc(loaded, 16)
                    sp.dma_start(load[0][FULL:P, 0:REST, n:n + 1],
                                 a[FULL * T:E].rearrange("(p t a) -> p t a", p=1, a=1)).then_inc(loaded, 16)
            sp.wait_ge(loaded, 16 * 8)
            body = K.BY_DST[1:EP + 1, :].rearrange("(p t) c -> p (t c)", p=P)
            sp.dma_start(body, load[0][:, :, :].rearrange("p t c -> p (t c)")).then_inc(by_dst, 16)
            for table in (K.BY_DST, K.BY_SRC):
                sp.dma_start(table[0:1, :], edge_row[0:1, :]).then_inc(by_dst, 16)
                sp.dma_start(table[EP + 1:EP + 2, :], edge_row[0:1, :]).then_inc(by_dst, 16)
            for i in range(2):
                sp.wait_ge(passes[0]["sent"][i], 16 * U * (NB // 2 + 1 - i))
            sp.dma_start(load[1][:, :, :].rearrange("p t c -> p (t c)"),
                         K.PASS1.rearrange("(p t) c -> p (t c)", p=P)).then_inc(reloaded, 16)
            sp.wait_ge(by_dst, 16 * 5)

        @block.gpsimd
        def _(pool):
            pool.memset(edge_row[:, :], -1).then_inc(pads_set, 1)
            pool.memset(load[0][:, :, :], 0).then_inc(consts, 1)
            pool.wait_ge(consts, 1)
            pool.memset(load[0][:, :, 0:2], N).then_inc(pads_set, 1)
            pool.memset(ones[:, :], 1.0).then_inc(consts, 1)
            pool.memset(scan_ones[:, :], 1.0).then_inc(consts, 1)
            pool.memset(pick[:, :], 0.0).then_inc(consts, 1)
            pool.wait_ge(consts, 4)
            pool.memset(pick[:, P:P + 1], 1.0).then_inc(consts, 1)
            pool.iota(iota[:, :], pattern=[[1, LO]], base=-LO // 2, channel_multiplier=0,
                      allow_small_or_imprecise_dtypes=True).then_inc(consts, 1)
            pool.tensor_copy(ident[:, :], K.ident[:, :]).then_inc(consts, 1)
            pool.affine_select(out=tri[:, :], in_=K.ones[:, :], compare_op=ALU.is_ge, fill=0.0,
                               base=0, pattern=[[1, P]], channel_multiplier=-1).then_inc(consts, 1)
            for n, table in ((0, K.PASS1[:, :]), (1, K.BY_SRC[:, :])):
                sems = passes[n]

                def send(b):
                    wait(pool, sems["places"], 2 * (b.blk + 1))
                    settle(pool, settled)
                    for u in range(U):
                        pool.indirect_dma_start(
                            table, bass.IndirectOffsetOnAxis(ap=place[:, b.par, u:u + 1], axis=0),
                            stage[:, b.par, u, :], None).then_inc(sems["sent"][b.par], 16)

                sweep(pool, send)
            for i in range(2):
                pool.wait_ge(passes[1]["sent"][i], 16 * U * (NB // 2 + 1 - i))

        @block.vector
        def _(dve):
            line = Line(dve, line_sem)
            dve.wait_ge(loaded, 16 * 8)
            dve.wait_ge(consts, 8)
            for n, (width, op, amount) in enumerate(((LO, ALU.bitwise_and, LO - 1),
                                                     (HI, ALU.logical_shift_right, 9))):
                sems, source = passes[n], load[n]
                if n:
                    dve.wait_ge(reloaded, 16)
                line(dve.tensor_scalar(digit_i[:, :], source[:, :, 0], amount, None, op))
                line(dve.tensor_scalar(digit[:, :], digit_i[:, :], float(-LO // 2), None, ALU.add))

                def hot(b, u, sem):
                    dve.tensor_scalar(onehot[:, u, 0:width], iota[:, 0:width],
                                      digit[:, bass.ds(b.blk * U + u, 1)], None, ALU.is_equal)\
                        .then_inc(sem, 1)

                def histogram(b):
                    for u in range(U):
                        wait(dve, sems["counted"], (b.blk - 1) * U + u + 1)
                        hot(b, u, sems["hist_hot"])

                sweep(dve, histogram)
                dve.wait_ge(sems["counted"], T)
                c = counts[:, 0:width]
                dve.tensor_copy(c, totals[:, 0:width]).then_inc(sems["copied"], 1)
                dve.wait_ge(sems["before"], 1)
                line(dve.tensor_copy(begins[:, 0:width], before[:, 0:width]))
                dve.sem_inc(sems["copied"], 1)
                dve.wait_ge(sems["before"], 2)
                line(dve.tensor_copy(c, before[:, 0:width]))
                line(dve.tensor_tensor_scan(firsts[:, 0:width], scan_ones[:, 0:width], c,
                                            0.0, ALU.mult, ALU.add))
                line(dve.tensor_tensor(firsts[:, 0:width], firsts[:, 0:width], c, ALU.subtract))
                line(dve.tensor_tensor(begins[:, 0:width], begins[:, 0:width], firsts[:, 0:width], ALU.add))
                line(dve.tensor_copy(begins_i[:, 0, 0:width], begins[:, 0:width]))
                line(dve.tensor_scalar(begins_i[:, 1, 0:width], begins_i[:, 0, 0:width], 255, None,
                                       ALU.bitwise_and))
                line(dve.tensor_copy(begins_lo[:, 0:width], begins_i[:, 1, 0:width]))
                line(dve.tensor_scalar(begins_i[:, 1, 0:width], begins_i[:, 0, 0:width], 0xFFFF00, None,
                                       ALU.bitwise_and))
                dve.tensor_copy(begins_hi[:, 0:width], begins_i[:, 1, 0:width]).then_inc(sems["begun"], 1)

                def rank_block(b):
                    static = isinstance(b.blk, int)
                    for u in range(U):
                        wait(dve, sems["summed"], (b.blk - 1) * U + GROUP * (u // GROUP + 1))
                        hot(b, u, sems["hot"])
                        if u:
                            tile_rank(b, u - 1)
                        elif not static or b.blk:
                            tile_rank(b.ago(1), U - 1)
                            send_places(b.ago(1))

                def tile_rank(b, u):
                    dve.wait_ge(sems["summed"], b.blk * U + u + 1)
                    dve.tensor_tensor_reduce(
                        out=junk[:, u % 4, 0:width], in0=onehot[:, u, 0:width],
                        in1=running[:, u % 4, 0:width], scale=1.0, scalar=0.0,
                        op0=ALU.mult, op1=ALU.add, accum_out=rank[:, b.par, u:u + 1])\
                        .then_inc(sems["ranked"], 1)

                def send_places(b):
                    dve.wait_ge(sems["ranked"], (b.blk + 1) * U)
                    wait(dve, sems["sent"][b.par], 16 * U * b.k)
                    settle(dve, sems["small"])
                    dve.tensor_copy(stage[:, b.par, :, :], source[:, bass.ds(b.blk * U, U), :])\
                        .then_inc(sems["places"], 1)
                    got = rank[:, b.par, :]
                    if n == 1:
                        dve.tensor_copy(place[:, b.par, :], got).then_inc(sems["places"], 1)
                        return
                    small = 4 * b.blk
                    dve.tensor_scalar(place_i[:, 0, :], got, -1.0, None, ALU.add).then_inc(sems["small"], 1)
                    dve.wait_ge(sems["small"], small + 2)
                    dve.tensor_scalar(place_i[:, 1, :], place_i[:, 0, :], P - 1, None, ALU.bitwise_and)\
                        .then_inc(sems["small"], 1)
                    dve.tensor_scalar(place_i[:, 2, :], place_i[:, 0, :], 7, None, ALU.logical_shift_right)\
                        .then_inc(sems["small"], 1)
                    dve.wait_ge(sems["small"], small + 4)
                    dve.scalar_tensor_tensor(place[:, b.par, :], place_i[:, 1, :], float(T),
                                             place_i[:, 2, :], ALU.mult, ALU.add)\
                        .then_inc(sems["places"], 1)

                sweep(dve, rank_block)
                tile_rank(Step(NB // 2, 0), U - 1)
                send_places(Step(NB // 2, 0))

        @block.tensor
        def _(pe):
            pe.wait_ge(consts, 8)
            for n, width in enumerate((LO, HI)):
                sems = passes[n]

                def count(b):
                    static = isinstance(b.blk, int)
                    for u in range(U):
                        wait(pe, sems["hist_hot"], b.blk * U + u + 1)
                        settle(pe, pe_settled)
                        group = b.blk * 2 + u // GROUP
                        pe.matmul(totals[:, 0:width], pick[:, bass.ds(P - group, P)],
                                  onehot[:, u, 0:width], start=static and b.blk == 0 and u == 0,
                                  stop=static and b.blk == NB - 1 and u == U - 1)\
                            .then_inc(sems["counted"], 1)

                sweep(pe, count)
                pe.wait_ge(sems["copied"], 1)
                pe.matmul(before[:, 0:width], K.below[:, :], counts[:, 0:width], start=True, stop=True)\
                    .then_inc(sems["before"], 1)
                pe.wait_ge(sems["copied"], 2)
                pe.matmul(before[:, 0:width], K.ones[:, :], counts[:, 0:width], start=True, stop=True)\
                    .then_inc(sems["before"], 1)
                pe.wait_ge(sems["begun"], 1)

                def sums(b):
                    for u in range(U):
                        wait(pe, sems["ranked"], b.blk * U + u - 3)
                        wait(pe, sems["hot"], b.blk * U + u + 1)
                        settle(pe, pe_settled)
                        bank = running[:, u % 4, 0:width]
                        mine = ident[:, bass.ds(b.blk * 2 + u // GROUP, 1)].to_broadcast([P, P])
                        pe.matmul(bank, mine, begins_hi[:, 0:width], start=True, stop=False)
                        pe.matmul(bank, mine, begins_lo[:, 0:width], start=False, stop=False)
                        for earlier in range(u // GROUP * GROUP, u):
                            pe.matmul(bank, ones[:, :], onehot[:, earlier, 0:width], start=False, stop=False)
                        pe.matmul(bank, tri[:, :], onehot[:, u, 0:width], start=False, stop=True)\
                            .then_inc(sems["summed"], 1)

                sweep(pe, sums)


def order_tables(K):
    nc = K.nc
    with Phase(K, "tables") as ph:
        loaded, consts, pe_step, act_step = ph.sem("loaded"), ph.sem("consts"), ph.sem("pe_step"), ph.sem("act_step")
        dve_line, rows_ready = ph.sem("dve_line"), ph.sem("rows_ready")
        orders = [("s", K.BY_SRC, 0, 1), ("d", K.BY_DST, 1, 0)]
        payload = [ph.sb(f"payload{n}", [P, T + 2, 4], I32) for n in range(2)]
        key = ph.sb("key", [P, T + 2])
        spare = ph.sb("spare", [P, T])
        t_ones = ph.sb("t_ones", [P, T])
        end, first, ok, t1, t2 = (ph.sb(n, [P, T]) for n in ("end", "first", "ok", "t1", "t2"))
        cross, begun, s1, s2, deg = (ph.sb(n, [P, 1]) for n in ("cross", "begun", "s1", "s2", "deg"))
        diag = ph.sb("diag", [P, 2, P])
        tail = ph.sb("tail", [P, 1])
        rows = ph.ps("rows", [P, 2, P])
        carry = ph.ps("carry", [P, 1])
        block = ph.block()

        @block.sync
        def _(sp):
            for n, (_, table, _, _) in enumerate(orders):
                src = bass.AP(table.tensor, 0, [[T * 4, P], [1, (T + 2) * 4]])
                sp.dma_start(payload[n][:, :, :].rearrange("p t c -> p (t c)"), src).then_inc(loaded, 16)

        @block.gpsimd
        def _(pool):
            pool.iota(spare[:, :], pattern=[[1, T]], base=N, channel_multiplier=T,
                      allow_small_or_imprecise_dtypes=True).then_inc(consts, 1)
            pool.memset(t_ones[:, :], 1.0).then_inc(consts, 1)

        @block.tensor
        def _(pe):
            for n, (o, _, _, _) in enumerate(orders):
                for m in range(2):
                    pe.wait_ge(rows_ready, 3 * n + m + 1)
                    pe.matmul(rows[:, m, :], K.ones[:, :], diag[:, m, :], start=True, stop=True)\
                        .then_inc(pe_step, 1)
                pe.wait_ge(rows_ready, 3 * n + 3)
                pe.matmul(carry[:, :], K.order[o]["to_later"][:, :], tail[:, :], start=True, stop=True)\
                    .then_inc(pe_step, 1)

        @block.scalar
        def _(act):
            for n, (o, _, _, _) in enumerate(orders):
                d = K.order[o]
                act.wait_ge(rows_ready, 3 * n + 3)
                act.activation(d["flags"][:, :, RSQRT], t1[:, :], ACT.Sqrt).then_inc(act_step, 1)
                act.wait_ge(pe_step, 3 * n + 3)
                act.activation(deg[:, :], carry[:, :], ACT.Identity, bias=begun[:, :]).then_inc(act_step, 1)
                act.wait_ge(act_step, 3 * n + 2)
                act.activation(d["scale_first"][:, 0:1], deg[:, :], ACT.Sqrt).then_inc(act_step, 1)

        @block.vector
        def _(dve):
            line = Line(dve, dve_line)
            dve.wait_ge(loaded, 32)
            dve.wait_ge(consts, 2)
            for n, (o, _, own, other) in enumerate(orders):
                d, pay = K.order[o], payload[n]
                fl = d["flags"]
                cur, prev, nxt = key[:, 1:T + 1], key[:, 0:T], key[:, 2:T + 2]
                key0, keyT = key[:, 1:2], key[:, T:T + 1]
                line(dve.tensor_copy(key[:, :], pay[:, :, own]))
                line(dve.tensor_scalar(d["near"][:, :], cur, float(N - 1), None, ALU.min))
                line(dve.tensor_scalar(d["far"][:, :], pay[:, 1:T + 1, other], float(N - 1), None, ALU.min))
                line(dve.tensor_tensor(fl[:, :, CONT], cur, prev, ALU.is_equal))
                line(dve.tensor_copy(cross[:, :], fl[:, 0:1, CONT]))
                line(dve.memset(fl[:, 0:1, CONT], 0.0))
                line(dve.tensor_tensor(end[:, :], cur, nxt, ALU.not_equal))
                line(dve.tensor_scalar(first[:, :], cur, key0, None, ALU.is_equal))
                line(dve.tensor_copy(fl[:, :, FIRST], first[:, :]))
                line(dve.tensor_scalar(d["real"][:, :], cur, float(N), None, ALU.is_lt))
                line(dve.tensor_copy(fl[:, :, TYPE], pay[:, 1:T + 1, 2]))
                line(dve.tensor_copy(d["weight"][:, :], pay[:, 1:T + 1, 3].bitcast(F32)))
                line(dve.tensor_scalar(d["last_seg"][:, :], cur, keyT, None, ALU.is_equal))
                line(dve.tensor_scalar(d["next_cont"][:, :], end[:, :], -1.0, 1.0, ALU.mult, ALU.add))
                line(dve.memset(d["next_cont"][:, T - 1:T], 0.0))
                line(dve.tensor_tensor(t1[:, :], end[:, :], first[:, :], ALU.mult))
                line(dve.tensor_reduce(s1[:, :], t1[:, :], AX.X, ALU.add))
                line(dve.tensor_scalar(t1[:, :], first[:, :], cross[:, :], None, ALU.mult))
                line(dve.tensor_scalar(t1[:, :], t1[:, :], -1.0, 1.0, ALU.mult, ALU.add))
                line(dve.tensor_tensor(t1[:, :], t1[:, :], end[:, :], ALU.mult))
                line(dve.tensor_tensor(ok[:, :], t1[:, :], d["real"][:, :], ALU.mult))
                line(dve.scalar_tensor_tensor(t1[:, :], cur, float(-SKIP), ok[:, :], ALU.add, ALU.mult))
                line(dve.tensor_scalar(d["put"][:, :], t1[:, :], float(SKIP), None, ALU.add))
                line(dve.tensor_tensor(t1[:, :], cur, spare[:, :], ALU.subtract))
                line(dve.tensor_tensor(t1[:, :], t1[:, :], ok[:, :], ALU.mult))
                line(dve.tensor_tensor(d["add"][:, :], t1[:, :], spare[:, :], ALU.add))
                line(dve.tensor_tensor(s1[:, :], s1[:, :], cross[:, :], ALU.mult))
                line(dve.tensor_tensor(s1[:, :], s1[:, :], d["real"][:, 0:1], ALU.mult))
                line(dve.scalar_tensor_tensor(s2[:, :], key0, float(-SKIP), s1[:, :], ALU.add, ALU.mult))
                line(dve.tensor_scalar(d["put_first"][:, :], s2[:, :], float(SKIP), None, ALU.add))
                line(dve.tensor_tensor(s2[:, :], key0, spare[:, 0:1], ALU.subtract))
                line(dve.tensor_tensor(s2[:, :], s2[:, :], s1[:, :], ALU.mult))
                line(dve.tensor_tensor(d["add_first"][:, :], s2[:, :], spare[:, 0:1], ALU.add))
                for m, k in enumerate((key0, keyT)):
                    dve.tensor_scalar(diag[:, m, :], K.ident[:, :], k, None, ALU.mult).then_inc(rows_ready, 1)
                dve.wait_ge(pe_step, 3 * n + 2)
                line(dve.tensor_scalar(d["to_later"][:, :], rows[:, 0, :], keyT, None, ALU.is_equal))
                line(dve.tensor_tensor(d["to_later"][:, :], d["to_later"][:, :], K.below[:, :], ALU.mult))
                line(dve.tensor_scalar(d["from_earlier"][:, :], rows[:, 1, :], key0, None, ALU.is_equal))
                line(dve.tensor_tensor(d["from_earlier"][:, :], d["from_earlier"][:, :], K.above[:, :], ALU.mult))
                line(dve.tensor_copy(t2[:, :], fl[:, :, CONT]))
                line(dve.tensor_reduce(begun[:, :], first[:, :], AX.X, ALU.add))
                line(dve.tensor_tensor_scan(t1[:, :], t2[:, :], t_ones[:, :], 0.0, ALU.mult, ALU.add))
                dve.tensor_copy(tail[:, :], t1[:, T - 1:T]).then_inc(rows_ready, 1)
                line(dve.reciprocal(fl[:, :, RDEG], t1[:, :]))
                dve.wait_ge(act_step, 3 * n + 3)
                line(dve.reciprocal(fl[:, :, RSQRT], fl[:, :, RSQRT]))
                line(dve.reciprocal(d["scale_first"][:, 0:1], d["scale_first"][:, 0:1]))
                line(dve.reciprocal(d["scale_first"][:, 1:2], deg[:, :]))


def norm_sums(dve, chain, x, n, bn, small):
    for u in range(n):
        last = chain.done(dve.bn_stats(bn[:, u, :], x[:, u, :]))
    dve.wait_ge(chain.sem, last)
    chain.done(dve.tensor_tensor(small["diff"], bn[:, 0:n, 1], bn[:, 0:n, 4], ALU.subtract))
    chain.done(dve.tensor_tensor(small["sum"], bn[:, 0:n, 1], bn[:, 0:n, 4], ALU.add))
    last = chain.done(dve.tensor_tensor(small["m2"], bn[:, 0:n, 2], bn[:, 0:n, 5], ALU.add))
    dve.wait_ge(chain.sem, last)
    last = chain.done(dve.tensor_tensor(small["sq"], small["diff"], small["diff"], ALU.mult))
    dve.wait_ge(chain.sem, last)
    chain.done(dve.scalar_tensor_tensor(small["q"], small["sq"], C / 4.0, small["m2"], ALU.mult, ALU.add))


def norm_scales(dve, chain, small):
    last = chain.done(dve.reciprocal(small["rstd"], small["std"]))
    dve.wait_ge(chain.sem, last)
    chain.done(dve.scalar_tensor_tensor(small["nmr"], small["sum"], -0.5, small["rstd"], ALU.mult, ALU.mult))


def small_tiles(ph, name, n):
    return {k: ph.sb(f"{name}_{k}", [P, n])[:, :] for k in ("diff", "sum", "m2", "sq", "q", "std", "rstd", "nmr")}


def stage_index(sp, buffer, source, b, sem):
    sp.dma_start(buffer[:, b.par, :], source[:, bass.ds(b.blk * U, U)]).then_inc(sem[b.par], 16)


def gather_rows(pool, table, index, par, rows, sem):
    for u in range(U):
        pool.indirect_dma_start(rows[:, par, u, :], None, table,
                                bass.IndirectOffsetOnAxis(ap=index[:, par, u:u + 1], axis=0)).then_inc(sem[par], 16)


def scatter_rows(pool, table, index, par, rows, sem, accumulate=False):
    for u in range(U):
        at = bass.IndirectOffsetOnAxis(ap=index[:, par, u:u + 1], axis=0)
        put_rows(pool, table, at, rows[:, par, u, :], accumulate).then_inc(sem[par], 16)


def put_rows(pool, table, at, rows, accumulate):
    if accumulate:
        return pool.indirect_dma_start(table, at, rows, None, bounds_check=table.shape[0] - 1,
                                       oob_is_err=True, compute_op=ALU.add)
    return pool.indirect_dma_start(table, at, rows, None, bounds_check=table.shape[0] - 1, oob_is_err=False)


def uses(blocks, par):
    return (blocks + 1 - par) // 2


def layer0(K):
    edge_sum_layer(K, "layer0", relational=False)


def layer2(K):
    edge_sum_layer(K, "layer2", relational=True)


def edge_sum_layer(K, name, relational):
    nc, A, d = K.nc, K.A, K.order["d"]
    W = C + D
    source = K.X[0:N, :] if relational else A["x"]
    w, we = (K.wmsg, K.wrel) if relational else (K.w0, K.w0e)
    bias = K.vec["L2_gnn_b_msg" if relational else "L0_gnn_bias"]
    target, put, put_first = (K.AGG[:, :], d["put"], d["put_first"]) if relational else \
        (K.X[:, :], d["add"], d["add_first"])
    scale = RDEG if relational else RSQRT
    with Phase(K, name) as ph:
        index = ph.sb("index", [P, 2, U], I32)
        put_index = ph.sb("put_index", [P, 2, U], I32)
        rows = ph.sb("rows", [P, 2, U, C])
        messages = ph.sb("messages", [P, 2, U, W])
        states = ph.sb("states", [P, 2, U, W])
        head = ph.sb("head", [P, W])
        flags = ph.sb("flags", [P, 2, U, FLAGS])
        turned_sb = ph.sb("turned", [P, 4, 512])
        result = ph.sb("result", [P, 2, U, C])
        bn = ph.sb("bn", [P, U, 6])
        small = small_tiles(ph, "norm", U)
        turned_ps = ph.ps("turned_ps", [P, 4, 512])
        mixed_ps = ph.ps("mixed", [P, 2, 512])
        over_ps = ph.ps("over", [P, W])

        def pair(n):
            return [ph.sem(f"{n}{i}") for i in range(2)]

        index_in, put_in, gathered, features_in, sent = (
            pair(n) for n in ("index_in", "put_in", "gathered", "features_in", "sent"))
        stat, state, post = ph.sem("stat"), ph.sem("state"), ph.sem("post")
        deviation, normed, turned, copied, mixed, settled, cleared, ends = (ph.sem(n) for n in (
            "deviation", "normed", "turned", "copied", "mixed", "settled", "cleared", "ends"))
        stats = Chain(stat, U + 5 + 2 + (2 if relational else 0))
        sums = Chain(state, 2 * U)
        posts = Chain(post, U + (0 if relational else 1))
        first_sem, first_sem_pe, flags_in, settled_dve = (ph.sem(n) for n in (
            "first_sent", "over_ready", "flags_in", "settled_dve"))
        block = ph.block()

        @block.sync
        def _(sp):
            for par in range(2):
                stage_index(sp, index, d["far"], Step(0, par), index_in)

            def step(b):
                ahead = b.ago(-2)
                if not relational:
                    wait(sp, state, sums.end(b.ago(2)))
                    sp.dma_start(messages[:, b.par, :, C:W],
                                 K.EDGE.rearrange("(p t) d -> p t d", p=P)[:, bass.ds(b.blk * U, U), :])\
                        .then_inc(features_in[b.par], 16)
                wait(sp, sent[b.par], 16 * U * b.k)
                stage_index(sp, put_index, put, b, put_in)
                if ahead.within(NB):
                    wait(sp, gathered[b.par], 16 * U * (b.k + 1))
                    stage_index(sp, index, d["far"], ahead, index_in)

            sweep(sp, step)

        @block.gpsimd
        def _(pool):
            def gather(b):
                wait(pool, index_in[b.par], 16 * (b.k + 1))
                wait(pool, normed, b.blk - 1)
                settle(pool, settled)
                gather_rows(pool, source, index, b.par, rows, gathered)

            def step(b):
                if b.ago(-2).within(NB):
                    gather(b.ago(-2))
                wait(pool, put_in[b.par], 16 * (b.k + 1))
                wait(pool, post, posts.end(b))
                settle(pool, settled)
                scatter_rows(pool, target, put_index, b.par, result, sent, accumulate=not relational)

            gather(Step(0, 0))
            gather(Step(0, 1))
            sweep(pool, step)
            for i in range(2):
                pool.wait_ge(sent[i], 16 * U * uses(NB, i))
            pool.wait_ge(ends, 3 if relational else 5)
            at = bass.IndirectOffsetOnAxis(ap=put_first[:, 0:1], axis=0)
            put_rows(pool, target, at, result[:, 1, 0, :], not relational).then_inc(first_sem, 16)
            pool.wait_ge(first_sem, 16)

        @block.scalar
        def _(act):
            def step(b):
                wait(act, stat, stats.end(b) - 2)
                act.activation(small["std"], small["q"], ACT.Sqrt, bias=K.eps[:, :], scale=1.0 / C)\
                    .then_inc(deviation, 1)
                wait(act, stat, stats.end(b))
                wait(act, state, sums.end(b.ago(2)))
                for u in range(U):
                    last = act.activation(messages[:, b.par, u, 0:C], rows[:, b.par, u, :], ACT.Relu,
                                          bias=small["nmr"][:, u:u + 1], scale=small["rstd"][:, u:u + 1])
                last.then_inc(normed, 1)
                wait(act, turned, b.blk + 1)
                wait(act, mixed, b.blk)
                for m in range(4):
                    part = P if m < 2 else D
                    last = act.activation(turned_sb[0:part, m, :], turned_ps[0:part, m, :], ACT.Copy)
                last.then_inc(copied, 1)

            sweep(act, step)
            act.wait_ge(turned, NB + 1)
            act.wait_ge(mixed, NB)
            act.activation(turned_sb[:, 0, 0:C], turned_ps[:, 0, 0:C], ACT.Copy).then_inc(copied, 1)
            act.activation(turned_sb[0:D, 2, 0:P], turned_ps[0:D, 2, 0:P], ACT.Copy).then_inc(copied, 1)

        @block.tensor
        def _(pe):
            def turn(par, u):
                return pe.transpose(turned_ps[:, u // 4, u % 4 * C:(u % 4 + 1) * C],
                                    states[:, par, u, 0:C], K.ident[:, :])

            def turn_features(par, u):
                return pe.transpose(turned_ps[0:D, 2 + u // 4, u % 4 * C:(u % 4 + 1) * C],
                                    states[:, par, u, C:W], K.ident[:, :])

            def mix(u):
                at = slice(u % 4 * C, (u % 4 + 1) * C)
                out = mixed_ps[:, u // 4, at]
                pe.matmul(out, turned_sb[:, u // 4, at], w[:, :], start=True, stop=False)
                return pe.matmul(out, turned_sb[0:D, 2 + u // 4, at], we[0:D, :], start=False, stop=True)

            def step(b):
                wait(pe, state, sums.end(b))
                wait(pe, copied, b.blk)
                for u in range(U):
                    turn(b.par, u)
                    last = turn_features(b.par, u)
                last.then_inc(turned, 1)
                wait(pe, copied, b.blk + 1)
                wait(pe, post, posts.end(b.ago(1)))
                for u in range(U):
                    last = mix(u)
                last.then_inc(mixed, 1)

            sweep(pe, step)
            pe.matmul(over_ps[:, :], d["to_later"][:, :], states[:, (NB - 1) % 2, U - 1, :],
                      start=True, stop=True).then_inc(first_sem_pe, 1)
            pe.wait_ge(ends, 1)
            pe.wait_ge(copied, NB)
            turn(1, 0)
            turn_features(1, 0).then_inc(turned, 1)
            pe.wait_ge(copied, NB + 2)
            pe.wait_ge(post, posts.per * NB)
            mix(0).then_inc(mixed, 1)

        @block.vector
        def _(dve):
            dve.memset(states[:, 1, U - 1, :], 0.0).then_inc(cleared, 1)
            dve.memset(head[:, :], 0.0).then_inc(cleared, 1)

            def statistics(b):
                stats.at(b)
                wait(dve, gathered[b.par], 16 * U * (b.k + 1))
                if relational:
                    wait(dve, state, sums.end(b.ago(2)))
                    x = rows[:, b.par, :, :]
                    last = stats.done(dve.tensor_tensor(x, x, middle(K.c1[:, :], U), ALU.add))
                    dve.wait_ge(stat, last)
                    stats.done(dve.tensor_tensor(messages[:, b.par, :, C:W], middle(K.iota64[:, :], U),
                                                 inner(flags[:, b.par, :, TYPE], D), ALU.is_equal))
                norm_sums(dve, stats, rows[:, b.par, :, :], U, bn, small)
                wait(dve, deviation, b.blk + 1)
                norm_scales(dve, stats, small)

            def load_flags(b):
                wait(dve, state, sums.end(b.ago(2)))
                wait(dve, post, posts.end(b.ago(2)))
                settle(dve, settled_dve)
                dve.tensor_copy(flags[:, b.par, :, :], d["flags"][:, bass.ds(b.blk * U, U), :])\
                    .then_inc(flags_in, 1)
                wait(dve, flags_in, b.blk + 1)

            def running_sums(b):
                sums.at(b)
                wait(dve, normed, b.blk + 1)
                if not relational:
                    wait(dve, features_in[b.par], 16 * (b.k + 1))
                else:
                    wait(dve, stat, stats.end(b))
                wait(dve, turned, b.blk - 1)
                dve.wait_ge(cleared, 2)
                for u in range(U):
                    before = states[:, b.par, u - 1, :] if u else states[:, 1 - b.par, U - 1, :]
                    message = messages[:, b.par, u, :]
                    wait(dve, state, sums.base + 2 * u - 1)
                    sums.done(dve.scalar_tensor_tensor(states[:, b.par, u, :], before,
                                                       flags[:, b.par, u, CONT:CONT + 1], message,
                                                       ALU.mult, ALU.add))
                    wait(dve, state, sums.base + 2 * u)
                    sums.done(dve.scalar_tensor_tensor(head[:, :], message, flags[:, b.par, u, FIRST:FIRST + 1],
                                                       head[:, :], ALU.mult, ALU.add))

            def finish(b):
                posts.at(b)
                wait(dve, mixed, b.blk + 1)
                wait(dve, sent[b.par], 16 * U * b.k)
                for u in range(U):
                    last = posts.done(dve.scalar_tensor_tensor(
                        result[:, b.par, u, :], mixed_ps[:, u // 4, u % 4 * C:(u % 4 + 1) * C],
                        flags[:, b.par, u, scale:scale + 1], bias[:, :], ALU.mult, ALU.add))
                if not relational:
                    r = result[:, b.par, :, :]
                    dve.wait_ge(post, last)
                    posts.done(dve.scalar_tensor_tensor(r, r, 0.0, middle(K.relu_b0[:, :], U),
                                                        ALU.max, ALU.subtract))

            def step(b):
                if b.within(NB):
                    load_flags(b)
                    statistics(b)
                if b.ago(1).within(NB):
                    finish(b.ago(1))
                if b.within(NB):
                    running_sums(b)

            sweep(dve, step, lag=1)
            dve.wait_ge(first_sem_pe, 1)
            dve.wait_ge(state, sums.per * NB)
            dve.wait_ge(sent[1], 16 * U * uses(NB, 1))
            line = Line(dve, ends)
            line(dve.tensor_tensor(states[:, 1, 0, :], over_ps[:, :], head[:, :], ALU.add))
            dve.wait_ge(mixed, NB + 1)
            s = d["scale_first"][:, 1:2] if relational else d["scale_first"][:, 0:1]
            r = result[:, 1, 0, :]
            line(dve.tensor_scalar(r, mixed_ps[:, 0, 0:C], s, None, ALU.mult))
            line(dve.tensor_tensor(r, r, bias[:, :], ALU.add))
            if not relational:
                line(dve.tensor_scalar(r, r, 0.0, None, ALU.max))
                line(dve.tensor_tensor(r, r, K.relu_b0[:, :], ALU.subtract))


def attention_inputs(K):
    nc, d = K.nc, K.order["s"]
    with Phase(K, "att_in") as ph:
        sides = ("far", "near")
        index = {s: ph.sb(f"index_{s}", [P, 2, U], I32) for s in sides}
        rows = {s: ph.sb(f"rows_{s}", [P, 2, U, C]) for s in sides}
        hidden = {s: ph.sb(f"hidden_{s}", [P, 2, U, C]) for s in sides}
        bn = ph.sb("bn", [P, U, 6])
        small = {s: small_tiles(ph, f"norm_{s}", U) for s in sides}
        turned_sb = {s: ph.sb(f"turned_{s}", [P, 2, 512]) for s in sides}
        heads = ph.sb("heads", [P, 2, 2, U, D])
        score = ph.sb("score", [P, U, 2])
        turned_ps = ph.ps("turned_ps", [P, 2, 512])
        far_ps = ph.ps("far_ps", [P, 4, 512])
        near_ps = ph.ps("near_ps", [P, U, 2])
        w1 = 2 * D + 2

        def pair(n):
            return [ph.sem(f"{n}{i}") for i in range(2)]

        index_in, gathered, stored = pair("index_in"), pair("gathered"), pair("stored")
        stat, out = ph.sem("stat"), ph.sem("out")
        deviation, normed, turned, copied, mixed, settled, settled_dve = (ph.sem(n) for n in (
            "deviation", "normed", "turned", "copied", "mixed", "settled", "settled_dve"))
        stats = Chain(stat, 2 * (U + 7))
        outs = Chain(out, 4 + 1 + 2)
        block = ph.block()

        @block.sync
        def _(sp):
            def index_blocks(b):
                for s in sides:
                    stage_index(sp, index[s], d[s], b, index_in)

            index_blocks(Step(0, 0))
            index_blocks(Step(0, 1))

            def step(b):
                if b.ago(-2).within(NB):
                    wait(sp, gathered[b.par], 2 * 16 * U * (b.k + 1))
                    index_blocks(b.ago(-2))
                if b.ago(1).within(NB):
                    store(b.ago(1))

            def store(b):
                wait(sp, out, outs.end(b))
                for i, table in enumerate((K.H0, K.H1)):
                    sp.dma_start(table.rearrange("(p t) d -> p t d", p=P)[:, bass.ds(b.blk * U, U), :],
                                 heads[:, b.par, i, :, :]).then_inc(stored[b.par], 16)

            sweep(sp, step, lag=1)
            for i in range(2):
                sp.wait_ge(stored[i], 32 * uses(NB, i))

        @block.gpsimd
        def _(pool):
            def step(b):
                wait(pool, index_in[b.par], 32 * (b.k + 1))
                wait(pool, normed, 2 * (b.blk - 1))
                settle(pool, settled)
                for s in sides:
                    gather_rows(pool, K.X[0:N, :], index[s], b.par, rows[s], gathered)

            sweep(pool, step)

        @block.scalar
        def _(act):
            def step(b):
                for n, s in enumerate(sides):
                    wait(act, stat, stats.per * b.blk + (n + 1) * (U + 7) - 2)
                    act.activation(small[s]["std"], small[s]["q"], ACT.Sqrt, bias=K.eps[:, :], scale=1.0 / C)\
                        .then_inc(deviation, 1)
                for n, s in enumerate(sides):
                    wait(act, stat, stats.per * b.blk + (n + 1) * (U + 7))
                    wait(act, turned, 2 * (b.blk - 2) + n + 1)
                    for u in range(U):
                        last = act.activation(hidden[s][:, b.par, u, :], rows[s][:, b.par, u, :], ACT.Relu,
                                              bias=small[s]["nmr"][:, u:u + 1],
                                              scale=small[s]["rstd"][:, u:u + 1])
                    last.then_inc(normed, 1)
                for n, s in enumerate(sides):
                    wait(act, turned, 2 * b.blk + n + 1)
                    wait(act, mixed, 2 * (b.blk - 1) + n + 1)
                    for m in range(2):
                        last = act.activation(turned_sb[s][:, m, :], turned_ps[:, m, :], ACT.Copy)
                    last.then_inc(copied, 1)

            sweep(act, step)

        @block.tensor
        def _(pe):
            def step(b):
                for n, s in enumerate(sides):
                    wait(pe, normed, 2 * b.blk + n + 1)
                    wait(pe, copied, 2 * b.blk + n)
                    for u in range(U):
                        last = pe.transpose(turned_ps[:, u // 4, u % 4 * C:(u % 4 + 1) * C],
                                            hidden[s][:, b.par, u, :], K.ident[:, :])
                    last.then_inc(turned, 1)
                wait(pe, out, outs.end(b.ago(1)))
                for n, s in enumerate(sides):
                    wait(pe, copied, 2 * b.blk + n + 1)
                    for u in range(U):
                        lhs = turned_sb[s][:, u // 4, u % 4 * C:(u % 4 + 1) * C]
                        if s == "far":
                            at = u % 2 * w1
                            last = pe.matmul(far_ps[:, u // 2, at:at + w1], lhs, K.w1[:, :], start=True, stop=True)
                        else:
                            last = pe.matmul(near_ps[:, u, :], lhs, K.w1r[:, :], start=True, stop=True)
                    last.then_inc(mixed, 1)

            sweep(pe, step)

        @block.vector
        def _(dve):
            def statistics(b):
                stats.at(b)
                wait(dve, gathered[b.par], 2 * 16 * U * (b.k + 1))
                for s in sides:
                    norm_sums(dve, stats, rows[s][:, b.par, :, :], U, bn, small[s])
                    wait(dve, deviation, 2 * b.blk + sides.index(s) + 1)
                    norm_scales(dve, stats, small[s])

            def results(b):
                outs.at(b)
                wait(dve, mixed, 2 * (b.blk + 1))
                wait(dve, stored[b.par], 32 * b.k)
                for m in range(4):
                    got = far_ps[:, m, 0:2 * w1].rearrange("p (u c) -> p u c", u=2)
                    outs.done(dve.tensor_copy(
                        heads[:, b.par, :, 2 * m:2 * m + 2, :].rearrange("p h u d -> p u h d"),
                        got[:, :, 0:2 * D].rearrange("p u (h d) -> p u h d", h=2)))
                last = outs.done(dve.tensor_copy(score[:, :, :], near_ps[:, :, :]))
                dve.wait_ge(out, last)
                settle(dve, settled_dve)
                for i in range(2):
                    columns = far_ps[:, :, 0:2 * w1].rearrange("p m (u c) -> p m u c", u=2)
                    outs.done(dve.tensor_tensor(
                        K.att[i][:, bass.ds(b.blk * U, U)].rearrange("p (m u) -> p m u", u=2),
                        columns[:, :, :, 2 * D + i], score[:, :, i].rearrange("p (m u) -> p m u", u=2),
                        ALU.add))

            def step(b):
                if b.within(NB):
                    statistics(b)
                if b.ago(1).within(NB):
                    results(b.ago(1))

            sweep(dve, step, lag=1)


def attention_weights(K):
    nc, d = K.nc, K.order["s"]
    with Phase(K, "att_w") as ph:
        cont, back = ph.sb("cont", [P, T]), d["next_cont"]
        cut, back_cut, first, first_cut, last_cut = (
            ph.sb(n, [P, T]) for n in ("cut", "back_cut", "first", "first_cut", "last_cut"))
        run, total, t1, shifted = (ph.sb(n, [P, T]) for n in ("run", "total", "t1", "shifted"))
        later_cut, earlier_cut, t2 = (ph.sb(n, [P, P]) for n in ("later_cut", "earlier_cut", "t2"))
        diag = ph.sb("diag", [P, 2, P])
        ends = ph.sb("ends", [P, 2])
        in1, in2 = ph.sb("in1", [P, 1]), ph.sb("in2", [P, 1])
        rows = ph.ps("rows", [P, 2, P])
        sums_ps = ph.ps("sums", [P, 2])
        line_sem, pe_step, act_step = ph.sem("dve_line"), ph.sem("pe_step"), ph.sem("act_step")
        ends_ready = ph.sem("ends_ready")
        exps = ph.sem("exps")
        block = ph.block()
        rounds = [(i, op) for i in range(2) for op in ("max", "add", "add")]

        @block.tensor
        def _(pe):
            for n, (_, op) in enumerate(rounds):
                pe.wait_ge(ends_ready, n + 1)
                if op == "max":
                    pe.matmul(rows[:, 0, :], K.ones[:, :], diag[:, 0, :], start=True, stop=True)
                    pe.matmul(rows[:, 1, :], K.ones[:, :], diag[:, 1, :], start=True, stop=True)\
                        .then_inc(pe_step, 1)
                else:
                    pe.matmul(sums_ps[:, 0:1], d["to_later"][:, :], ends[:, 0:1], start=True, stop=True)
                    pe.matmul(sums_ps[:, 1:2], d["from_earlier"][:, :], ends[:, 1:2], start=True, stop=True)\
                        .then_inc(pe_step, 1)

        @block.scalar
        def _(act):
            for i in range(2):
                act.wait_ge(exps, i + 1)
                act.activation(K.att[i][:, :], shifted[:, :], ACT.Exp).then_inc(act_step, 1)

        @block.vector
        def _(dve):
            line = Line(dve, line_sem)
            state = {"round": 0}
            line(dve.tensor_copy(cont[:, :], d["flags"][:, :, CONT]))
            line(dve.tensor_copy(first[:, :], d["flags"][:, :, FIRST]))
            for target, source in ((cut, cont[:, :]), (back_cut, back[:, :]), (first_cut, first[:, :]),
                                   (last_cut, d["last_seg"][:, :]), (later_cut, d["to_later"][:, :]),
                                   (earlier_cut, d["from_earlier"][:, :])):
                line(dve.tensor_scalar(target[:, :], source, BIG, -BIG, ALU.mult, ALU.add))

            def backwards(t):
                return t[:, T - 1::-1]

            def carry_ends(op):
                if op == "max":
                    line(dve.tensor_tensor_scan(backwards(total), backwards(back_cut), backwards(run),
                                                -BIG, ALU.add, ALU.max))
                else:
                    line(dve.scalar_tensor_tensor(t1[:, :], back[:, :], 0.0, run[:, :], ALU.is_equal, ALU.mult))
                    line(dve.tensor_tensor_scan(backwards(total), backwards(back), backwards(t1),
                                                0.0, ALU.mult, ALU.add))

            def segment_total(values, op):
                if op == "max":
                    line(dve.tensor_tensor_scan(run[:, :], cut[:, :], values, -BIG, ALU.add, ALU.max))
                else:
                    line(dve.tensor_tensor_scan(run[:, :], cont[:, :], values, 0.0, ALU.mult, ALU.add))
                carry_ends(op)
                line(dve.tensor_copy(ends[:, 0:1], run[:, T - 1:T]))
                if op == "max":
                    line(dve.tensor_copy(ends[:, 1:2], total[:, 0:1]))
                    line(dve.tensor_scalar(diag[:, 0, :], K.ident[:, :], ends[:, 0:1], None, ALU.mult))
                    dve.tensor_scalar(diag[:, 1, :], K.ident[:, :], ends[:, 1:2], None, ALU.mult)\
                        .then_inc(ends_ready, 1)
                else:
                    dve.tensor_copy(ends[:, 1:2], total[:, 0:1]).then_inc(ends_ready, 1)
                state["round"] += 1
                dve.wait_ge(pe_step, state["round"])
                if op == "max":
                    for m, (mask, target, edge_cut) in enumerate(((earlier_cut, in1, first_cut),
                                                                  (later_cut, in2, last_cut))):
                        line(dve.tensor_tensor(t2[:, :], mask[:, :], rows[:, m, :], ALU.add))
                        line(dve.tensor_reduce(target[:, :], t2[:, :], AX.X, ALU.max))
                        line(dve.tensor_scalar(t1[:, :], edge_cut[:, :], target[:, :], None, ALU.add))
                        line(dve.tensor_tensor(total[:, :], total[:, :], t1[:, :], ALU.max))
                else:
                    line(dve.tensor_copy(in1[:, :], sums_ps[:, 0:1]))
                    line(dve.tensor_copy(in2[:, :], sums_ps[:, 1:2]))
                    for mask, amount in ((first, in1), (d["last_seg"], in2)):
                        line(dve.scalar_tensor_tensor(total[:, :], mask[:, :], amount[:, :], total[:, :],
                                                      ALU.mult, ALU.add))

            for i in range(2):
                a = K.att[i][:, :]
                line(dve.scalar_tensor_tensor(a, a, ALPHA, a, ALU.mult, ALU.max))
                segment_total(a, "max")
                dve.tensor_tensor(shifted[:, :], a, total[:, :], ALU.subtract).then_inc(exps, 1)
                dve.wait_ge(act_step, i + 1)
                segment_total(a, "add")
                line(dve.reciprocal(t1[:, :], total[:, :]))
                line(dve.tensor_tensor(a, a, t1[:, :], ALU.mult))
                segment_total(a, "add")
                line(dve.scalar_tensor_tensor(total[:, :], total[:, :], 0.0, total[:, :], ALU.is_equal, ALU.add))
                line(dve.reciprocal(t1[:, :], total[:, :]))
                line(dve.tensor_tensor(a, a, t1[:, :], ALU.mult))


def running(dve, chain, b, states, messages, flags, head):
    chain.at(b)
    for u in range(U):
        before = states[:, b.par, u - 1, :] if u else states[:, 1 - b.par, U - 1, :]
        message = messages[:, b.par, u, :]
        wait(dve, chain.sem, chain.base + 2 * u - 1)
        chain.done(dve.scalar_tensor_tensor(states[:, b.par, u, :], before, flags[:, b.par, u, CONT:CONT + 1],
                                            message, ALU.mult, ALU.add))
        wait(dve, chain.sem, chain.base + 2 * u)
        chain.done(dve.scalar_tensor_tensor(head[:, :], message, flags[:, b.par, u, FIRST:FIRST + 1],
                                            head[:, :], ALU.mult, ALU.add))


def attention_hop1(K):
    nc, d = K.nc, K.order["s"]
    with Phase(K, "hop1") as ph:
        put_index = ph.sb("put_index", [P, 2, U], I32)
        messages = ph.sb("messages", [P, 2, U, D])
        states = ph.sb("states", [P, 2, U, D])
        head = ph.sb("head", [P, D])
        flags = ph.sb("flags", [P, 2, U, FLAGS])
        over_ps = ph.ps("over", [P, D])

        def pair(n):
            return [ph.sem(f"{n}{i}") for i in range(2)]

        put_in, rows_in, flags_in, sent = (pair(n) for n in ("put_in", "rows_in", "flags_in", "sent"))
        weigh, state = ph.sem("weigh"), ph.sem("state")
        settled, settled_dve, cleared, over, last_sem = (ph.sem(n) for n in (
            "settled", "settled_dve", "cleared", "over", "last"))
        weighed, sums = Chain(weigh, 1), Chain(state, 2 * U)
        block = ph.block()

        @block.sync
        def _(sp):
            def step(b):
                wait(sp, state, sums.end(b.ago(2)))
                sp.dma_start(messages[:, b.par, :, :],
                             K.H1.rearrange("(p t) d -> p t d", p=P)[:, bass.ds(b.blk * U, U), :])\
                    .then_inc(rows_in[b.par], 16)
                sp.dma_start(flags[:, b.par, :, :], d["flags"][:, bass.ds(b.blk * U, U), :])\
                    .then_inc(flags_in[b.par], 16)
                wait(sp, sent[b.par], 16 * U * b.k)
                stage_index(sp, put_index, d["put"], b, put_in)

            sweep(sp, step)

        @block.gpsimd
        def _(pool):
            def step(b):
                wait(pool, put_in[b.par], 16 * (b.k + 1))
                wait(pool, state, sums.end(b))
                settle(pool, settled)
                scatter_rows(pool, K.HOP[:, :], put_index, b.par, states, sent)

            sweep(pool, step)
            for i in range(2):
                pool.wait_ge(sent[i], 16 * U * uses(NB, i))
            pool.wait_ge(cleared, 3)
            at = bass.IndirectOffsetOnAxis(ap=d["put_first"][:, 0:1], axis=0)
            put_rows(pool, K.HOP[:, :], at, states[:, 1, 0, :], False).then_inc(last_sem, 16)
            pool.wait_ge(last_sem, 16)

        @block.tensor
        def _(pe):
            pe.wait_ge(state, sums.per * NB)
            pe.matmul(over_ps[:, :], d["to_later"][:, :], states[:, (NB - 1) % 2, U - 1, :],
                      start=True, stop=True).then_inc(over, 1)

        @block.vector
        def _(dve):
            dve.memset(states[:, 1, U - 1, :], 0.0).then_inc(cleared, 1)
            dve.memset(head[:, :], 0.0).then_inc(cleared, 1)

            def step(b):
                weighed.at(b)
                wait(dve, rows_in[b.par], 16 * (b.k + 1))
                wait(dve, flags_in[b.par], 16 * (b.k + 1))
                wait(dve, sent[b.par], 16 * U * b.k)
                dve.wait_ge(cleared, 2)
                settle(dve, settled_dve)
                m = messages[:, b.par, :, :]
                weighed.done(dve.tensor_tensor(m, m, inner(K.att[1][:, bass.ds(b.blk * U, U)], D), ALU.mult))
                wait(dve, weigh, weighed.end(b))
                running(dve, sums, b, states, messages, flags, head)

            sweep(dve, step)
            dve.wait_ge(over, 1)
            dve.wait_ge(sent[1], 16 * U * uses(NB, 1))
            dve.wait_ge(state, sums.per * NB)
            dve.tensor_tensor(states[:, 1, 0, :], over_ps[:, :], head[:, :], ALU.add).then_inc(cleared, 1)


def attention_hop2(K):
    nc, d = K.nc, K.order["s"]
    b1, fc, bf = K.vec["L1_gnn_b"], K.vec["L1_gnn_fc"], K.vec["L1_gnn_bf"]
    with Phase(K, "hop2") as ph:
        index = ph.sb("index", [P, 2, U], I32)
        put_index = ph.sb("put_index", [P, 2, U], I32)
        messages = ph.sb("messages", [P, 2, U, C])
        states = ph.sb("states", [P, 2, U, C])
        result = ph.sb("result", [P, 2, U, C])
        work = ph.sb("work", [P, U, C])
        nan = ph.sb("nan", [P, U, C], I32)
        gate = ph.sb("gate", [P, U, 2])
        gate_sig = ph.sb("gate_sig", [P, U, 2])
        head = ph.sb("head", [P, C])
        flags = ph.sb("flags", [P, 2, U, FLAGS])
        over_ps = ph.ps("over", [P, C])

        def pair(n):
            return [ph.sem(f"{n}{i}") for i in range(2)]

        index_in, put_in, rows_in, flags_in, gathered, sent = (
            pair(n) for n in ("index_in", "put_in", "rows_in", "flags_in", "gathered", "sent"))
        weigh, state, post, gated = ph.sem("weigh"), ph.sem("state"), ph.sem("post"), ph.sem("gated")
        settled, settled_dve, cleared, over, last_sem, ends = (ph.sem(n) for n in (
            "settled", "settled_dve", "cleared", "over", "last", "ends"))
        weighed, sums = Chain(weigh, 2), Chain(state, 2 * U)
        posts = Chain(post, 9)
        BEFORE_GATE = 6
        block = ph.block()

        @block.sync
        def _(sp):
            stage_index(sp, index, d["far"], Step(0, 0), index_in)
            stage_index(sp, index, d["far"], Step(0, 1), index_in)

            def step(b):
                wait(sp, state, sums.end(b.ago(2)))
                sp.dma_start(messages[:, b.par, :, 0:D],
                             K.H0.rearrange("(p t) d -> p t d", p=P)[:, bass.ds(b.blk * U, U), :])\
                    .then_inc(rows_in[b.par], 16)
                sp.dma_start(flags[:, b.par, :, :], d["flags"][:, bass.ds(b.blk * U, U), :])\
                    .then_inc(flags_in[b.par], 16)
                wait(sp, sent[b.par], 16 * U * b.k)
                stage_index(sp, put_index, d["add"], b, put_in)
                if b.ago(-2).within(NB):
                    wait(sp, gathered[b.par], 16 * U * (b.k + 1))
                    stage_index(sp, index, d["far"], b.ago(-2), index_in)

            sweep(sp, step)

        @block.gpsimd
        def _(pool):
            def gather(b):
                wait(pool, index_in[b.par], 16 * (b.k + 1))
                wait(pool, state, sums.end(b.ago(2)))
                settle(pool, settled)
                for u in range(U):
                    pool.indirect_dma_start(messages[:, b.par, u, D:C], None, K.HOP[:, :],
                                            bass.IndirectOffsetOnAxis(ap=index[:, b.par, u:u + 1], axis=0))\
                        .then_inc(gathered[b.par], 16)

            def step(b):
                if b.ago(-2).within(NB):
                    gather(b.ago(-2))
                wait(pool, put_in[b.par], 16 * (b.k + 1))
                wait(pool, post, posts.end(b))
                settle(pool, settled)
                scatter_rows(pool, K.X[:, :], put_index, b.par, result, sent, accumulate=True)

            gather(Step(0, 0))
            gather(Step(0, 1))
            sweep(pool, step)
            for i in range(2):
                pool.wait_ge(sent[i], 16 * U * uses(NB, i))
            pool.wait_ge(ends, 9)
            at = bass.IndirectOffsetOnAxis(ap=d["add_first"][:, 0:1], axis=0)
            put_rows(pool, K.X[:, :], at, result[:, 1, 0, :], True).then_inc(last_sem, 16)
            pool.wait_ge(last_sem, 16)

        @block.tensor
        def _(pe):
            pe.wait_ge(state, sums.per * NB)
            pe.matmul(over_ps[:, :], d["to_later"][:, :], states[:, (NB - 1) % 2, U - 1, :],
                      start=True, stop=True).then_inc(over, 1)

        @block.scalar
        def _(act):
            def gates(u):
                act.activation(gate_sig[:, 0:u, :], gate[:, 0:u, :], ACT.Sigmoid).then_inc(gated, 1)

            def step(b):
                wait(act, post, posts.base_of(b) + BEFORE_GATE)
                gates(U)

            sweep(act, step)
            act.wait_ge(ends, 6)
            gates(1)

        @block.vector
        def _(dve):
            dve.memset(states[:, 1, U - 1, :], 0.0).then_inc(cleared, 1)
            dve.memset(head[:, :], 0.0).then_inc(cleared, 1)

            def message_sums(b):
                weighed.at(b)
                wait(dve, rows_in[b.par], 16 * (b.k + 1))
                wait(dve, flags_in[b.par], 16 * (b.k + 1))
                wait(dve, gathered[b.par], 16 * U * (b.k + 1))
                wait(dve, post, posts.base_of(b.ago(2)) + 2)
                dve.wait_ge(cleared, 2)
                settle(dve, settled_dve)
                for i in range(2):
                    m = messages[:, b.par, :, i * D:(i + 1) * D]
                    weighed.done(dve.tensor_tensor(m, m, inner(K.att[i][:, bass.ds(b.blk * U, U)], D), ALU.mult))
                wait(dve, weigh, weighed.end(b))
                running(dve, sums, b, states, messages, flags, head)

            def rows_out(step_done, sem, s, v, n, wait_gate):
                w, m, g, gs = work[:, 0:n, :], nan[:, 0:n, :], gate[:, 0:n, :], gate_sig[:, 0:n, :]
                halves = lambda t: t.rearrange("p u (h d) -> p (u h) d", h=2)
                step_done(dve.tensor_tensor(m, s, s, ALU.not_equal))
                last = step_done(dve.tensor_tensor(v, s, middle(b1[:, :], n), ALU.add))
                dve.wait_ge(sem, last)
                settle(dve, settled_dve)
                last = step_done(dve.copy_predicated(v, m, middle(b1[:, :], n)))
                dve.wait_ge(sem, last)
                last = step_done(dve.tensor_tensor(w, v, middle(fc[:, :], n), ALU.mult))
                dve.wait_ge(sem, last)
                last = step_done(dve.tensor_reduce(g.rearrange("p u h -> p (u h)"), halves(w), AX.X, ALU.add))
                dve.wait_ge(sem, last)
                step_done(dve.tensor_tensor(g, g, middle(bf[:, :], n), ALU.add))
                wait_gate()
                flat = gs.rearrange("p u h -> p (u h)")
                last = step_done(dve.scalar_tensor_tensor(halves(w), halves(v), 0.0, inner(flat, D),
                                                          ALU.min, ALU.mult))
                dve.wait_ge(sem, last)
                last = step_done(dve.scalar_tensor_tensor(w, w, ALPHA, middle(K.c1[:, :], n),
                                                          ALU.mult, ALU.subtract))
                dve.wait_ge(sem, last)
                step_done(dve.scalar_tensor_tensor(v, v, 0.0, w, ALU.max, ALU.add))

            def finish(b):
                posts.at(b)
                wait(dve, state, sums.end(b))
                wait(dve, sent[b.par], 16 * U * b.k)
                wait(dve, post, posts.base_of(b))
                rows_out(posts.done, post, states[:, b.par, :, :], result[:, b.par, :, :], U,
                         lambda: wait(dve, gated, b.blk + 1))

            def step(b):
                message_sums(b)
                finish(b)

            sweep(dve, step)
            dve.wait_ge(over, 1)
            dve.wait_ge(sent[1], 16 * U * uses(NB, 1))
            dve.wait_ge(post, posts.per * NB)
            line = Chain(ends, 9)
            line.at(Step(0, 0))
            dve.tensor_tensor(states[:, 1, 0, :], over_ps[:, :], head[:, :], ALU.add).then_inc(cleared, 1)
            dve.wait_ge(cleared, 3)
            rows_out(line.done, ends, states[:, 1, 0:1, :], result[:, 1, 0:1, :], 1,
                     lambda: dve.wait_ge(gated, NB + 1))


NP = 125
R = 10
NODE_BLOCKS = N // (NP * R)
assert NODE_BLOCKS * NP * R == N
SPLIT = 112


def layer2_nodes(K):
    nc = K.nc
    with Phase(K, "nodes") as ph:
        def buf(n, parities=2):
            return ph.sb(n, [NP, parities, R, C])

        x, agg, result = buf("x"), buf("agg"), buf("result")
        base = buf("base")
        hidden = buf("hidden")
        turned_sb = ph.sb("turned_sb", [P, 3, 512])
        pre, act_out = buf("pre"), buf("act_out")
        offset = ph.sb("offset", [NP, C])
        half = ph.sb("half", [NP, R])
        bn = ph.sb("bn", [NP, 2, R, 6])
        small = [{k: ph.sb(f"n{i}_{k}", [NP, R])[:, :] for k in
                  ("diff", "sum", "m2", "sq", "q", "std", "rstd", "nmr")} for i in range(2)]
        turned_ps = ph.ps("turned_ps", [P, 3, 512])
        mixed_ps = ph.ps("mixed_ps", [P, 3, 512])

        def pair(n):
            return [ph.sem(f"{n}{i}") for i in range(2)]

        loaded, stored = pair("loaded"), pair("stored")
        names = ("added", "stat1", "stat2", "rstd1", "rstd2", "pre", "gelu", "normed1", "normed2",
                 "turned", "copied", "mixed", "out", "ready", "based", "settled")
        s = {n: ph.sem(n) for n in names}
        stats = [Chain(s["stat1"], R + 7 - 1), Chain(s["stat2"], R + 7 - 1 + 1)]
        adds, rstds = Chain(s["added"], 2), [Chain(s["rstd1"], 2), Chain(s["rstd2"], 2)]
        outs = Chain(s["out"], 2)
        block = ph.block()
        view = lambda t: t.rearrange("(p r) d -> p r d", p=NP)
        X, AGG, OUT = view(K.X[0:N, :]), view(K.AGG[:, :]), view(K.out)
        parts = (slice(0, SPLIT), slice(SPLIT, NP))
        bank = lambda u: (u // 4, slice(u % 4 * C, (u % 4 + 1) * C))

        @block.sync
        def _(sp):
            def step(b):
                wait(sp, s["normed1"], b.blk - 1)
                wait(sp, s["pre"], b.blk - 1)
                wait(sp, s["based"], b.blk - 1)
                for p in parts:
                    rows = bass.ds(b.blk * R, R)
                    sp.dma_start(x[p, b.par, :, :], X[p, rows, :]).then_inc(loaded[b.par], 16)
                    sp.dma_start(agg[p, b.par, :, :], AGG[p, rows, :]).then_inc(loaded[b.par], 16)

            sweep(sp, step, NODE_BLOCKS)

        @block.gpsimd
        def _(pool):
            pool.memset(half[:, :], -0.5).then_inc(s["ready"], 1)
            pool.tensor_tensor(offset[:, :], K.vec["L2_gnn_beta"][0:NP, :], K.vec["L3_gnn_bo"][0:NP, :], ALU.add)\
                .then_inc(s["ready"], 1)
            pool.wait_ge(s["ready"], 2)

            def sums_in(b):
                adds.at(b)
                wait(pool, loaded[b.par], 64 * (b.k + 1))
                xb, ab = x[:, b.par, :, :], agg[:, b.par, :, :]
                adds.done(pool.tensor_tensor(xb, xb, middle(K.c1[0:NP, :], R), ALU.add))
                adds.done(pool.tensor_tensor(ab, ab, middle(K.vec["L2_gnn_b_self"][0:NP, :], R), ALU.add))

            def root(b, i):
                c, sm = rstds[i], small[i]
                c.at(b)
                wait(pool, stats[i].sem, stats[i].end(b) - 1)
                settle(pool, s["settled"])
                last = c.done(pool.tensor_scalar(sm["std"], sm["q"], 1.0 / C, EPS, ALU.mult, ALU.add))
                wait(pool, c.sem, last)
                c.done(pool.tensor_tensor(sm["rstd"], sm["std"], half[:, :], ALU.pow))

            def step(b):
                if b.within(NODE_BLOCKS):
                    sums_in(b)
                    root(b, 0)
                if b.ago(1).within(NODE_BLOCKS):
                    root(b.ago(1), 1)
                if b.within(NODE_BLOCKS):
                    wait(pool, s["out"], outs.end(b.ago(2)))
                    pool.tensor_tensor(base[:, b.par, :, :], x[:, b.par, :, :], middle(offset[:, :], R), ALU.add)\
                        .then_inc(s["based"], 1)
                if b.ago(2).within(NODE_BLOCKS):
                    store(b.ago(2))

            def store(b):
                wait(pool, s["out"], outs.end(b))
                settle(pool, s["settled"])
                pool.dma_start(OUT[:, bass.ds(b.blk * R, R), :], result[:, b.par, :, :])\
                    .then_inc(stored[b.par], 16)

            sweep(pool, step, NODE_BLOCKS, lag=2)
            for i in range(2):
                pool.wait_ge(stored[i], 16 * uses(NODE_BLOCKS, i))

        @block.scalar
        def _(act):
            def norm(b, i, source, target, func):
                wait(act, stats[i].sem, stats[i].end(b))
                for u in range(R):
                    last = act.activation(target[:, b.par, u, :], source[:, b.par, u, :], func,
                                          bias=small[i]["nmr"][:, u:u + 1], scale=small[i]["rstd"][:, u:u + 1])
                return last

            def step(b):
                before = b.ago(1)
                if before.within(NODE_BLOCKS):
                    wait(act, s["pre"], before.blk + 1)
                    act.activation(act_out[:, before.par, :, :], pre[:, before.par, :, :], ACT.Gelu)\
                        .then_inc(s["gelu"], 1)
                if b.within(NODE_BLOCKS):
                    wait(act, s["stat2"], stats[1].base_of(b.ago(2)) + 1)
                    wait(act, s["turned"], b.blk - 1)
                    norm(b, 0, x, hidden, ACT.Relu).then_inc(s["normed1"], 1)
                    wait(act, s["turned"], b.blk + 1)
                    wait(act, s["mixed"], b.blk)
                    for m in range(3):
                        w = min(4, R - 4 * m) * NP
                        last = act.activation(turned_sb[:, m, 0:w], turned_ps[:, m, 0:w], ACT.Copy)
                    last.then_inc(s["copied"], 1)
                if before.within(NODE_BLOCKS):
                    norm(before, 1, act_out, act_out, ACT.Identity).then_inc(s["normed2"], 1)

            sweep(act, step, NODE_BLOCKS, lag=1)

        @block.tensor
        def _(pe):
            def step(b):
                wait(pe, s["normed1"], b.blk + 1)
                wait(pe, s["copied"], b.blk)
                for u in range(R):
                    last = pe.transpose(turned_ps[:, u // 4, u % 4 * NP:(u % 4 + 1) * NP],
                                        hidden[:, b.par, u, :], K.ident[0:NP, 0:NP])
                last.then_inc(s["turned"], 1)
                wait(pe, s["copied"], b.blk + 1)
                wait(pe, s["pre"], b.blk)
                for u in range(R):
                    m, at = bank(u)
                    last = pe.matmul(mixed_ps[0:NP, m, at], turned_sb[:, m, u % 4 * NP:(u % 4 + 1) * NP],
                                     K.wself[:, :], start=True, stop=True)
                last.then_inc(s["mixed"], 1)

            sweep(pe, step, NODE_BLOCKS)

        @block.vector
        def _(dve):
            def statistics(b, i, rows):
                c = stats[i]
                norm_sums(dve, c, rows, R, bn[:, i, :, :], small[i])

            def scales(b, i):
                wait(dve, rstds[i].sem, rstds[i].end(b))
                c, sm = stats[i], small[i]
                c.base, c.n = c.base_of(b), c.per - 1
                c.done(dve.scalar_tensor_tensor(sm["nmr"], sm["sum"], -0.5, sm["rstd"], ALU.mult, ALU.mult))

            def step(b):
                before, older = b.ago(1), b.ago(2)
                if before.within(NODE_BLOCKS):
                    wait(dve, s["mixed"], before.blk + 1)
                    wait(dve, s["added"], adds.end(before))
                    wait(dve, s["gelu"], before.blk - 1)
                    for m in range(3):
                        n = min(4, R - 4 * m)
                        got = mixed_ps[0:NP, m, 0:n * C].rearrange("p (u c) -> p u c", c=C)
                        last = dve.tensor_tensor(pre[:, before.par, 4 * m:4 * m + n, :], got,
                                                 agg[:, before.par, 4 * m:4 * m + n, :], ALU.add)
                    last.then_inc(s["pre"], 1)
                if b.within(NODE_BLOCKS):
                    stats[0].at(b)
                    wait(dve, s["added"], adds.base_of(b) + 1)
                    statistics(b, 0, x[:, b.par, :, :])
                    scales(b, 0)
                if before.within(NODE_BLOCKS):
                    stats[1].at(before)
                    wait(dve, s["gelu"], before.blk + 1)
                    a = act_out[:, before.par, :, :]
                    last = stats[1].done(dve.tensor_tensor(a, a, hidden[:, before.par, :, :], ALU.add))
                    wait(dve, s["stat2"], last)
                    statistics(before, 1, a)
                if older.within(NODE_BLOCKS):
                    results(older)
                if before.within(NODE_BLOCKS):
                    scales(before, 1)

            def results(b):
                outs.at(b)
                wait(dve, s["normed2"], b.blk + 1)
                wait(dve, stored[b.par], 16 * b.k)
                wait(dve, s["based"], b.blk + 1)
                r = result[:, b.par, :, :]
                last = outs.done(dve.tensor_tensor(r, act_out[:, b.par, :, :],
                                                   middle(K.vec["L2_gnn_gamma"][0:NP, :], R), ALU.mult))
                wait(dve, s["out"], last)
                outs.done(dve.tensor_tensor(r, r, base[:, b.par, :, :], ALU.add))

            sweep(dve, step, NODE_BLOCKS, lag=2)


def scores(K):
    nc, d = K.nc, K.order["s"]
    with Phase(K, "scores") as ph:
        sides = ("near", "far")
        G = U // 2
        index = {s: ph.sb(f"index_{s}", [P, 2, U], I32) for s in sides}
        rows = {s: ph.sb(f"rows_{s}", [P, 2, U, C]) for s in sides}
        plain = ph.sb("plain", [P, U, C])
        hidden = {s: ph.sb(f"hidden_{s}", [P, U, C]) for s in sides}
        bn = ph.sb("bn", [P, U, 6])
        small = {s: small_tiles(ph, f"norm_{s}", U) for s in sides}
        turned_sb = {s: ph.sb(f"turned_{s}", [P, 2, 512]) for s in sides}
        q_sb, k_sb = ph.sb("q_sb", [P, G, C]), ph.sb("k_sb", [P, G, C])
        values = ph.sb("values", [P, 2, U, C])
        score = ph.sb("score", [P, 2, U, HEADS])
        means = ph.sb("means", [P, 2, U])
        turned_ps = ph.ps("turned_ps", [P, 2, 512])
        q_ps = ph.ps("q_ps", [P, 512])
        kv_ps = ph.ps("kv_ps", [P, 2, 512])
        mean_ps = ph.ps("mean_ps", [P, 2, U])

        def pair(n):
            return [ph.sem(f"{n}{i}") for i in range(2)]

        index_in, gathered, v_out, row_out = pair("index_in"), pair("gathered"), pair("v_out"), pair("row_out")
        stat, out = ph.sem("stat"), ph.sem("out")
        deviation, normed, turned, copied, mixed, settled, settled_dve, kept_sem = (ph.sem(n) for n in (
            "deviation", "normed", "turned", "copied", "mixed", "settled", "settled_dve", "kept"))
        SIDE = 1 + U + 7
        stats = Chain(stat, 2 * SIDE)
        outs = Chain(out, 2 * 5 + 2)
        block = ph.block()

        @block.sync
        def _(sp):
            def index_blocks(b):
                for s in sides:
                    stage_index(sp, index[s], d[s], b, index_in)

            index_blocks(Step(0, 0))
            index_blocks(Step(0, 1))
            at = lambda table, b: table.rearrange("(p t) d -> p t d", p=P)[:, bass.ds(b.blk * U, U), :]

            def step(b):
                if b.within(NB):
                    wait(sp, gathered[b.par], 2 * 16 * U * (b.k + 1))
                    sp.dma_start(at(K.ROW, b), rows["near"][:, b.par, :, :]).then_inc(row_out[b.par], 16)
                if b.ago(-2).within(NB):
                    index_blocks(b.ago(-2))
                if b.ago(1).within(NB):
                    before = b.ago(1)
                    wait(sp, out, outs.end(before))
                    sp.dma_start(at(K.V, before), values[:, before.par, :, :]).then_inc(v_out[before.par], 16)

            sweep(sp, step, lag=1)
            for i in range(2):
                sp.wait_ge(row_out[i], 16 * uses(NB, i))
                sp.wait_ge(v_out[i], 16 * uses(NB, i))

        @block.gpsimd
        def _(pool):
            def step(b):
                wait(pool, index_in[b.par], 32 * (b.k + 1))
                wait(pool, row_out[b.par], 16 * b.k)
                wait(pool, stat, stats.base_of(b.ago(2)) + SIDE + 1)
                settle(pool, settled)
                for s in sides:
                    gather_rows(pool, K.out, index[s], b.par, rows[s], gathered)

            sweep(pool, step)

        @block.scalar
        def _(act):
            def step(b):
                for n, s in enumerate(sides):
                    at = stats.base_of(b) + (n + 1) * SIDE
                    wait(act, stat, at - 2)
                    act.activation(small[s]["std"], small[s]["q"], ACT.Sqrt, bias=K.eps[:, :], scale=1.0 / C)\
                        .then_inc(deviation, 1)
                    wait(act, stat, at)
                    wait(act, turned, 2 * (b.blk - 1) + n + 1)
                    for u in range(U):
                        last = act.activation(hidden[s][:, u, :], plain[:, u, :], ACT.Relu,
                                              bias=small[s]["nmr"][:, u:u + 1],
                                              scale=small[s]["rstd"][:, u:u + 1])
                    last.then_inc(normed, 1)
                for n, s in enumerate(sides):
                    wait(act, turned, 2 * b.blk + n + 1)
                    wait(act, mixed, 2 * b.blk)
                    for m in range(2):
                        last = act.activation(turned_sb[s][:, m, :], turned_ps[:, m, :], ACT.Copy)
                    last.then_inc(copied, 1)

            sweep(act, step)

        @block.tensor
        def _(pe):
            def step(b):
                for n, s in enumerate(sides):
                    wait(pe, normed, 2 * b.blk + n + 1)
                    wait(pe, copied, 2 * b.blk + n)
                    for u in range(U):
                        last = pe.transpose(turned_ps[:, u // 4, u % 4 * C:(u % 4 + 1) * C],
                                            hidden[s][:, u, :], K.ident[:, :])
                    last.then_inc(turned, 1)
                wait(pe, copied, 2 * (b.blk + 1))
                for half in range(2):
                    wait(pe, out, outs.base_of(b) + 5 if half else outs.end(b.ago(1)))
                    for g in range(G):
                        near = turned_sb["near"][:, half, g * C:(g + 1) * C]
                        far = turned_sb["far"][:, half, g * C:(g + 1) * C]
                        pe.matmul(q_ps[:, g * C:(g + 1) * C], near, K.wq[:, 0:C], start=True, stop=True)
                        pe.matmul(mean_ps[:, 0, half * G + g:half * G + g + 1], near, K.wq[:, C:C + 1],
                                  start=True, stop=True)
                        pe.matmul(kv_ps[:, g // 2, g % 2 * 2 * C:(g % 2 + 1) * 2 * C], far, K.wkv[:, 0:2 * C],
                                  start=True, stop=True)
                        last = pe.matmul(mean_ps[:, 1, half * G + g:half * G + g + 1], far,
                                         K.wkv[:, 2 * C:2 * C + 1], start=True, stop=True)
                    last.then_inc(mixed, 1)

            sweep(pe, step)

        @block.vector
        def _(dve):
            def statistics(b):
                stats.at(b)
                wait(dve, gathered[b.par], 2 * 16 * U * (b.k + 1))
                for n, s in enumerate(sides):
                    wait(dve, normed, 2 * b.blk + n)
                    last = stats.done(dve.tensor_tensor(plain[:, :, :], rows[s][:, b.par, :, :],
                                                        middle(K.vec["L3_gnn_bo"][:, :], U), ALU.subtract))
                    wait(dve, stat, last)
                    norm_sums(dve, stats, plain, U, bn, small[s])
                    wait(dve, deviation, 2 * b.blk + n + 1)
                    norm_scales(dve, stats, small[s])

            def products(b):
                outs.at(b)
                wait(dve, v_out[b.par], 16 * b.k)
                wait(dve, kept_sem, 2 * (b.blk - 1))
                for half in range(2):
                    wait(dve, mixed, 2 * b.blk + half + 1)
                    wait(dve, out, outs.base + 5 * half)
                    g3 = lambda t: t.rearrange("p (g c) -> p g c", c=C)
                    bias = lambda n: middle(K.vec[n][:, :], G)
                    outs.done(dve.tensor_tensor(q_sb[:, :, :], g3(q_ps[:, :]), bias("L3_gnn_bq"), ALU.add))
                    kv = kv_ps[:, :, :].rearrange("p m (g c) -> p (m g) c", g=2)
                    last = outs.done(dve.tensor_tensor(k_sb[:, :, :], kv[:, :, 0:C], bias("L3_gnn_bk"), ALU.add))
                    outs.done(dve.tensor_tensor(values[:, b.par, half * G:(half + 1) * G, :], kv[:, :, C:2 * C],
                                                bias("L3_gnn_bv"), ALU.add))
                    wait(dve, out, last)
                    last = outs.done(dve.tensor_tensor(q_sb[:, :, :], q_sb[:, :, :], k_sb[:, :, :], ALU.mult))
                    wait(dve, out, last)
                    outs.done(dve.tensor_reduce(
                        score[:, b.par, half * G:(half + 1) * G, :].rearrange("p g h -> p (g h)"),
                        q_sb[:, :, :].rearrange("p g (h e) -> p (g h) e", e=HD), AX.X, ALU.add))
                last = outs.done(dve.tensor_copy(means[:, 0, :], mean_ps[:, 0, :]))
                wait(dve, out, last)
                last = outs.done(dve.tensor_tensor(means[:, 1, :], mean_ps[:, 1, :], means[:, 0, :], ALU.subtract))
                wait(dve, out, last)
                settle(dve, settled_dve)
                dve.tensor_copy(K.score[:, bass.ds(b.blk * U, U), :], score[:, b.par, :, :]).then_inc(kept_sem, 1)
                dve.tensor_copy(K.mean_diff[:, bass.ds(b.blk * U, U)], means[:, 1, :]).then_inc(kept_sem, 1)

            def step(b):
                if b.within(NB):
                    statistics(b)
                if b.ago(1).within(NB):
                    products(b.ago(1))

            sweep(dve, step, lag=1)


def score_softmax(K):
    nc, d = K.nc, K.order["s"]
    with Phase(K, "softmax") as ph:
        t1 = ph.sb("t1", [P, T, HEADS])
        cut = ph.sb("cut", [P, T])
        top = ph.sb("top", [P, HEADS])
        top8 = ph.sb("top8", [HEADS, 1])
        diag = ph.sb("diag", [HEADS, HEADS])
        total = ph.sb("total", [P, HEADS])
        turned_ps = ph.ps("turned_ps", [HEADS, P])
        max_ps = ph.ps("max_ps", [P, HEADS])
        sum_ps = ph.ps("sum_ps", [P, HEADS])
        line_sem, ready, pe_step, act_step = (ph.sem(n) for n in ("line", "ready", "pe_step", "act_step"))
        block = ph.block()
        by_head = lambda t: t.rearrange("p t h -> p h t")

        @block.tensor
        def _(pe):
            pe.wait_ge(ready, 1)
            pe.transpose(turned_ps[:, :], top[:, :], K.ident[:, :]).then_inc(pe_step, 1)
            pe.wait_ge(ready, 2)
            pe.matmul(max_ps[:, :], K.ones[0:HEADS, :], diag[:, :], start=True, stop=True).then_inc(pe_step, 1)
            pe.wait_ge(ready, 4)
            pe.matmul(sum_ps[:, :], K.ones[:, :], total[:, :], start=True, stop=True).then_inc(pe_step, 1)

        @block.scalar
        def _(act):
            act.wait_ge(ready, 3)
            act.activation(K.score[:, :, :], K.score[:, :, :], ACT.Exp).then_inc(act_step, 1)

        @block.vector
        def _(dve):
            line = Line(dve, line_sem)
            sc = K.score[:, :, :]
            line(dve.scalar_tensor_tensor(sc, sc, float(1 / np.sqrt(HD)), inner(d["weight"][:, :], HEADS),
                                          ALU.mult, ALU.add))
            line(dve.tensor_tensor(t1[:, :, :], inner(K.mean_diff[:, :], HEADS), middle(K.vec["L3_gnn_Wd"][:, :], T),
                                   ALU.mult))
            line(dve.tensor_tensor(sc, sc, t1[:, :, :], ALU.add))
            line(dve.tensor_tensor(sc, sc, middle(K.vec["L3_gnn_bd"][:, :], T), ALU.add))
            line(dve.tensor_scalar(cut[:, :], d["real"][:, :], BIG, -BIG, ALU.mult, ALU.add))
            line(dve.tensor_tensor(sc, sc, inner(cut[:, :], HEADS), ALU.add))
            dve.tensor_reduce(top[:, :], by_head(sc), AX.X, ALU.max).then_inc(ready, 1)
            dve.wait_ge(pe_step, 1)
            line(dve.tensor_reduce(top8[:, :], turned_ps[:, :], AX.X, ALU.max))
            dve.tensor_scalar(diag[:, :], K.ident[0:HEADS, 0:HEADS], top8[:, :], None, ALU.mult).then_inc(ready, 1)
            dve.wait_ge(pe_step, 2)
            line(dve.tensor_copy(top[:, :], max_ps[:, :]))
            dve.tensor_tensor(sc, sc, middle(top[:, :], T), ALU.subtract).then_inc(ready, 1)
            dve.wait_ge(act_step, 1)
            dve.tensor_reduce(total[:, :], by_head(sc), AX.X, ALU.add).then_inc(ready, 1)
            dve.wait_ge(pe_step, 3)
            line(dve.reciprocal(total[:, :], sum_ps[:, :]))
            line(dve.tensor_tensor(sc, sc, middle(total[:, :], T), ALU.mult))


def layer3(K):
    nc, d = K.nc, K.order["s"]
    with Phase(K, "layer3") as ph:
        put_index = ph.sb("put_index", [P, 2, U], I32)
        messages = ph.sb("messages", [P, 2, U, C])
        own = ph.sb("own", [P, 2, U, C])
        own_first = ph.sb("own_first", [P, C])
        states = ph.sb("states", [P, 2, U, C])
        result = ph.sb("result", [P, 2, U, C])
        head = ph.sb("head", [P, C])
        flags = ph.sb("flags", [P, 2, U, FLAGS])
        turned_sb = ph.sb("turned_sb", [P, 2, 512])
        turned_ps = ph.ps("turned_ps", [P, 2, 512])
        mixed_ps = ph.ps("mixed_ps", [P, 2, 512])
        over_ps = ph.ps("over", [P, C])

        def pair(n):
            return [ph.sem(f"{n}{i}") for i in range(2)]

        put_in, rows_in, flags_in, own_in, sent = (pair(n) for n in ("put_in", "rows_in", "flags_in", "own_in", "sent"))
        weigh, state, post = ph.sem("weigh"), ph.sem("state"), ph.sem("post")
        settled, settled_dve, cleared, over, last_sem, turned, copied, mixed, first_in = (ph.sem(n) for n in (
            "settled", "settled_dve", "cleared", "over", "last", "turned", "copied", "mixed", "first_in"))
        weighed, sums, posts = Chain(weigh, 1), Chain(state, 2 * U), Chain(post, 2)
        block = ph.block()

        @block.sync
        def _(sp):
            at = lambda table, b: table.rearrange("(p t) d -> p t d", p=P)[:, bass.ds(b.blk * U, U), :]
            sp.dma_start(own_first[:, :], K.ROW.rearrange("(p t) d -> p t d", p=P)[:, 0, :]).then_inc(first_in, 16)

            def step(b):
                wait(sp, state, sums.end(b.ago(2)))
                sp.dma_start(messages[:, b.par, :, :], at(K.V, b)).then_inc(rows_in[b.par], 16)
                sp.dma_start(flags[:, b.par, :, :], d["flags"][:, bass.ds(b.blk * U, U), :])\
                    .then_inc(flags_in[b.par], 16)
                wait(sp, post, posts.end(b.ago(2)))
                sp.dma_start(own[:, b.par, :, :], at(K.ROW, b)).then_inc(own_in[b.par], 16)
                wait(sp, sent[b.par], 16 * U * b.k)
                stage_index(sp, put_index, d["put"], b, put_in)

            sweep(sp, step)

        @block.gpsimd
        def _(pool):
            def step(b):
                wait(pool, put_in[b.par], 16 * (b.k + 1))
                wait(pool, post, posts.end(b))
                settle(pool, settled)
                scatter_rows(pool, K.out, put_index, b.par, result, sent)

            sweep(pool, step)
            for i in range(2):
                pool.wait_ge(sent[i], 16 * U * uses(NB, i))
            pool.wait_ge(cleared, 4)
            at = bass.IndirectOffsetOnAxis(ap=d["put_first"][:, 0:1], axis=0)
            put_rows(pool, K.out, at, result[:, 1, 0, :], False).then_inc(last_sem, 16)
            pool.wait_ge(last_sem, 16)

        @block.scalar
        def _(act):
            def step(b):
                wait(act, turned, b.blk + 1)
                wait(act, mixed, b.blk)
                for m in range(2):
                    last = act.activation(turned_sb[:, m, :], turned_ps[:, m, :], ACT.Copy)
                last.then_inc(copied, 1)

            sweep(act, step)
            act.wait_ge(turned, NB + 1)
            act.wait_ge(mixed, NB)
            act.activation(turned_sb[:, 0, 0:C], turned_ps[:, 0, 0:C], ACT.Copy).then_inc(copied, 1)

        @block.tensor
        def _(pe):
            tile_at = lambda t, u: t[:, u // 4, u % 4 * C:(u % 4 + 1) * C]

            def step(b):
                wait(pe, state, sums.end(b))
                wait(pe, copied, b.blk)
                for u in range(U):
                    last = pe.transpose(tile_at(turned_ps, u), states[:, b.par, u, :], K.ident[:, :])
                last.then_inc(turned, 1)
                wait(pe, copied, b.blk + 1)
                wait(pe, post, posts.end(b.ago(1)))
                for u in range(U):
                    last = pe.matmul(tile_at(mixed_ps, u), tile_at(turned_sb, u), K.wo[:, :], start=True, stop=True)
                last.then_inc(mixed, 1)

            sweep(pe, step)
            pe.matmul(over_ps[:, :], d["to_later"][:, :], states[:, (NB - 1) % 2, U - 1, :],
                      start=True, stop=True).then_inc(over, 1)
            pe.wait_ge(cleared, 3)
            pe.wait_ge(copied, NB)
            pe.transpose(tile_at(turned_ps, 0), states[:, 1, 0, :], K.ident[:, :]).then_inc(turned, 1)
            pe.wait_ge(copied, NB + 1)
            pe.wait_ge(post, posts.per * NB)
            pe.matmul(tile_at(mixed_ps, 0), tile_at(turned_sb, 0), K.wo[:, :], start=True, stop=True).then_inc(mixed, 1)

        @block.vector
        def _(dve):
            dve.memset(states[:, 1, U - 1, :], 0.0).then_inc(cleared, 1)
            dve.memset(head[:, :], 0.0).then_inc(cleared, 1)

            def message_sums(b):
                weighed.at(b)
                wait(dve, rows_in[b.par], 16 * (b.k + 1))
                wait(dve, flags_in[b.par], 16 * (b.k + 1))
                wait(dve, turned, b.blk - 1)
                dve.wait_ge(cleared, 2)
                settle(dve, settled_dve)
                m = messages[:, b.par, :, :].rearrange("p u (h e) -> p (u h) e", e=HD)
                share = K.score[:, bass.ds(b.blk * U, U), :].rearrange("p u h -> p (u h)")
                weighed.done(dve.tensor_tensor(m, m, inner(share, HD), ALU.mult))
                wait(dve, weigh, weighed.end(b))
                running(dve, sums, b, states, messages, flags, head)

            def finish(b):
                posts.at(b)
                wait(dve, mixed, b.blk + 1)
                wait(dve, own_in[b.par], 16 * (b.k + 1))
                wait(dve, sent[b.par], 16 * U * b.k)
                for m in range(2):
                    part = slice(4 * m, 4 * m + 4)
                    posts.done(dve.tensor_tensor(result[:, b.par, part, :],
                                                 mixed_ps[:, m, :].rearrange("p (u c) -> p u c", c=C),
                                                 own[:, b.par, part, :], ALU.add))

            def step(b):
                if b.within(NB):
                    message_sums(b)
                if b.ago(1).within(NB):
                    finish(b.ago(1))

            sweep(dve, step, lag=1)
            dve.wait_ge(over, 1)
            dve.wait_ge(first_in, 16)
            dve.wait_ge(sent[1], 16 * U * uses(NB, 1))
            dve.wait_ge(state, sums.per * NB)
            dve.tensor_tensor(states[:, 1, 0, :], over_ps[:, :], head[:, :], ALU.add).then_inc(cleared, 1)
            dve.wait_ge(mixed, NB + 1)
            dve.tensor_tensor(result[:, 1, 0, :], mixed_ps[:, 0, 0:C], own_first[:, :], ALU.add).then_inc(cleared, 1)


_OUT = ("out_0", (N, C))


def kernel(**inputs):
    import concourse.bacc as _bacc
    from concourse.bass_utils import run_bass_kernel_spmd as _run

    nc = _bacc.Bacc("TRN2", target_bir_lowering=False, num_devices=1)
    arrays, A = {}, {}
    for name, value in inputs.items():
        a = np.ascontiguousarray(value)
        arrays[f"in_{name}"] = a
        A[name] = nc.dram_tensor(f"in_{name}", a.shape, mybir.dt.from_np(a.dtype), kind="ExternalInput").ap()
    out = nc.dram_tensor(_OUT[0], _OUT[1], F32, kind="ExternalOutput").ap()
    build(nc, A, out)
    r = _run(nc, [arrays], core_ids=[0])
    return r.results[0][_OUT[0]]
```

```python
import numpy as np
from contextlib import ExitStack

import concourse.bass as bass
from concourse import mybir

F32 = mybir.dt.float32
I32 = mybir.dt.int32
BF16 = mybir.dt.bfloat16
ALU = mybir.AluOpType
ACT = mybir.ActivationFunctionType
AX = mybir.AxisListType

P = 128
N = 100000
E = 50000
C = 128
D = 64
HEADS = 8
HD = C // HEADS
U = 8
NB = -(-E // (P * U))
T = NB * U
EP = P * T
FULL = E // T
REST = E - FULL * T
SKIP = 1 << 20
BIG = 1e30
EPS = 1e-5
LO = 512
HI = 256
GROUP = 4
ALPHA = 0.2
FLAGS = 5
CONT, FIRST, RSQRT, RDEG, TYPE = range(FLAGS)
SLICE_PARTS, SLICES = 80, 50
assert NB == SLICES - 1
assert NB % 2 == 1 and FULL == P - 1


class Step:

    def __init__(self, k, par, quad=None, slot=None):
        self.k, self.par, self.blk = k, par, 2 * k + par
        self.quad, self.slot = quad, slot

    def ago(self, n):
        at = self.par - n
        if self.slot is None:
            return Step(self.k + at // 2, at % 2)
        slot = self.slot - n
        return Step(self.k + at // 2, at % 2, self.quad + slot // 4, slot % 4)

    def within(self, blocks):
        return not isinstance(self.blk, int) or 0 <= self.blk < blocks


def sweep(eng, body, blocks=NB, lag=0):
    body(Step(0, 0))
    body(Step(0, 1))
    pairs_end = (blocks - 3) // 2
    with eng.Fori(1, pairs_end) as k:
        body(Step(k, 0))
        body(Step(k, 1))
    for blk in range(2 * pairs_end, blocks + lag):
        body(Step(blk // 2, blk % 2))


def sweep_by_4(eng, body, blocks, lag):
    for blk in range(4):
        body(Step(blk // 2, blk % 2, 0, blk))
    with eng.Fori(1, blocks // 4 - 1) as k:
        for slot in range(4):
            body(Step(2 * k + slot // 2, slot % 2, k, slot))
    for blk in range(blocks // 4 * 4 - 4, blocks + lag):
        body(Step(blk // 2, blk % 2, blk // 4, blk % 4))


def wait(eng, sem, value):
    if not isinstance(value, int) or value > 0:
        eng.wait_ge(sem, value)


def settle(eng, sem):
    eng.sem_inc(sem, 1)


class Chain:

    def __init__(self, sem, per):
        self.sem, self.per = sem, per

    def at(self, step):
        self.base, self.n = step.blk * self.per, 0

    def base_of(self, step):
        return step.blk * self.per

    def done(self, instruction):
        instruction.then_inc(self.sem, 1)
        self.n += 1
        assert self.n <= self.per
        return self.base + self.n

    def end(self, step):
        return (step.blk + 1) * self.per


class Line:

    def __init__(self, eng, sem):
        self.eng, self.sem, self.n = eng, sem, 0

    def __call__(self, instruction):
        self.n += 1
        instruction.then_inc(self.sem, 1)
        self.eng.wait_ge(self.sem, self.n)


def middle(vector, n):
    return vector.unsqueeze(1).to_broadcast([vector.shape[0], n, vector.shape[1]])


def inner(vector, n):
    return vector.unsqueeze(2).to_broadcast([vector.shape[0], vector.shape[1], n])


class Kernel:
    pass


def build(nc, A, out):
    K = Kernel()
    K.nc, K.A, K.out = nc, A, out
    with ExitStack() as keep:
        K.keep = keep
        declare(K)
        phases = (setup_tables, sort_by_src, sort_by_dst, order_tables, layer0, attention_inputs, attention_weights,
                  attention_hop1, attention_hop2, layer2, layer2_nodes, scores, score_softmax, layer3)
        for phase in phases:
            phase(K)


def dram(K, name, shape, dt=F32):
    return K.nc.dram_tensor(name, shape, dt).ap()


def kept(K, name, shape, dt=F32):
    return K.keep.enter_context(K.nc.sbuf_tensor(name, shape, dt))


class Phase:

    def __init__(self, K, name):
        self.K, self.name = K, name

    def __enter__(self):
        self.stack = ExitStack()
        self.sems = []
        return self

    def __exit__(self, *error):
        self.stack.close()
        self.K.nc.clear_and_free_semaphores(self.sems)
        self.K.nc.all_engine_barrier()

    def sb(self, name, shape, dt=F32):
        return self.stack.enter_context(self.K.nc.sbuf_tensor(f"{self.name}_{name}", shape, dt))

    def ps(self, name, shape, dt=F32):
        return self.stack.enter_context(self.K.nc.psum_tensor(f"{self.name}_{name}", shape, dt))

    def sem(self, name):
        self.sems.append(self.K.nc.alloc_semaphore(f"{self.name}_{name}"))
        return self.sems[-1]

    def block(self):
        return self.stack.enter_context(self.K.nc.Block())


def declare(K):
    K.X = dram(K, "node_states", (N + EP, C))
    K.HOP = dram(K, "hop1_rows", (N, D))
    K.AGG = dram(K, "relation_rows", (N, C))
    K.PASS1 = dram(K, "sorted_by_low_digit", (EP, 4), I32)
    K.COUNTS = dram(K, "digit_counts", (T // GROUP, LO))
    K.BY_SRC = dram(K, "edges_by_src", (EP + 2, 4), I32)
    K.BY_DST = dram(K, "edges_by_dst", (EP + 2, 4), I32)
    K.EDGE = dram(K, "edge_features", (EP, D))
    K.H0 = dram(K, "col_rows_head0", (EP, D))
    K.H1 = dram(K, "col_rows_head1", (EP, D))
    K.V = dram(K, "value_rows", (EP, C))
    K.ROW = dram(K, "row_states", (EP, C))

    K.ident = kept(K, "ident", [P, P])
    K.ones = kept(K, "ones", [P, P])
    K.eps = kept(K, "eps", [P, 1])
    K.below = kept(K, "below", [P, P])
    K.above = kept(K, "above", [P, P])
    K.iota64 = kept(K, "iota64", [P, D])
    K.w0 = kept(K, "w0", [P, C])
    K.w0e = kept(K, "w0e", [D, C])
    K.w1 = kept(K, "w1", [P, 2 * D + 2])
    K.w1r = kept(K, "w1r", [P, 2])
    K.wmsg = kept(K, "wmsg", [P, C])
    K.wrel = kept(K, "wrel", [D, C])
    K.wself = kept(K, "wself", [P, C])
    K.wq = kept(K, "wq", [P, C])
    K.wkv = kept(K, "wkv", [P, 2 * C])
    K.wo = kept(K, "wo", [P, C])
    K.vec = {n: kept(K, f"v_{n}", [P, size]) for n, size in VECTORS}
    K.relu_b0 = kept(K, "relu_b0", [P, C])
    K.c1 = kept(K, "c1", [P, C])
    K.x2_less_x = kept(K, "x2_less_x", [P, C])
    K.bias2 = kept(K, "bias2", [P, C])
    K.order = {}
    for o in ("s", "d"):
        K.order[o] = {
            "near": kept(K, f"near_{o}", [P, T], I32),
            "far": kept(K, f"far_{o}", [P, T], I32),
            "put": kept(K, f"put_{o}", [P, T], I32),
            "add": kept(K, f"add_{o}", [P, T], I32),
            "put_first": kept(K, f"put_first_{o}", [P, 1], I32),
            "add_first": kept(K, f"add_first_{o}", [P, 1], I32),
            "flags": kept(K, f"flags_{o}", [P, T, FLAGS]),
            "scale_first": kept(K, f"scale_first_{o}", [P, 2]),
            "to_later": kept(K, f"to_later_{o}", [P, P]),
            "from_earlier": kept(K, f"from_earlier_{o}", [P, P]),
            "last_seg": kept(K, f"last_seg_{o}", [P, T]),
            "next_cont": kept(K, f"next_cont_{o}", [P, T]),
            "real": kept(K, f"real_{o}", [P, T]),
            "weight": kept(K, f"weight_{o}", [P, T]),
        }
    K.unsorted = kept(K, "unsorted", [P, 1], I32)
    K.score = kept(K, "score", [P, T, HEADS])
    K.mean_diff = kept(K, "mean_diff", [P, T])
    K.att = [kept(K, f"att{i}", [P, T]) for i in range(2)]


VECTORS = [("L0_gnn_bias", C), ("L1_gnn_b", C), ("L1_gnn_fc", C), ("L1_gnn_bf", 2),
           ("L1_gnn_a_src", C), ("L1_gnn_a_dst", C), ("L2_gnn_b_self", C), ("L2_gnn_b_msg", C),
           ("L2_gnn_gamma", C), ("L2_gnn_beta", C), ("L3_gnn_bq", C), ("L3_gnn_bk", C),
           ("L3_gnn_bv", C), ("L3_gnn_Wd", HEADS), ("L3_gnn_bd", HEADS), ("L3_gnn_bo", C)]
VECTOR_DIMS = {"L1_gnn_b": "a b -> (a b)", "L1_gnn_fc": "a b c -> (a b c)",
               "L1_gnn_a_src": "a b -> (a b)", "L1_gnn_a_dst": "a b -> (a b)",
               "L3_gnn_Wd": "a b -> (a b)"}


def setup_tables(K):
    nc, A = K.nc, K.A
    with Phase(K, "setup") as ph:
        names = ["weight_edge", "W_self", "W_msg", "rel_emb", "Wq", "Wk", "Wv", "Wo"]
        raw = {n: ph.sb(n, [P, C]) for n in names}
        weT = ph.sb("weT", [P, D])
        relT = ph.sb("relT", [P, D])
        prod = ph.sb("prod", [P, C])
        t1 = ph.sb("t1", [P, C])
        t2 = ph.sb("t2", [P, C])
        t3 = ph.sb("t3", [P, 2])
        t4 = ph.sb("t4", [P, 2])
        pT = ph.ps("pT", [P, 512])
        loaded, weights_loaded, consts, dve_step, pe_step, act_step, copied = (ph.sem(n) for n in (
            "vectors_loaded", "weights_loaded", "consts", "dve_step", "pe_step", "act_step", "copied"))
        block = ph.block()

        @block.sync
        def _(sp):
            for n, size in VECTORS:
                v = A[n].rearrange(VECTOR_DIMS[n]) if n in VECTOR_DIMS else A[n]
                sp.dma_start(K.vec[n][:, :], v.partition_broadcast(P)).then_inc(loaded, 16)

        @block.scalar
        def _(act):
            act.dma_start(raw["weight_edge"][0:D, :], A["L0_gnn_weight_edge"]).then_inc(weights_loaded, 16)
            act.dma_start(raw["rel_emb"][0:D, :], A["L2_gnn_rel_emb"]).then_inc(weights_loaded, 16)
            act.dma_start(K.w0[:, :], A["L0_gnn_weight"]).then_inc(weights_loaded, 16)
            for n in ("W_self", "W_msg"):
                act.dma_start(raw[n][:, :], A[f"L2_gnn_{n}"]).then_inc(weights_loaded, 16)
            for n in ("Wq", "Wk", "Wv", "Wo"):
                act.dma_start(raw[n][:, :], A[f"L3_gnn_{n}"]).then_inc(weights_loaded, 16)
            for i in range(2):
                act.dma_start(K.w1[:, i * D:(i + 1) * D], A["L1_gnn_W"][i, :, :]).then_inc(weights_loaded, 16)
            act.wait_ge(dve_step, SETUP_SIGMOID)
            act.activation(t4[:, :], t3[:, :], ACT.Sigmoid).then_inc(act_step, 1)

        @block.gpsimd
        def _(pool):
            pool.memset(K.ones[:, :], 1.0).then_inc(consts, 1)
            pool.memset(K.eps[:, :], EPS).then_inc(consts, 1)
            pool.iota(K.iota64[:, :], pattern=[[1, D]], base=0, channel_multiplier=0,
                      allow_small_or_imprecise_dtypes=True).then_inc(consts, 1)
            pool.wait_ge(consts, 1)
            for target, compare, step in ((K.ident, ALU.is_equal, 1), (K.below, ALU.is_gt, 1),
                                          (K.above, ALU.is_gt, -1)):
                pool.affine_select(out=target[:, :], in_=K.ones[:, :], compare_op=compare, fill=0.0,
                                   base=0, pattern=[[step, P]], channel_multiplier=-step).then_inc(consts, 1)

        turns = [(raw["weight_edge"], D, weT[:, :]), (raw["rel_emb"], D, relT[:, :]),
                 (raw["W_self"], P, K.wself[:, :]), (raw["W_msg"], P, K.wmsg[:, :]),
                 (raw["Wq"], P, K.wq[:, :]), (raw["Wk"], P, K.wkv[:, 0:C]),
                 (raw["Wv"], P, K.wkv[:, C:2 * C]), (raw["Wo"], P, K.wo[:, :])]
        products = [(weT, K.w0, K.w0e), (relT, K.wmsg, K.wrel)]

        @block.tensor
        def _(pe):
            pe.wait_ge(consts, 6)
            pe.wait_ge(weights_loaded, 16 * 11)
            for n, (source, rows, _) in enumerate(turns):
                wait(pe, copied, n)
                pe.transpose(pT[:, 0:rows], source[0:rows, :], K.ident[0:rows, 0:rows]).then_inc(pe_step, 1)
            for n, (lhs, rhs, _) in enumerate(products):
                pe.wait_ge(copied, len(turns) + n)
                pe.matmul(pT[0:D, 0:C], lhs[:, :], rhs[:, :], start=True, stop=True).then_inc(pe_step, 1)

        @block.vector
        def _(dve):
            line = Line(dve, dve_step)
            for n, (_, rows, target) in enumerate(turns):
                dve.wait_ge(pe_step, n + 1)
                dve.tensor_copy(target, pT[:, 0:rows]).then_inc(copied, 1)
            for n, (_, _, target) in enumerate(products):
                dve.wait_ge(pe_step, len(turns) + n + 1)
                dve.tensor_copy(target[:, :], pT[0:D, 0:C]).then_inc(copied, 1)
            dve.wait_ge(loaded, 16 * len(VECTORS))
            line(dve.tensor_scalar(K.relu_b0[:, :], K.vec["L0_gnn_bias"][:, :], 0.0, None, ALU.max))
            line(dve.tensor_tensor(K.bias2[:, :], K.vec["L2_gnn_b_msg"][:, :], K.vec["L2_gnn_b_self"][:, :], ALU.add))
            for a, target in ((K.vec["L1_gnn_a_dst"], K.w1[:, 2 * D:2 * D + 2]),
                              (K.vec["L1_gnn_a_src"], K.w1r[:, :])):
                line(dve.tensor_tensor(prod[:, :], K.w1[:, 0:C], a[:, :], ALU.mult))
                line(dve.tensor_reduce(target, prod[:, :].rearrange("p (h d) -> p h d", h=2), AX.X, ALU.add))
            b1, fc, bf = K.vec["L1_gnn_b"], K.vec["L1_gnn_fc"], K.vec["L1_gnn_bf"]
            line(dve.tensor_tensor(t1[:, :], b1[:, :], fc[:, :], ALU.mult))
            line(dve.tensor_reduce(t3[:, :], t1[:, :].rearrange("p (h d) -> p h d", h=2), AX.X, ALU.add))
            line(dve.tensor_tensor(t3[:, :], t3[:, :], bf[:, :], ALU.add))
            assert line.n == SETUP_SIGMOID
            line(dve.tensor_scalar(t1[:, :], b1[:, :], 0.0, None, ALU.min))
            dve.wait_ge(act_step, 1)
            half = lambda t: t[:, :].rearrange("p (h d) -> p h d", h=2)
            line(dve.tensor_tensor(half(t2), half(t1), inner(t4[:, :], D), ALU.mult))
            line(dve.scalar_tensor_tensor(t1[:, :], b1[:, :], 0.0, t2[:, :], ALU.max, ALU.add))
            line(dve.scalar_tensor_tensor(K.c1[:, :], t1[:, :], ALPHA, t1[:, :], ALU.mult, ALU.max))
            line(dve.tensor_tensor(K.x2_less_x[:, :], K.c1[:, :], K.relu_b0[:, :], ALU.add))


SETUP_SIGMOID = 9



def sort_by_src(K):
    sort_edges(K, "by_src", 0, K.BY_SRC)


def sort_by_dst(K):
    nc = K.nc
    with Phase(K, "check") as ph:
        payload = ph.sb("payload", [P, T + 2, 4], I32)
        falls, fall_count = ph.sb("falls", [P, T]), ph.sb("fall_count", [P, 1])
        total = ph.ps("total", [P, 1])
        loaded, line_sem, counted, summed = (ph.sem(n) for n in ("loaded", "line", "counted", "summed"))
        block = ph.block()

        @block.sync
        def _(sp):
            load_payload(sp, payload, K.BY_DST).then_inc(loaded, 16)

        @block.tensor
        def _(pe):
            pe.wait_ge(counted, 1)
            pe.matmul(total[:, :], K.ones[:, :], fall_count[:, :], start=True, stop=True).then_inc(summed, 1)

        @block.vector
        def _(dve):
            line = Line(dve, line_sem)
            dve.wait_ge(loaded, 16)
            line(dve.tensor_tensor(falls[:, :], payload[:, 1:T + 1, 1], payload[:, 0:T, 1], ALU.is_lt))
            dve.tensor_reduce(fall_count[:, :], falls[:, :], AX.X, ALU.add).then_inc(counted, 1)
            dve.wait_ge(summed, 1)
            line(dve.tensor_scalar(K.unsorted[:, :], total[:, :], 1.0, None, ALU.min))
    unsorted = nc.values_load(K.unsorted[0:1, 0:1], min_val=0, max_val=1)
    with nc.If(unsorted > 0):
        sort_edges(K, "by_dst", 1, K.BY_DST)
        gather_features(K)


def load_payload(sp, payload, table):
    return sp.dma_start(payload[:, :, :].rearrange("p t c -> p (t c)"),
                        bass.AP(table.tensor, 0, [[T * 4, P], [1, (T + 2) * 4]]))


def gather_features(K):
    nc = K.nc
    with Phase(K, "features") as ph:
        payload = ph.sb("payload", [P, T + 2, 4], I32)
        number = ph.sb("number", [P, T], I32)
        index = ph.sb("index", [P, 2, U], I32)
        rows = ph.sb("rows", [P, 2, U, D])
        loaded, numbered, settled = ph.sem("loaded"), ph.sem("numbered"), ph.sem("settled")
        index_in, gathered, stored = ([ph.sem(f"{n}{i}") for i in range(2)] for n in ("index_in", "gathered", "stored"))
        block = ph.block()

        @block.vector
        def _(dve):
            dve.wait_ge(loaded, 16)
            dve.tensor_scalar(number[:, :], payload[:, 1:T + 1, 3], float(E - 1), None, ALU.min).then_inc(numbered, 1)

        @block.scalar
        def _(act):
            pass

        @block.tensor
        def _(pe):
            pass

        @block.gpsimd
        def _(pool):
            def step(b):
                wait(pool, index_in[b.par], 16 * (b.k + 1))
                wait(pool, stored[b.par], 16 * b.k)
                settle(pool, settled)
                gather_rows(pool, K.A["edge_attr_64"], index, b.par, rows, gathered)

            sweep(pool, step)

        @block.sync
        def _(sp):
            load_payload(sp, payload, K.BY_DST).then_inc(loaded, 16)
            sp.wait_ge(numbered, 1)

            def step(b):
                wait(sp, gathered[b.par], 16 * U * b.k)
                stage_index(sp, index, number, b, index_in)
                wait(sp, gathered[b.par], 16 * U * (b.k + 1))
                sp.dma_start(K.EDGE.rearrange("(p t) d -> p t d", p=P)[:, bass.ds(b.blk * U, U), :],
                             rows[:, b.par, :, :]).then_inc(stored[b.par], 16)

            sweep(sp, step)
            for i in range(2):
                sp.wait_ge(stored[i], 16 * uses(NB, i))


def sort_edges(K, name, key, target):
    nc, A = K.nc, K.A
    groups = T // GROUP
    LOW = 32
    CHUNKS = 7
    CG = groups // CHUNKS
    CT = CG * GROUP
    LAG = 2
    assert CHUNKS * CT == T and CG * LOW <= 512
    assert groups <= P and U == 2 * GROUP
    by_src = key == 0
    with Phase(K, name) as ph:
        load = [ph.sb(f"load{n}", [P, T, 4], I32) for n in range(2)]
        if by_src:
            fields = ph.sb("fields", [P, 4, T], I32)
        digit_i = ph.sb("digit_i", [P, T], I32)
        digit = ph.sb("digit", [P, T])
        rank = ph.sb("rank", [P, 2, U])
        iota = ph.sb("iota", [P, LO], BF16)
        onehot = ph.sb("onehot", [P, U, LO], BF16)
        junk = ph.sb("junk", [P, 4, LO], BF16)
        tri = ph.sb("tri", [P, P], BF16)
        ones = ph.sb("ones", [P, P], BF16)
        ident = ph.sb("ident", [P, P], BF16)
        halves_i = ph.sb("halves_i", [P, 2, T], I32)
        iota_low = ph.sb("iota_low", [P, LOW], BF16)
        halves = ph.sb("halves", [P, 2, T], BF16)
        hot_upper = ph.sb("hot_upper", [P, 2, CT, LO // LOW], BF16)
        hot_lower = ph.sb("hot_lower", [P, 2, CT, LOW], BF16)
        hist = ph.sb("hist", [LO // LOW, groups, LOW])
        counts = ph.sb("counts", [P, LO])
        firsts = ph.sb("firsts", [P, LO])
        sizes = ph.sb("sizes", [P, LO])
        begins = ph.sb("begins", [P, LO])
        begins_i = ph.sb("begins_i", [P, 2, LO], I32)
        begins_hi = ph.sb("begins_hi", [P, LO], BF16)
        begins_lo = ph.sb("begins_lo", [P, LO], BF16)
        scan_ones = ph.sb("scan_ones", [P, LO])
        place_i = ph.sb("place_i", [P, 3, U], I32)
        place = ph.sb("place", [P, 2, U], I32)
        stage = ph.sb("stage", [P, 2, U, 4], I32)
        edge_row = ph.sb("edge_row", [2, 4], I32)
        if by_src:
            zeros = ph.sb("zeros", [P, SLICE_PARTS * 20])
            fill = ph.sb("fill", [P, 25, C])
        hist_ps = ph.ps("hist_ps", [LO // LOW, 2, 512])
        before = ph.ps("before", [P, LO])
        running = ph.ps("running", [P, 4, LO])

        loaded, consts, line_sem = ph.sem("loaded"), ph.sem("consts"), ph.sem("dve_line")
        pads_set, by_dst, reloaded, joined = (ph.sem(n) for n in ("pads_set", "by_dst", "reloaded", "joined"))
        settled, pe_settled, filled = ph.sem("pool_settled"), ph.sem("pe_settled"), ph.sem("filled")
        tables_set = ph.sem("tables_set")
        passes = [{n: ph.sem(f"{n}{w}") for n in ("halved", "counted", "taken", "spread", "copied", "before", "begun",
                                                    "hot", "summed", "ranked", "places", "small")}
                  | {"sent": [ph.sem(f"sent{w}_{i}") for i in range(2)]} for w in (LO, HI)]
        block = ph.block()

        @block.sync
        def _(sp):
            if by_src:
                sp.wait_ge(pads_set, 2)
                for n, name in enumerate(("src", "dst", "edge_type_64", "edge_weight")):
                    a = A[name].bitcast(I32) if name == "edge_weight" else A[name]
                    sp.dma_start(fields[0:FULL, n, :], a[0:FULL * T].rearrange("(p t) -> p t", t=T))\
                        .then_inc(loaded, 16)
                    sp.dma_start(fields[FULL:P, n, 0:REST], a[FULL * T:E].rearrange("(p t) -> p t", p=1))\
                        .then_inc(loaded, 16)
                sp.wait_ge(joined, 1)
                body = K.BY_DST[1:EP + 1, :].rearrange("(p t) c -> p (t c)", p=P)
                sp.dma_start(body, load[0][:, :, :].rearrange("p t c -> p (t c)")).then_inc(by_dst, 16)
                for table in (K.BY_DST, K.BY_SRC):
                    sp.dma_start(table[0:1, :], edge_row[0:1, :]).then_inc(by_dst, 16)
                    sp.dma_start(table[EP + 1:EP + 2, :], edge_row[0:1, :]).then_inc(by_dst, 16)
            else:
                sp.dma_start(load[0][:, :, :].rearrange("p t c -> p (t c)"),
                             target[1:EP + 1, :].rearrange("(p t) c -> p (t c)", p=P)).then_inc(loaded, 16)

            def spread(n, width):
                sp.wait_ge(passes[n]["taken"], 1 + CHUNKS)
                by_group = K.COUNTS[:, 0:width]
                sp.dma_start(by_group.rearrange("g (h l) -> h g l", l=LOW), hist[0:width // LOW, :, :])\
                    .then_inc(passes[n]["spread"], 16)
                sp.wait_ge(passes[n]["spread"], 16)
                sp.dma_start(counts[0:groups, 0:width], by_group).then_inc(passes[n]["spread"], 16)

            sp.wait_ge(consts, 9)
            spread(0, LO)
            for i in range(2):
                sp.wait_ge(passes[0]["sent"][i], 16 * U * (NB // 2 + 1 - i))
            sp.dma_start(load[1][:, :, :].rearrange("p t c -> p (t c)"),
                         K.PASS1.rearrange("(p t) c -> p (t c)", p=P)).then_inc(reloaded, 16)
            spread(1, HI)
            if by_src:
                sp.wait_ge(by_dst, 16 * 5)

        @block.scalar
        def _(act):
            if not by_src:
                return
            flat = lambda t: t.rearrange("n d -> (n d)").rearrange("(p f) -> p f", p=SLICE_PARTS)
            cut = lambda t, blk: t[:, bass.ds(blk * (t.shape[1] // SLICES), t.shape[1] // SLICES)]
            x, features = flat(A["x"]), flat(A["edge_attr_64"])
            X, FEATURES, HOP, AGG = flat(K.X[0:N, :]), flat(K.EDGE[0:E, :]), flat(K.HOP[:, :]), flat(K.AGG[:, :])
            spare = K.X[N:N + EP, :].rearrange("(p t) d -> p (t d)", p=P)

            def copies(blk):
                act.dma_start(cut(X, blk), cut(x, blk)).then_inc(tables_set, 16)
                act.dma_start(cut(FEATURES, blk), cut(features, blk)).then_inc(tables_set, 16)

            def fills(blk):
                act.dma_start(cut(HOP, blk), zeros[0:SLICE_PARTS, 0:HOP.shape[1] // SLICES]).then_inc(tables_set, 16)
                act.dma_start(cut(AGG, blk), fill[0:SLICE_PARTS, :, :].rearrange("p r c -> p (r c)"))\
                    .then_inc(tables_set, 16)

            def copy_step(b):
                wait(act, passes[0]["places"], 2 * b.blk)
                copies(b.blk)

            def fill_step(b):
                wait(act, passes[1]["places"], 2 * b.blk)
                fills(b.blk)
                act.dma_start(spare[:, bass.ds(b.blk * U * C, U * C)], zeros[:, 0:U * C]).then_inc(tables_set, 16)

            sweep(act, copy_step)
            copies(SLICES - 1)
            act.wait_ge(filled, 2)
            sweep(act, fill_step)
            fills(SLICES - 1)
            act.dma_start(K.EDGE[E:EP, :].rearrange("(p a) d -> p (a d)", p=16),
                          zeros[0:16, 0:(EP - E) * D // 16]).then_inc(tables_set, 16)
            act.wait_ge(tables_set, 16 * (4 * SLICES + NB + 1))

        @block.gpsimd
        def _(pool):
            if by_src:
                pool.memset(edge_row[:, :], -1).then_inc(pads_set, 1)
                pool.memset(fields[:, :, :], 0).then_inc(consts, 1)
                pool.wait_ge(consts, 1)
                pool.memset(fields[:, 0:2, :], N).then_inc(pads_set, 1)
            else:
                pool.wait_ge(loaded, 16)
                pool.iota(load[0][:, :, 3], pattern=[[1, T]], base=0, channel_multiplier=T).then_inc(consts, 1)
            pool.memset(ones[:, :], 1.0).then_inc(consts, 1)
            pool.memset(scan_ones[:, :], 1.0).then_inc(consts, 1)
            pool.memset(counts[:, :], 0.0).then_inc(consts, 1)
            pool.memset(hist[:, :, :], 0.0).then_inc(consts, 1)
            pool.iota(iota[:, :], pattern=[[1, LO]], base=-LO // 2, channel_multiplier=0,
                      allow_small_or_imprecise_dtypes=True).then_inc(consts, 1)
            pool.tensor_copy(ident[:, :], K.ident[:, :]).then_inc(consts, 1)
            pool.tensor_copy(iota_low[:, :], K.iota64[:, 0:LOW]).then_inc(consts, 1)
            pool.affine_select(out=tri[:, :], in_=K.ones[:, :], compare_op=ALU.is_ge, fill=0.0,
                               base=0, pattern=[[1, P]], channel_multiplier=-1).then_inc(consts, 1)
            if by_src:
                pool.memset(zeros[:, :], 0.0).then_inc(filled, 1)
                pool.tensor_copy(fill[:, :, :], middle(K.vec["L2_gnn_b_self"][:, :], 25)).then_inc(filled, 1)
            for n, table in ((0, K.PASS1[:, :]), (1, target[:, :])):
                sems = passes[n]

                def send(b):
                    wait(pool, sems["places"], 2 * (b.blk + 1))
                    settle(pool, settled)
                    for u in range(U):
                        pool.indirect_dma_start(
                            table, bass.IndirectOffsetOnAxis(ap=place[:, b.par, u:u + 1], axis=0),
                            stage[:, b.par, u, :], None).then_inc(sems["sent"][b.par], 16)

                sweep(pool, send)
            for i in range(2):
                pool.wait_ge(passes[1]["sent"][i], 16 * U * (NB // 2 + 1 - i))

        @block.vector
        def _(dve):
            line = Line(dve, line_sem)
            dve.wait_ge(loaded, 16 * (8 if by_src else 1))
            if by_src:
                line(dve.tensor_copy(load[0][:, :, :], fields[:, :, :].rearrange("p c t -> p t c")))
                dve.sem_inc(joined, 1)
            dve.wait_ge(consts, 9)
            for n, (width, op, amount) in enumerate(((LO, ALU.bitwise_and, LO - 1),
                                                     (HI, ALU.logical_shift_right, 9))):
                sems, source = passes[n], load[n]
                if n:
                    dve.wait_ge(reloaded, 16)
                line(dve.tensor_scalar(digit_i[:, :], source[:, :, key], amount, None, op))
                line(dve.tensor_scalar(digit[:, :], digit_i[:, :], float(-LO // 2), None, ALU.add))

                def hot(b, u, sem):
                    dve.tensor_scalar(onehot[:, u, 0:width], iota[:, 0:width],
                                      digit[:, bass.ds(b.blk * U + u, 1)], None, ALU.is_equal)\
                        .then_inc(sem, 1)

                upper = width // LOW
                for m, (halve, by) in enumerate(((ALU.logical_shift_right, 5), (ALU.bitwise_and, LOW - 1))):
                    line(dve.tensor_scalar(halves_i[:, m, :], digit_i[:, :], by, None, halve))
                    line(dve.tensor_copy(halves[:, m, :], halves_i[:, m, :]))

                dve.sem_inc(sems["taken"], 1)

                def take(c):
                    dve.wait_ge(sems["counted"], c + 1)
                    dve.tensor_copy(hist[0:upper, c * CG:(c + 1) * CG, :],
                                    hist_ps[0:upper, c % 2, 0:CG * LOW].rearrange("h (g l) -> h g l", l=LOW))\
                        .then_inc(sems["taken"], 1)

                for c in range(CHUNKS):
                    for m, (hot_half, values) in enumerate(((hot_upper, upper), (hot_lower, LOW))):
                        dve.tensor_tensor(hot_half[:, c % 2, :, 0:values], middle(iota_low[:, 0:values], CT),
                                          inner(halves[:, m, c * CT:(c + 1) * CT], values), ALU.is_equal)\
                            .then_inc(sems["halved"], 1)
                    if c:
                        take(c - 1)
                take(CHUNKS - 1)
                dve.wait_ge(sems["before"], 1)
                line(dve.tensor_copy(begins[:, 0:width], before[:, 0:width]))
                dve.sem_inc(sems["copied"], 1)
                c = sizes[:, 0:width]
                dve.wait_ge(sems["before"], 2)
                line(dve.tensor_copy(c, before[:, 0:width]))
                line(dve.tensor_tensor_scan(firsts[:, 0:width], scan_ones[:, 0:width], c,
                                            0.0, ALU.mult, ALU.add))
                line(dve.tensor_tensor(firsts[:, 0:width], firsts[:, 0:width], c, ALU.subtract))
                line(dve.tensor_tensor(begins[:, 0:width], begins[:, 0:width], firsts[:, 0:width], ALU.add))
                line(dve.tensor_copy(begins_i[:, 0, 0:width], begins[:, 0:width]))
                line(dve.tensor_scalar(begins_i[:, 1, 0:width], begins_i[:, 0, 0:width], 255, None,
                                       ALU.bitwise_and))
                line(dve.tensor_copy(begins_lo[:, 0:width], begins_i[:, 1, 0:width]))
                line(dve.tensor_scalar(begins_i[:, 1, 0:width], begins_i[:, 0, 0:width], 0xFFFF00, None,
                                       ALU.bitwise_and))
                dve.tensor_copy(begins_hi[:, 0:width], begins_i[:, 1, 0:width]).then_inc(sems["begun"], 1)

                def rank_block(b):
                    static = isinstance(b.blk, int)
                    wait(dve, sems["ranked"], b.blk * U - LAG)
                    for u in range(U):
                        wait(dve, sems["summed"], (b.blk - 1) * U + GROUP * (u // GROUP + 1))
                        hot(b, u, sems["hot"])
                        if u >= LAG:
                            tile_rank(b, u - LAG)
                        elif not static or b.blk:
                            tile_rank(b.ago(1), U + u - LAG)
                            if u == LAG - 1:
                                send_places(b.ago(1))

                def tile_rank(b, u):
                    dve.wait_ge(sems["summed"], b.blk * U + u + 1)
                    dve.tensor_tensor_reduce(
                        out=junk[:, u % 4, 0:width], in0=onehot[:, u, 0:width],
                        in1=running[:, u % 4, 0:width], scale=1.0, scalar=0.0,
                        op0=ALU.mult, op1=ALU.add, accum_out=rank[:, b.par, u:u + 1])\
                        .then_inc(sems["ranked"], 1)

                def send_places(b):
                    dve.wait_ge(sems["ranked"], (b.blk + 1) * U)
                    wait(dve, sems["sent"][b.par], 16 * U * b.k)
                    settle(dve, sems["small"])
                    dve.tensor_copy(stage[:, b.par, :, :], source[:, bass.ds(b.blk * U, U), :])\
                        .then_inc(sems["places"], 1)
                    got = rank[:, b.par, :]
                    if n == 1:
                        dve.tensor_copy(place[:, b.par, :], got).then_inc(sems["places"], 1)
                        return
                    small = 4 * b.blk
                    dve.tensor_scalar(place_i[:, 0, :], got, -1.0, None, ALU.add).then_inc(sems["small"], 1)
                    dve.wait_ge(sems["small"], small + 2)
                    dve.tensor_scalar(place_i[:, 1, :], place_i[:, 0, :], P - 1, None, ALU.bitwise_and)\
                        .then_inc(sems["small"], 1)
                    dve.tensor_scalar(place_i[:, 2, :], place_i[:, 0, :], 7, None, ALU.logical_shift_right)\
                        .then_inc(sems["small"], 1)
                    dve.wait_ge(sems["small"], small + 4)
                    dve.scalar_tensor_tensor(place[:, b.par, :], place_i[:, 1, :], float(T),
                                             place_i[:, 2, :], ALU.mult, ALU.add)\
                        .then_inc(sems["places"], 1)

                sweep(dve, rank_block)
                for u in range(U - LAG, U):
                    tile_rank(Step(NB // 2, 0), u)
                send_places(Step(NB // 2, 0))

        @block.tensor
        def _(pe):
            pe.wait_ge(consts, 9)
            for n, width in enumerate((LO, HI)):
                sems = passes[n]

                def count(k, par):
                    c = 2 * k + par
                    pe.wait_ge(sems["halved"], 2 * (c + 1))
                    pe.wait_ge(sems["taken"], c)
                    for t in range(CT):
                        g = t // GROUP
                        last = pe.matmul(hist_ps[0:width // LOW, par, g * LOW:(g + 1) * LOW],
                                         hot_upper[:, par, t, 0:width // LOW], hot_lower[:, par, t, :],
                                         start=t % GROUP == 0, stop=t % GROUP == GROUP - 1)
                    last.then_inc(sems["counted"], 1)

                with pe.Fori(0, CHUNKS // 2) as k:
                    count(k, 0)
                    count(k, 1)
                count(CHUNKS // 2, 0)
                pe.wait_ge(sems["spread"], 32)
                pe.matmul(before[:, 0:width], K.below[:, :], counts[:, 0:width], start=True, stop=True)\
                    .then_inc(sems["before"], 1)
                pe.wait_ge(sems["copied"], 1)
                pe.matmul(before[:, 0:width], K.ones[:, :], counts[:, 0:width], start=True, stop=True)\
                    .then_inc(sems["before"], 1)
                pe.wait_ge(sems["begun"], 1)

                def sums(b):
                    for u in range(U):
                        wait(pe, sems["ranked"], b.blk * U + u - 3)
                        wait(pe, sems["hot"], b.blk * U + u + 1)
                        settle(pe, pe_settled)
                        bank = running[:, u % 4, 0:width]
                        mine = ident[:, bass.ds(b.blk * 2 + u // GROUP, 1)].to_broadcast([P, P])
                        pe.matmul(bank, mine, begins_hi[:, 0:width], start=True, stop=False)
                        pe.matmul(bank, mine, begins_lo[:, 0:width], start=False, stop=False)
                        for earlier in range(u // GROUP * GROUP, u):
                            pe.matmul(bank, ones[:, :], onehot[:, earlier, 0:width], start=False, stop=False)
                        pe.matmul(bank, tri[:, :], onehot[:, u, 0:width], start=False, stop=True)\
                            .then_inc(sems["summed"], 1)

                sweep(pe, sums)


def order_tables(K):
    nc = K.nc
    with Phase(K, "tables") as ph:
        loaded, consts, pe_step, act_step = ph.sem("loaded"), ph.sem("consts"), ph.sem("pe_step"), ph.sem("act_step")
        dve_line, rows_ready = ph.sem("dve_line"), ph.sem("rows_ready")
        orders = [("s", K.BY_SRC, 0, 1), ("d", K.BY_DST, 1, 0)]
        payload = [ph.sb(f"payload{n}", [P, T + 2, 4], I32) for n in range(2)]
        key = ph.sb("key", [P, T + 2])
        spare = ph.sb("spare", [P, T])
        t_ones = ph.sb("t_ones", [P, T])
        end, first, ok, t1, t2 = (ph.sb(n, [P, T]) for n in ("end", "first", "ok", "t1", "t2"))
        cross, begun, s1, s2, deg = (ph.sb(n, [P, 1]) for n in ("cross", "begun", "s1", "s2", "deg"))
        diag = ph.sb("diag", [P, 2, P])
        tail = ph.sb("tail", [P, 1])
        rows = ph.ps("rows", [P, 2, P])
        carry = ph.ps("carry", [P, 1])
        block = ph.block()

        @block.sync
        def _(sp):
            for n, (_, table, _, _) in enumerate(orders):
                load_payload(sp, payload[n], table).then_inc(loaded, 16)

        @block.gpsimd
        def _(pool):
            pool.iota(spare[:, :], pattern=[[1, T]], base=N, channel_multiplier=T,
                      allow_small_or_imprecise_dtypes=True).then_inc(consts, 1)
            pool.memset(t_ones[:, :], 1.0).then_inc(consts, 1)

        @block.tensor
        def _(pe):
            for n, (o, _, _, _) in enumerate(orders):
                for m in range(2):
                    pe.wait_ge(rows_ready, 3 * n + m + 1)
                    pe.matmul(rows[:, m, :], K.ones[:, :], diag[:, m, :], start=True, stop=True)\
                        .then_inc(pe_step, 1)
                pe.wait_ge(rows_ready, 3 * n + 3)
                pe.matmul(carry[:, :], K.order[o]["to_later"][:, :], tail[:, :], start=True, stop=True)\
                    .then_inc(pe_step, 1)

        @block.scalar
        def _(act):
            for n, (o, _, _, _) in enumerate(orders):
                d = K.order[o]
                act.wait_ge(rows_ready, 3 * n + 3)
                act.activation(d["flags"][:, :, RSQRT], t1[:, :], ACT.Sqrt).then_inc(act_step, 1)
                act.wait_ge(pe_step, 3 * n + 3)
                act.activation(deg[:, :], carry[:, :], ACT.Identity, bias=begun[:, :]).then_inc(act_step, 1)
                act.wait_ge(act_step, 3 * n + 2)
                act.activation(d["scale_first"][:, 0:1], deg[:, :], ACT.Sqrt).then_inc(act_step, 1)

        @block.vector
        def _(dve):
            line = Line(dve, dve_line)
            dve.wait_ge(loaded, 32)
            dve.wait_ge(consts, 2)
            for n, (o, _, own, other) in enumerate(orders):
                d, pay = K.order[o], payload[n]
                fl = d["flags"]
                cur, prev, nxt = key[:, 1:T + 1], key[:, 0:T], key[:, 2:T + 2]
                key0, keyT = key[:, 1:2], key[:, T:T + 1]
                line(dve.tensor_copy(key[:, :], pay[:, :, own]))
                line(dve.tensor_scalar(d["near"][:, :], cur, float(N - 1), None, ALU.min))
                line(dve.tensor_scalar(d["far"][:, :], pay[:, 1:T + 1, other], float(N - 1), None, ALU.min))
                line(dve.tensor_tensor(fl[:, :, CONT], cur, prev, ALU.is_equal))
                line(dve.tensor_copy(cross[:, :], fl[:, 0:1, CONT]))
                line(dve.memset(fl[:, 0:1, CONT], 0.0))
                line(dve.tensor_tensor(end[:, :], cur, nxt, ALU.not_equal))
                line(dve.tensor_scalar(first[:, :], cur, key0, None, ALU.is_equal))
                line(dve.tensor_copy(fl[:, :, FIRST], first[:, :]))
                line(dve.tensor_scalar(d["real"][:, :], cur, float(N), None, ALU.is_lt))
                line(dve.tensor_scalar(fl[:, :, TYPE], pay[:, 1:T + 1, 2], 0.0, float(D - 1), ALU.max, ALU.min))
                line(dve.tensor_copy(d["weight"][:, :], pay[:, 1:T + 1, 3].bitcast(F32)))
                line(dve.tensor_scalar(d["last_seg"][:, :], cur, keyT, None, ALU.is_equal))
                line(dve.tensor_scalar(d["next_cont"][:, :], end[:, :], -1.0, 1.0, ALU.mult, ALU.add))
                line(dve.memset(d["next_cont"][:, T - 1:T], 0.0))
                line(dve.tensor_tensor(t1[:, :], end[:, :], first[:, :], ALU.mult))
                line(dve.tensor_reduce(s1[:, :], t1[:, :], AX.X, ALU.add))
                line(dve.tensor_scalar(t1[:, :], first[:, :], cross[:, :], None, ALU.mult))
                line(dve.tensor_scalar(t1[:, :], t1[:, :], -1.0, 1.0, ALU.mult, ALU.add))
                line(dve.tensor_tensor(t1[:, :], t1[:, :], end[:, :], ALU.mult))
                line(dve.tensor_tensor(ok[:, :], t1[:, :], d["real"][:, :], ALU.mult))
                line(dve.scalar_tensor_tensor(t1[:, :], cur, float(-SKIP), ok[:, :], ALU.add, ALU.mult))
                line(dve.tensor_scalar(d["put"][:, :], t1[:, :], float(SKIP), None, ALU.add))
                line(dve.tensor_tensor(t1[:, :], cur, spare[:, :], ALU.subtract))
                line(dve.tensor_tensor(t1[:, :], t1[:, :], ok[:, :], ALU.mult))
                line(dve.tensor_tensor(d["add"][:, :], t1[:, :], spare[:, :], ALU.add))
                line(dve.tensor_tensor(s1[:, :], s1[:, :], cross[:, :], ALU.mult))
                line(dve.tensor_tensor(s1[:, :], s1[:, :], d["real"][:, 0:1], ALU.mult))
                line(dve.scalar_tensor_tensor(s2[:, :], key0, float(-SKIP), s1[:, :], ALU.add, ALU.mult))
                line(dve.tensor_scalar(d["put_first"][:, :], s2[:, :], float(SKIP), None, ALU.add))
                line(dve.tensor_tensor(s2[:, :], key0, spare[:, 0:1], ALU.subtract))
                line(dve.tensor_tensor(s2[:, :], s2[:, :], s1[:, :], ALU.mult))
                line(dve.tensor_tensor(d["add_first"][:, :], s2[:, :], spare[:, 0:1], ALU.add))
                for m, k in enumerate((key0, keyT)):
                    dve.tensor_scalar(diag[:, m, :], K.ident[:, :], k, None, ALU.mult).then_inc(rows_ready, 1)
                dve.wait_ge(pe_step, 3 * n + 2)
                line(dve.tensor_scalar(d["to_later"][:, :], rows[:, 0, :], keyT, None, ALU.is_equal))
                line(dve.tensor_tensor(d["to_later"][:, :], d["to_later"][:, :], K.below[:, :], ALU.mult))
                line(dve.tensor_scalar(d["from_earlier"][:, :], rows[:, 1, :], key0, None, ALU.is_equal))
                line(dve.tensor_tensor(d["from_earlier"][:, :], d["from_earlier"][:, :], K.above[:, :], ALU.mult))
                line(dve.tensor_copy(t2[:, :], fl[:, :, CONT]))
                line(dve.tensor_reduce(begun[:, :], first[:, :], AX.X, ALU.add))
                line(dve.tensor_tensor_scan(t1[:, :], t2[:, :], t_ones[:, :], 0.0, ALU.mult, ALU.add))
                dve.tensor_copy(tail[:, :], t1[:, T - 1:T]).then_inc(rows_ready, 1)
                line(dve.reciprocal(fl[:, :, RDEG], t1[:, :]))
                dve.wait_ge(act_step, 3 * n + 3)
                line(dve.reciprocal(fl[:, :, RSQRT], fl[:, :, RSQRT]))
                line(dve.reciprocal(d["scale_first"][:, 0:1], d["scale_first"][:, 0:1]))
                line(dve.reciprocal(d["scale_first"][:, 1:2], deg[:, :]))


def norm_sums(dve, chain, x, n, bn, small):
    for u in range(n):
        last = chain.done(dve.bn_stats(bn[:, u, :], x[:, u, :]))
    dve.wait_ge(chain.sem, last)
    chain.done(dve.tensor_tensor(small["diff"], bn[:, 0:n, 1], bn[:, 0:n, 4], ALU.subtract))
    chain.done(dve.tensor_tensor(small["sum"], bn[:, 0:n, 1], bn[:, 0:n, 4], ALU.add))
    last = chain.done(dve.tensor_tensor(small["m2"], bn[:, 0:n, 2], bn[:, 0:n, 5], ALU.add))
    dve.wait_ge(chain.sem, last)
    last = chain.done(dve.tensor_tensor(small["sq"], small["diff"], small["diff"], ALU.mult))
    dve.wait_ge(chain.sem, last)
    chain.done(dve.scalar_tensor_tensor(small["q"], small["sq"], C / 4.0, small["m2"], ALU.mult, ALU.add))


def norm_scales(dve, chain, small):
    last = chain.done(dve.reciprocal(small["rstd"], small["std"]))
    dve.wait_ge(chain.sem, last)
    chain.done(dve.scalar_tensor_tensor(small["nmr"], small["sum"], -0.5, small["rstd"], ALU.mult, ALU.mult))


def small_tiles(ph, name, n):
    return {k: ph.sb(f"{name}_{k}", [P, n])[:, :] for k in ("diff", "sum", "m2", "sq", "q", "std", "rstd", "nmr")}


def stage_index(sp, buffer, source, b, sem):
    sp.dma_start(buffer[:, b.par, :], source[:, bass.ds(b.blk * U, U)]).then_inc(sem[b.par], 16)


def gather_rows(pool, table, index, par, rows, sem):
    for u in range(U):
        pool.indirect_dma_start(rows[:, par, u, :], None, table,
                                bass.IndirectOffsetOnAxis(ap=index[:, par, u:u + 1], axis=0)).then_inc(sem[par], 16)


def scatter_rows(pool, table, index, par, rows, sem, accumulate=False):
    for u in range(U):
        at = bass.IndirectOffsetOnAxis(ap=index[:, par, u:u + 1], axis=0)
        put_rows(pool, table, at, rows[:, par, u, :], accumulate).then_inc(sem[par], 16)


def put_rows(pool, table, at, rows, accumulate):
    if accumulate:
        return pool.indirect_dma_start(table, at, rows, None, bounds_check=table.shape[0] - 1,
                                       oob_is_err=True, compute_op=ALU.add)
    return pool.indirect_dma_start(table, at, rows, None, bounds_check=table.shape[0] - 1, oob_is_err=False)


def uses(blocks, par):
    return (blocks + 1 - par) // 2


def layer0(K):
    edge_sum_layer(K, "layer0", relational=False)


def layer2(K):
    edge_sum_layer(K, "layer2", relational=True)


def edge_sum_layer(K, name, relational):
    nc, A, d = K.nc, K.A, K.order["d"]
    W = C + D
    source = K.X[0:N, :] if relational else A["x"]
    w, we = (K.wmsg, K.wrel) if relational else (K.w0, K.w0e)
    bias = K.bias2 if relational else K.vec["L0_gnn_bias"]
    target, put, put_first = (K.AGG[:, :], d["put"], d["put_first"]) if relational else \
        (K.X[:, :], d["add"], d["add_first"])
    scale = RDEG if relational else RSQRT
    with Phase(K, name) as ph:
        index = ph.sb("index", [P, 2, U], I32)
        put_index = ph.sb("put_index", [P, 2, U], I32)
        rows = ph.sb("rows", [P, 2, U, C])
        messages = ph.sb("messages", [P, 2, U, W])
        states = ph.sb("states", [P, 2, U, W])
        head = ph.sb("head", [P, W])
        flags = ph.sb("flags", [P, 2, U, FLAGS])
        turned_sb = ph.sb("turned", [P, 4, 512])
        result = ph.sb("result", [P, 2, U, C])
        bn = ph.sb("bn", [P, U, 6])
        small = small_tiles(ph, "norm", U)
        turned_ps = ph.ps("turned_ps", [P, 4, 512])
        mixed_ps = ph.ps("mixed", [P, 2, 512])
        over_ps = ph.ps("over", [P, W])

        def pair(n):
            return [ph.sem(f"{n}{i}") for i in range(2)]

        index_in, put_in, gathered, features_in, sent = (
            pair(n) for n in ("index_in", "put_in", "gathered", "features_in", "sent"))
        stat, state, post = ph.sem("stat"), ph.sem("state"), ph.sem("post")
        deviation, normed, turned, copied, mixed, settled, cleared, ends = (ph.sem(n) for n in (
            "deviation", "normed", "turned", "copied", "mixed", "settled", "cleared", "ends"))
        stats = Chain(stat, U + 5 + 2 + (2 if relational else 0))
        sums = Chain(state, 2 * U)
        posts = Chain(post, U + (0 if relational else 1))
        first_sem, first_sem_pe, flags_in, settled_dve = (ph.sem(n) for n in (
            "first_sent", "over_ready", "flags_in", "settled_dve"))
        block = ph.block()

        @block.sync
        def _(sp):
            for par in range(2):
                stage_index(sp, index, d["far"], Step(0, par), index_in)

            def put_stage(b):
                wait(sp, sent[b.par], 16 * U * b.k)
                stage_index(sp, put_index, put, b, put_in)

            def step(b):
                ahead = b.ago(-2)
                if not relational:
                    wait(sp, state, sums.end(b.ago(2)))
                    sp.dma_start(messages[:, b.par, :, C:W],
                                 K.EDGE.rearrange("(p t) d -> p t d", p=P)[:, bass.ds(b.blk * U, U), :])\
                        .then_inc(features_in[b.par], 16)
                if b.within(NB) and b.ago(1).within(NB):
                    put_stage(b.ago(1))
                if ahead.within(NB):
                    wait(sp, gathered[b.par], 16 * U * (b.k + 1))
                    stage_index(sp, index, d["far"], ahead, index_in)

            sweep(sp, step)
            put_stage(Step(NB // 2, 0))

        @block.gpsimd
        def _(pool):
            def gather(b):
                wait(pool, index_in[b.par], 16 * (b.k + 1))
                wait(pool, normed, b.blk - 1)
                settle(pool, settled)
                gather_rows(pool, source, index, b.par, rows, gathered)

            def scatter(b):
                wait(pool, put_in[b.par], 16 * (b.k + 1))
                wait(pool, post, posts.end(b))
                settle(pool, settled)
                scatter_rows(pool, target, put_index, b.par, result, sent, accumulate=not relational)

            def step(b):
                if b.ago(-2).within(NB):
                    gather(b.ago(-2))
                if b.ago(1).within(NB):
                    scatter(b.ago(1))

            gather(Step(0, 0))
            gather(Step(0, 1))
            sweep(pool, step, lag=1)
            for i in range(2):
                pool.wait_ge(sent[i], 16 * U * uses(NB, i))
            pool.wait_ge(ends, 3 if relational else 5)
            at = bass.IndirectOffsetOnAxis(ap=put_first[:, 0:1], axis=0)
            put_rows(pool, target, at, result[:, 1, 0, :], not relational).then_inc(first_sem, 16)
            pool.wait_ge(first_sem, 16)

        @block.scalar
        def _(act):
            def step(b):
                wait(act, stat, stats.end(b) - 2)
                act.activation(small["std"], small["q"], ACT.Sqrt, bias=K.eps[:, :], scale=1.0 / C)\
                    .then_inc(deviation, 1)
                wait(act, stat, stats.end(b))
                wait(act, state, sums.end(b.ago(2)))
                for u in range(U):
                    last = act.activation(messages[:, b.par, u, 0:C], rows[:, b.par, u, :], ACT.Relu,
                                          bias=small["nmr"][:, u:u + 1], scale=small["rstd"][:, u:u + 1])
                last.then_inc(normed, 1)
                wait(act, turned, b.blk + 1)
                wait(act, mixed, b.blk)
                for m in range(4):
                    part = P if m < 2 else D
                    last = act.activation(turned_sb[0:part, m, :], turned_ps[0:part, m, :], ACT.Copy)
                last.then_inc(copied, 1)

            sweep(act, step)
            act.wait_ge(turned, NB + 1)
            act.wait_ge(mixed, NB)
            act.activation(turned_sb[:, 0, 0:C], turned_ps[:, 0, 0:C], ACT.Copy).then_inc(copied, 1)
            act.activation(turned_sb[0:D, 2, 0:P], turned_ps[0:D, 2, 0:P], ACT.Copy).then_inc(copied, 1)

        @block.tensor
        def _(pe):
            def turn(par, u):
                return pe.transpose(turned_ps[:, u // 4, u % 4 * C:(u % 4 + 1) * C],
                                    states[:, par, u, 0:C], K.ident[:, :])

            def turn_features(par, u):
                return pe.transpose(turned_ps[0:D, 2 + u // 4, u % 4 * C:(u % 4 + 1) * C],
                                    states[:, par, u, C:W], K.ident[:, :])

            def mix(u):
                at = slice(u % 4 * C, (u % 4 + 1) * C)
                out = mixed_ps[:, u // 4, at]
                pe.matmul(out, turned_sb[:, u // 4, at], w[:, :], start=True, stop=False)
                return pe.matmul(out, turned_sb[0:D, 2 + u // 4, at], we[0:D, :], start=False, stop=True)

            def step(b):
                wait(pe, state, sums.end(b))
                wait(pe, copied, b.blk)
                for u in range(U):
                    turn(b.par, u)
                    last = turn_features(b.par, u)
                last.then_inc(turned, 1)
                wait(pe, copied, b.blk + 1)
                wait(pe, post, posts.end(b.ago(1)))
                for u in range(U):
                    last = mix(u)
                last.then_inc(mixed, 1)

            sweep(pe, step)
            pe.matmul(over_ps[:, :], d["to_later"][:, :], states[:, (NB - 1) % 2, U - 1, :],
                      start=True, stop=True).then_inc(first_sem_pe, 1)
            pe.wait_ge(ends, 1)
            pe.wait_ge(copied, NB)
            turn(1, 0)
            turn_features(1, 0).then_inc(turned, 1)
            pe.wait_ge(copied, NB + 2)
            pe.wait_ge(post, posts.per * NB)
            mix(0).then_inc(mixed, 1)

        @block.vector
        def _(dve):
            dve.memset(states[:, 1, U - 1, :], 0.0).then_inc(cleared, 1)
            dve.memset(head[:, :], 0.0).then_inc(cleared, 1)

            def statistics(b):
                stats.at(b)
                wait(dve, gathered[b.par], 16 * U * (b.k + 1))
                if relational:
                    wait(dve, state, sums.end(b.ago(2)))
                    x = rows[:, b.par, :, :]
                    last = stats.done(dve.tensor_tensor(x, x, middle(K.x2_less_x[:, :], U), ALU.add))
                    dve.wait_ge(stat, last)
                    stats.done(dve.tensor_tensor(messages[:, b.par, :, C:W], middle(K.iota64[:, :], U),
                                                 inner(flags[:, b.par, :, TYPE], D), ALU.is_equal))
                norm_sums(dve, stats, rows[:, b.par, :, :], U, bn, small)
                wait(dve, deviation, b.blk + 1)
                norm_scales(dve, stats, small)

            def load_flags(b):
                wait(dve, state, sums.end(b.ago(2)))
                wait(dve, post, posts.end(b.ago(2)))
                settle(dve, settled_dve)
                dve.tensor_copy(flags[:, b.par, :, :], d["flags"][:, bass.ds(b.blk * U, U), :])\
                    .then_inc(flags_in, 1)
                wait(dve, flags_in, b.blk + 1)

            def running_sums(b):
                sums.at(b)
                wait(dve, normed, b.blk + 1)
                if not relational:
                    wait(dve, features_in[b.par], 16 * (b.k + 1))
                else:
                    wait(dve, stat, stats.end(b))
                wait(dve, turned, b.blk - 1)
                dve.wait_ge(cleared, 2)
                for u in range(U):
                    before = states[:, b.par, u - 1, :] if u else states[:, 1 - b.par, U - 1, :]
                    message = messages[:, b.par, u, :]
                    wait(dve, state, sums.base + 2 * u - 1)
                    sums.done(dve.scalar_tensor_tensor(states[:, b.par, u, :], before,
                                                       flags[:, b.par, u, CONT:CONT + 1], message,
                                                       ALU.mult, ALU.add))
                    wait(dve, state, sums.base + 2 * u)
                    sums.done(dve.scalar_tensor_tensor(head[:, :], message, flags[:, b.par, u, FIRST:FIRST + 1],
                                                       head[:, :], ALU.mult, ALU.add))

            def finish(b):
                posts.at(b)
                wait(dve, mixed, b.blk + 1)
                wait(dve, sent[b.par], 16 * U * b.k)
                for u in range(U):
                    last = posts.done(dve.scalar_tensor_tensor(
                        result[:, b.par, u, :], mixed_ps[:, u // 4, u % 4 * C:(u % 4 + 1) * C],
                        flags[:, b.par, u, scale:scale + 1], bias[:, :], ALU.mult, ALU.add))
                if not relational:
                    r = result[:, b.par, :, :]
                    dve.wait_ge(post, last)
                    posts.done(dve.scalar_tensor_tensor(r, r, 0.0, middle(K.relu_b0[:, :], U),
                                                        ALU.max, ALU.subtract))

            def step(b):
                if b.within(NB):
                    load_flags(b)
                    statistics(b)
                    running_sums(b)
                if b.ago(1).within(NB):
                    finish(b.ago(1))

            sweep(dve, step, lag=1)
            dve.wait_ge(first_sem_pe, 1)
            dve.wait_ge(state, sums.per * NB)
            dve.wait_ge(sent[1], 16 * U * uses(NB, 1))
            line = Line(dve, ends)
            line(dve.tensor_tensor(states[:, 1, 0, :], over_ps[:, :], head[:, :], ALU.add))
            dve.wait_ge(mixed, NB + 1)
            s = d["scale_first"][:, 1:2] if relational else d["scale_first"][:, 0:1]
            r = result[:, 1, 0, :]
            line(dve.tensor_scalar(r, mixed_ps[:, 0, 0:C], s, None, ALU.mult))
            line(dve.tensor_tensor(r, r, bias[:, :], ALU.add))
            if not relational:
                line(dve.tensor_scalar(r, r, 0.0, None, ALU.max))
                line(dve.tensor_tensor(r, r, K.relu_b0[:, :], ALU.subtract))


def attention_inputs(K):
    nc, d = K.nc, K.order["s"]
    with Phase(K, "att_in") as ph:
        sides = ("far", "near")
        index = {s: ph.sb(f"index_{s}", [P, 2, U], I32) for s in sides}
        rows = {s: ph.sb(f"rows_{s}", [P, 2, U, C]) for s in sides}
        hidden = {s: ph.sb(f"hidden_{s}", [P, 2, U, C]) for s in sides}
        bn = {s: ph.sb(f"bn_{s}", [P, U, 6]) for s in sides}
        small = {s: small_tiles(ph, f"norm_{s}", U) for s in sides}
        turned_sb = {s: ph.sb(f"turned_{s}", [P, 2, 512]) for s in sides}
        heads = ph.sb("heads", [P, 2, 2, U, D])
        score = ph.sb("score", [P, U, 2])
        turned_ps = ph.ps("turned_ps", [P, 2, 512])
        far_ps = ph.ps("far_ps", [P, 4, 512])
        near_ps = ph.ps("near_ps", [P, U, 2])
        w1 = 2 * D + 2

        def pair(n):
            return [ph.sem(f"{n}{i}") for i in range(2)]

        index_in, gathered, stored = pair("index_in"), pair("gathered"), pair("stored")
        stat, out = ph.sem("stat"), ph.sem("out")
        deviation, normed, turned, copied, mixed, settled, settled_dve = (ph.sem(n) for n in (
            "deviation", "normed", "turned", "copied", "mixed", "settled", "settled_dve"))
        SIDE = 1 + U + 7
        stats = Chain(stat, 2 * SIDE)
        outs = Chain(out, 4 + 1 + 2)
        block = ph.block()

        @block.sync
        def _(sp):
            def index_blocks(b):
                for s in sides:
                    stage_index(sp, index[s], d[s], b, index_in)

            index_blocks(Step(0, 0))
            index_blocks(Step(0, 1))

            def step(b):
                if b.ago(-2).within(NB):
                    wait(sp, gathered[b.par], 2 * 16 * U * (b.k + 1))
                    index_blocks(b.ago(-2))
                if b.ago(1).within(NB):
                    store(b.ago(1))

            def store(b):
                wait(sp, out, outs.end(b))
                for i, table in enumerate((K.H0, K.H1)):
                    sp.dma_start(table.rearrange("(p t) d -> p t d", p=P)[:, bass.ds(b.blk * U, U), :],
                                 heads[:, b.par, i, :, :]).then_inc(stored[b.par], 16)

            sweep(sp, step, lag=1)
            for i in range(2):
                sp.wait_ge(stored[i], 32 * uses(NB, i))

        @block.gpsimd
        def _(pool):
            def step(b):
                wait(pool, index_in[b.par], 32 * (b.k + 1))
                wait(pool, normed, 2 * (b.blk - 1))
                settle(pool, settled)
                for s in sides:
                    gather_rows(pool, K.X[0:N, :], index[s], b.par, rows[s], gathered)

            sweep(pool, step)

        @block.scalar
        def _(act):
            def step(b):
                for n, s in enumerate(sides):
                    wait(act, stat, stats.base_of(b) + U + 6 + (U + 6) * n)
                    act.activation(small[s]["std"], small[s]["q"], ACT.Sqrt, bias=K.eps[:, :], scale=1.0 / C)\
                        .then_inc(deviation, 1)
                for n, s in enumerate(sides):
                    wait(act, stat, stats.base_of(b) + 2 * (U + 6) + 2 * (n + 1))
                    wait(act, turned, 2 * (b.blk - 2) + n + 1)
                    for u in range(U):
                        last = act.activation(hidden[s][:, b.par, u, :], rows[s][:, b.par, u, :], ACT.Relu,
                                              bias=small[s]["nmr"][:, u:u + 1],
                                              scale=small[s]["rstd"][:, u:u + 1])
                    last.then_inc(normed, 1)
                for n, s in enumerate(sides):
                    wait(act, turned, 2 * b.blk + n + 1)
                    wait(act, mixed, 2 * (b.blk - 1) + n + 1)
                    for m in range(2):
                        last = act.activation(turned_sb[s][:, m, :], turned_ps[:, m, :], ACT.Copy)
                    last.then_inc(copied, 1)

            sweep(act, step)

        @block.tensor
        def _(pe):
            def step(b):
                for n, s in enumerate(sides):
                    wait(pe, normed, 2 * b.blk + n + 1)
                    wait(pe, copied, 2 * b.blk + n)
                    for u in range(U):
                        last = pe.transpose(turned_ps[:, u // 4, u % 4 * C:(u % 4 + 1) * C],
                                            hidden[s][:, b.par, u, :], K.ident[:, :])
                    last.then_inc(turned, 1)
                wait(pe, out, outs.end(b.ago(1)))
                for n, s in enumerate(sides):
                    wait(pe, copied, 2 * b.blk + n + 1)
                    for u in range(U):
                        lhs = turned_sb[s][:, u // 4, u % 4 * C:(u % 4 + 1) * C]
                        if s == "far":
                            at = u % 2 * w1
                            last = pe.matmul(far_ps[:, u // 2, at:at + w1], lhs, K.w1[:, :], start=True, stop=True)
                        else:
                            last = pe.matmul(near_ps[:, u, :], lhs, K.w1r[:, :], start=True, stop=True)
                    last.then_inc(mixed, 1)

            sweep(pe, step)

        @block.vector
        def _(dve):
            def statistics(b):
                stats.at(b)
                wait(dve, gathered[b.par], 2 * 16 * U * (b.k + 1))
                for n, s in enumerate(sides):
                    x = rows[s][:, b.par, :, :]
                    last = stats.done(dve.tensor_tensor(x, x, middle(K.relu_b0[:, :], U), ALU.add))
                    dve.wait_ge(stat, last)
                    norm_sums(dve, stats, x, U, bn[s], small[s])
                for n, s in enumerate(sides):
                    wait(dve, deviation, 2 * b.blk + n + 1)
                    norm_scales(dve, stats, small[s])

            def results(b):
                outs.at(b)
                wait(dve, mixed, 2 * (b.blk + 1))
                wait(dve, stored[b.par], 32 * b.k)
                for m in range(4):
                    got = far_ps[:, m, 0:2 * w1].rearrange("p (u c) -> p u c", u=2)
                    outs.done(dve.tensor_copy(
                        heads[:, b.par, :, 2 * m:2 * m + 2, :].rearrange("p h u d -> p u h d"),
                        got[:, :, 0:2 * D].rearrange("p u (h d) -> p u h d", h=2)))
                last = outs.done(dve.tensor_copy(score[:, :, :], near_ps[:, :, :]))
                dve.wait_ge(out, last)
                settle(dve, settled_dve)
                for i in range(2):
                    columns = far_ps[:, :, 0:2 * w1].rearrange("p m (u c) -> p m u c", u=2)
                    outs.done(dve.tensor_tensor(
                        K.att[i][:, bass.ds(b.blk * U, U)].rearrange("p (m u) -> p m u", u=2),
                        columns[:, :, :, 2 * D + i], score[:, :, i].rearrange("p (m u) -> p m u", u=2),
                        ALU.add))

            def step(b):
                if b.within(NB):
                    statistics(b)
                if b.ago(1).within(NB):
                    results(b.ago(1))

            sweep(dve, step, lag=1)


def attention_weights(K):
    nc, d = K.nc, K.order["s"]
    with Phase(K, "att_w") as ph:
        cont, back = ph.sb("cont", [P, T]), d["next_cont"]
        cut, back_cut, first, first_cut, last_cut = (
            ph.sb(n, [P, T]) for n in ("cut", "back_cut", "first", "first_cut", "last_cut"))
        run, total, t1, shifted = (ph.sb(n, [P, T]) for n in ("run", "total", "t1", "shifted"))
        later_cut, earlier_cut, t2 = (ph.sb(n, [P, P]) for n in ("later_cut", "earlier_cut", "t2"))
        diag = ph.sb("diag", [P, 2, P])
        ends = ph.sb("ends", [P, 2])
        in1, in2 = ph.sb("in1", [P, 1]), ph.sb("in2", [P, 1])
        rows = ph.ps("rows", [P, 2, P])
        sums_ps = ph.ps("sums", [P, 2])
        line_sem, pe_step, act_step = ph.sem("dve_line"), ph.sem("pe_step"), ph.sem("act_step")
        ends_ready = ph.sem("ends_ready")
        exps = ph.sem("exps")
        block = ph.block()
        rounds = [(i, op) for i in range(2) for op in ("max", "add", "add")]

        @block.tensor
        def _(pe):
            for n, (_, op) in enumerate(rounds):
                pe.wait_ge(ends_ready, n + 1)
                if op == "max":
                    pe.matmul(rows[:, 0, :], K.ones[:, :], diag[:, 0, :], start=True, stop=True)
                    pe.matmul(rows[:, 1, :], K.ones[:, :], diag[:, 1, :], start=True, stop=True)\
                        .then_inc(pe_step, 1)
                else:
                    pe.matmul(sums_ps[:, 0:1], d["to_later"][:, :], ends[:, 0:1], start=True, stop=True)
                    pe.matmul(sums_ps[:, 1:2], d["from_earlier"][:, :], ends[:, 1:2], start=True, stop=True)\
                        .then_inc(pe_step, 1)

        @block.scalar
        def _(act):
            for i in range(2):
                act.wait_ge(exps, i + 1)
                act.activation(K.att[i][:, :], shifted[:, :], ACT.Exp).then_inc(act_step, 1)

        @block.vector
        def _(dve):
            line = Line(dve, line_sem)
            state = {"round": 0}
            line(dve.tensor_copy(cont[:, :], d["flags"][:, :, CONT]))
            line(dve.tensor_copy(first[:, :], d["flags"][:, :, FIRST]))
            for target, source in ((cut, cont[:, :]), (back_cut, back[:, :]), (first_cut, first[:, :]),
                                   (last_cut, d["last_seg"][:, :]), (later_cut, d["to_later"][:, :]),
                                   (earlier_cut, d["from_earlier"][:, :])):
                line(dve.tensor_scalar(target[:, :], source, BIG, -BIG, ALU.mult, ALU.add))

            def backwards(t):
                return t[:, T - 1::-1]

            def carry_ends(op):
                if op == "max":
                    line(dve.tensor_tensor_scan(backwards(total), backwards(back_cut), backwards(run),
                                                -BIG, ALU.add, ALU.max))
                else:
                    line(dve.scalar_tensor_tensor(t1[:, :], back[:, :], 0.0, run[:, :], ALU.is_equal, ALU.mult))
                    line(dve.tensor_tensor_scan(backwards(total), backwards(back), backwards(t1),
                                                0.0, ALU.mult, ALU.add))

            def segment_total(values, op):
                if op == "max":
                    line(dve.tensor_tensor_scan(run[:, :], cut[:, :], values, -BIG, ALU.add, ALU.max))
                else:
                    line(dve.tensor_tensor_scan(run[:, :], cont[:, :], values, 0.0, ALU.mult, ALU.add))
                carry_ends(op)
                line(dve.tensor_copy(ends[:, 0:1], run[:, T - 1:T]))
                if op == "max":
                    line(dve.tensor_copy(ends[:, 1:2], total[:, 0:1]))
                    line(dve.tensor_scalar(diag[:, 0, :], K.ident[:, :], ends[:, 0:1], None, ALU.mult))
                    dve.tensor_scalar(diag[:, 1, :], K.ident[:, :], ends[:, 1:2], None, ALU.mult)\
                        .then_inc(ends_ready, 1)
                else:
                    dve.tensor_copy(ends[:, 1:2], total[:, 0:1]).then_inc(ends_ready, 1)
                state["round"] += 1
                dve.wait_ge(pe_step, state["round"])
                if op == "max":
                    for m, (mask, target, edge_cut) in enumerate(((earlier_cut, in1, first_cut),
                                                                  (later_cut, in2, last_cut))):
                        line(dve.tensor_tensor(t2[:, :], mask[:, :], rows[:, m, :], ALU.add))
                        line(dve.tensor_reduce(target[:, :], t2[:, :], AX.X, ALU.max))
                        line(dve.tensor_scalar(t1[:, :], edge_cut[:, :], target[:, :], None, ALU.add))
                        line(dve.tensor_tensor(total[:, :], total[:, :], t1[:, :], ALU.max))
                else:
                    line(dve.tensor_copy(in1[:, :], sums_ps[:, 0:1]))
                    line(dve.tensor_copy(in2[:, :], sums_ps[:, 1:2]))
                    for mask, amount in ((first, in1), (d["last_seg"], in2)):
                        line(dve.scalar_tensor_tensor(total[:, :], mask[:, :], amount[:, :], total[:, :],
                                                      ALU.mult, ALU.add))

            for i in range(2):
                a = K.att[i][:, :]
                line(dve.scalar_tensor_tensor(a, a, ALPHA, a, ALU.mult, ALU.max))
                segment_total(a, "max")
                dve.tensor_tensor(shifted[:, :], a, total[:, :], ALU.subtract).then_inc(exps, 1)
                dve.wait_ge(act_step, i + 1)
                segment_total(a, "add")
                line(dve.reciprocal(t1[:, :], total[:, :]))
                line(dve.tensor_tensor(a, a, t1[:, :], ALU.mult))
                segment_total(a, "add")
                line(dve.scalar_tensor_tensor(total[:, :], total[:, :], 0.0, total[:, :], ALU.is_equal, ALU.add))
                line(dve.reciprocal(t1[:, :], total[:, :]))
                line(dve.tensor_tensor(a, a, t1[:, :], ALU.mult))


def running(dve, chain, b, states, messages, flags, head):
    chain.at(b)
    for u in range(U):
        before = states[:, b.par, u - 1, :] if u else states[:, 1 - b.par, U - 1, :]
        message = messages[:, b.par, u, :]
        wait(dve, chain.sem, chain.base + 2 * u - 1)
        chain.done(dve.scalar_tensor_tensor(states[:, b.par, u, :], before, flags[:, b.par, u, CONT:CONT + 1],
                                            message, ALU.mult, ALU.add))
        wait(dve, chain.sem, chain.base + 2 * u)
        chain.done(dve.scalar_tensor_tensor(head[:, :], message, flags[:, b.par, u, FIRST:FIRST + 1],
                                            head[:, :], ALU.mult, ALU.add))


def attention_hop1(K):
    nc, d = K.nc, K.order["s"]
    with Phase(K, "hop1") as ph:
        put_index = ph.sb("put_index", [P, 2, U], I32)
        messages = ph.sb("messages", [P, 2, U, D])
        states = ph.sb("states", [P, 2, U, D])
        head = ph.sb("head", [P, D])
        flags = ph.sb("flags", [P, 2, U, FLAGS])
        over_ps = ph.ps("over", [P, D])

        def pair(n):
            return [ph.sem(f"{n}{i}") for i in range(2)]

        put_in, rows_in, flags_in, sent = (pair(n) for n in ("put_in", "rows_in", "flags_in", "sent"))
        weigh, state = ph.sem("weigh"), ph.sem("state")
        settled, settled_dve, cleared, over, last_sem = (ph.sem(n) for n in (
            "settled", "settled_dve", "cleared", "over", "last"))
        weighed, sums = Chain(weigh, 1), Chain(state, 2 * U)
        block = ph.block()

        @block.sync
        def _(sp):
            def put_stage(b):
                wait(sp, sent[b.par], 16 * U * b.k)
                stage_index(sp, put_index, d["put"], b, put_in)

            def step(b):
                wait(sp, state, sums.end(b.ago(2)))
                sp.dma_start(messages[:, b.par, :, :],
                             K.H1.rearrange("(p t) d -> p t d", p=P)[:, bass.ds(b.blk * U, U), :])\
                    .then_inc(rows_in[b.par], 16)
                sp.dma_start(flags[:, b.par, :, :], d["flags"][:, bass.ds(b.blk * U, U), :])\
                    .then_inc(flags_in[b.par], 16)
                if b.ago(1).within(NB):
                    put_stage(b.ago(1))

            sweep(sp, step)
            put_stage(Step(NB // 2, 0))

        @block.gpsimd
        def _(pool):
            def step(b):
                wait(pool, put_in[b.par], 16 * (b.k + 1))
                wait(pool, state, sums.end(b))
                settle(pool, settled)
                scatter_rows(pool, K.HOP[:, :], put_index, b.par, states, sent)

            sweep(pool, step)
            for i in range(2):
                pool.wait_ge(sent[i], 16 * U * uses(NB, i))
            pool.wait_ge(cleared, 3)
            at = bass.IndirectOffsetOnAxis(ap=d["put_first"][:, 0:1], axis=0)
            put_rows(pool, K.HOP[:, :], at, states[:, 1, 0, :], False).then_inc(last_sem, 16)
            pool.wait_ge(last_sem, 16)

        @block.tensor
        def _(pe):
            pe.wait_ge(state, sums.per * NB)
            pe.matmul(over_ps[:, :], d["to_later"][:, :], states[:, (NB - 1) % 2, U - 1, :],
                      start=True, stop=True).then_inc(over, 1)

        @block.vector
        def _(dve):
            dve.memset(states[:, 1, U - 1, :], 0.0).then_inc(cleared, 1)
            dve.memset(head[:, :], 0.0).then_inc(cleared, 1)

            def step(b):
                weighed.at(b)
                wait(dve, rows_in[b.par], 16 * (b.k + 1))
                wait(dve, flags_in[b.par], 16 * (b.k + 1))
                wait(dve, sent[b.par], 16 * U * b.k)
                dve.wait_ge(cleared, 2)
                settle(dve, settled_dve)
                m = messages[:, b.par, :, :]
                weighed.done(dve.tensor_tensor(m, m, inner(K.att[1][:, bass.ds(b.blk * U, U)], D), ALU.mult))
                wait(dve, weigh, weighed.end(b))
                running(dve, sums, b, states, messages, flags, head)

            sweep(dve, step)
            dve.wait_ge(over, 1)
            dve.wait_ge(sent[1], 16 * U * uses(NB, 1))
            dve.wait_ge(state, sums.per * NB)
            dve.tensor_tensor(states[:, 1, 0, :], over_ps[:, :], head[:, :], ALU.add).then_inc(cleared, 1)


def attention_hop2(K):
    nc, d = K.nc, K.order["s"]
    b1, fc, bf = K.vec["L1_gnn_b"], K.vec["L1_gnn_fc"], K.vec["L1_gnn_bf"]
    with Phase(K, "hop2") as ph:
        index = ph.sb("index", [P, 2, U], I32)
        put_index = ph.sb("put_index", [P, 2, U], I32)
        messages = ph.sb("messages", [P, 2, U, C])
        states = ph.sb("states", [P, 2, U, C])
        result = ph.sb("result", [P, 2, U, C])
        work = ph.sb("work", [P, U, C])
        nan = ph.sb("nan", [P, U, C], I32)
        gate = ph.sb("gate", [P, U, 2])
        gate_sig = ph.sb("gate_sig", [P, U, 2])
        head = ph.sb("head", [P, C])
        flags = ph.sb("flags", [P, 2, U, FLAGS])
        over_ps = ph.ps("over", [P, C])

        def pair(n):
            return [ph.sem(f"{n}{i}") for i in range(2)]

        index_in, put_in, rows_in, flags_in, gathered, sent = (
            pair(n) for n in ("index_in", "put_in", "rows_in", "flags_in", "gathered", "sent"))
        weigh, state, post, gated = ph.sem("weigh"), ph.sem("state"), ph.sem("post"), ph.sem("gated")
        settled, settled_dve, cleared, over, last_sem, ends = (ph.sem(n) for n in (
            "settled", "settled_dve", "cleared", "over", "last", "ends"))
        weighed, sums = Chain(weigh, 2), Chain(state, 2 * U)
        posts = Chain(post, 9)
        BEFORE_GATE = 6
        block = ph.block()

        @block.sync
        def _(sp):
            stage_index(sp, index, d["far"], Step(0, 0), index_in)
            stage_index(sp, index, d["far"], Step(0, 1), index_in)

            def put_stage(b):
                wait(sp, sent[b.par], 16 * U * b.k)
                stage_index(sp, put_index, d["add"], b, put_in)

            def step(b):
                wait(sp, state, sums.end(b.ago(2)))
                sp.dma_start(messages[:, b.par, :, 0:D],
                             K.H0.rearrange("(p t) d -> p t d", p=P)[:, bass.ds(b.blk * U, U), :])\
                    .then_inc(rows_in[b.par], 16)
                sp.dma_start(flags[:, b.par, :, :], d["flags"][:, bass.ds(b.blk * U, U), :])\
                    .then_inc(flags_in[b.par], 16)
                if b.ago(1).within(NB):
                    put_stage(b.ago(1))
                if b.ago(-2).within(NB):
                    wait(sp, gathered[b.par], 16 * U * (b.k + 1))
                    stage_index(sp, index, d["far"], b.ago(-2), index_in)

            sweep(sp, step)
            put_stage(Step(NB // 2, 0))

        @block.gpsimd
        def _(pool):
            def gather(b):
                wait(pool, index_in[b.par], 16 * (b.k + 1))
                wait(pool, state, sums.end(b.ago(2)))
                settle(pool, settled)
                for u in range(U):
                    pool.indirect_dma_start(messages[:, b.par, u, D:C], None, K.HOP[:, :],
                                            bass.IndirectOffsetOnAxis(ap=index[:, b.par, u:u + 1], axis=0))\
                        .then_inc(gathered[b.par], 16)

            def step(b):
                if b.ago(-2).within(NB):
                    gather(b.ago(-2))
                wait(pool, put_in[b.par], 16 * (b.k + 1))
                wait(pool, post, posts.end(b))
                settle(pool, settled)
                scatter_rows(pool, K.X[:, :], put_index, b.par, result, sent, accumulate=True)

            gather(Step(0, 0))
            gather(Step(0, 1))
            sweep(pool, step)
            for i in range(2):
                pool.wait_ge(sent[i], 16 * U * uses(NB, i))
            pool.wait_ge(ends, 9)
            at = bass.IndirectOffsetOnAxis(ap=d["add_first"][:, 0:1], axis=0)
            put_rows(pool, K.X[:, :], at, result[:, 1, 0, :], True).then_inc(last_sem, 16)
            pool.wait_ge(last_sem, 16)

        @block.tensor
        def _(pe):
            pe.wait_ge(state, sums.per * NB)
            pe.matmul(over_ps[:, :], d["to_later"][:, :], states[:, (NB - 1) % 2, U - 1, :],
                      start=True, stop=True).then_inc(over, 1)

        @block.scalar
        def _(act):
            def gates(u):
                act.activation(gate_sig[:, 0:u, :], gate[:, 0:u, :], ACT.Sigmoid).then_inc(gated, 1)

            def step(b):
                wait(act, post, posts.base_of(b) + BEFORE_GATE)
                gates(U)

            sweep(act, step)
            act.wait_ge(ends, 6)
            gates(1)

        @block.vector
        def _(dve):
            dve.memset(states[:, 1, U - 1, :], 0.0).then_inc(cleared, 1)
            dve.memset(head[:, :], 0.0).then_inc(cleared, 1)

            def message_sums(b):
                weighed.at(b)
                wait(dve, rows_in[b.par], 16 * (b.k + 1))
                wait(dve, flags_in[b.par], 16 * (b.k + 1))
                wait(dve, gathered[b.par], 16 * U * (b.k + 1))
                wait(dve, post, posts.base_of(b.ago(2)) + 2)
                dve.wait_ge(cleared, 2)
                settle(dve, settled_dve)
                for i in range(2):
                    m = messages[:, b.par, :, i * D:(i + 1) * D]
                    weighed.done(dve.tensor_tensor(m, m, inner(K.att[i][:, bass.ds(b.blk * U, U)], D), ALU.mult))
                wait(dve, weigh, weighed.end(b))
                running(dve, sums, b, states, messages, flags, head)

            def rows_out(step_done, sem, s, v, n, wait_gate):
                w, m, g, gs = work[:, 0:n, :], nan[:, 0:n, :], gate[:, 0:n, :], gate_sig[:, 0:n, :]
                halves = lambda t: t.rearrange("p u (h d) -> p (u h) d", h=2)
                step_done(dve.tensor_tensor(m, s, s, ALU.not_equal))
                last = step_done(dve.tensor_tensor(v, s, middle(b1[:, :], n), ALU.add))
                dve.wait_ge(sem, last)
                settle(dve, settled_dve)
                last = step_done(dve.copy_predicated(v, m, middle(b1[:, :], n)))
                dve.wait_ge(sem, last)
                last = step_done(dve.tensor_tensor(w, v, middle(fc[:, :], n), ALU.mult))
                dve.wait_ge(sem, last)
                last = step_done(dve.tensor_reduce(g.rearrange("p u h -> p (u h)"), halves(w), AX.X, ALU.add))
                dve.wait_ge(sem, last)
                step_done(dve.tensor_tensor(g, g, middle(bf[:, :], n), ALU.add))
                wait_gate()
                flat = gs.rearrange("p u h -> p (u h)")
                last = step_done(dve.scalar_tensor_tensor(halves(w), halves(v), 0.0, inner(flat, D),
                                                          ALU.min, ALU.mult))
                dve.wait_ge(sem, last)
                last = step_done(dve.scalar_tensor_tensor(w, w, ALPHA, middle(K.c1[:, :], n),
                                                          ALU.mult, ALU.subtract))
                dve.wait_ge(sem, last)
                step_done(dve.scalar_tensor_tensor(v, v, 0.0, w, ALU.max, ALU.add))

            def finish(b):
                posts.at(b)
                wait(dve, state, sums.end(b))
                wait(dve, sent[b.par], 16 * U * b.k)
                wait(dve, post, posts.base_of(b))
                rows_out(posts.done, post, states[:, b.par, :, :], result[:, b.par, :, :], U,
                         lambda: wait(dve, gated, b.blk + 1))

            def step(b):
                message_sums(b)
                finish(b)

            sweep(dve, step)
            dve.wait_ge(over, 1)
            dve.wait_ge(sent[1], 16 * U * uses(NB, 1))
            dve.wait_ge(post, posts.per * NB)
            line = Chain(ends, 9)
            line.at(Step(0, 0))
            dve.tensor_tensor(states[:, 1, 0, :], over_ps[:, :], head[:, :], ALU.add).then_inc(cleared, 1)
            dve.wait_ge(cleared, 3)
            rows_out(line.done, ends, states[:, 1, 0:1, :], result[:, 1, 0:1, :], 1,
                     lambda: dve.wait_ge(gated, NB + 1))


NP = 125
R = 10
NODE_BLOCKS = N // (NP * R)
assert NODE_BLOCKS * NP * R == N
SPLIT = 112


def layer2_nodes(K):
    nc = K.nc
    with Phase(K, "nodes") as ph:
        def buf(n, parities=2):
            return ph.sb(n, [NP, parities, R, C])

        x, agg, result = buf("x", 4), buf("agg"), buf("result")
        base = buf("base", 4)
        hidden = buf("hidden")
        turned_sb = ph.sb("turned_sb", [P, 3, 512])
        act_out = buf("act_out")
        offset = ph.sb("offset", [NP, C])
        half = ph.sb("half", [NP, R])
        bn = ph.sb("bn", [NP, 2, R, 6])
        small = [{k: ph.sb(f"n{i}_{k}", [NP, R])[:, :] for k in
                  ("diff", "sum", "m2", "sq", "q", "std", "rstd", "nmr")} for i in range(2)]
        turned_ps = ph.ps("turned_ps", [P, 3, 512])
        mixed_ps = ph.ps("mixed_ps", [P, 3, 512])

        def pair(n):
            return [ph.sem(f"{n}{i}") for i in range(2)]

        x_in, agg_in, stored = [ph.sem(f"x_in{i}") for i in range(4)], pair("agg_in"), pair("stored")
        added, based, gelu, normed1, normed2 = (ph.sem(n) for n in (
            "added", "based", "gelu", "normed1", "normed2"))
        turned, copied, mixed, ready, settled, joined, scaled1, scaled2 = (ph.sem(n) for n in (
            "turned", "copied", "mixed", "ready", "settled", "joined", "scaled1", "scaled2"))
        sums1, sums2 = (Chain(ph.sem(n), R + 5) for n in ("sums1", "sums2"))
        roots1, roots2 = (Chain(ph.sem(n), 2) for n in ("roots1", "roots2"))
        outs = Chain(ph.sem("out"), 2)
        block = ph.block()
        view = lambda t: t.rearrange("(p r) d -> p r d", p=NP)
        X, AGG, OUT = view(K.X[0:N, :]), view(K.AGG[:, :]), view(K.out)
        parts = (slice(0, SPLIT), slice(SPLIT, NP))
        banks = [(m, min(4, R - 4 * m)) for m in range(3)]

        @block.sync
        def _(sp):
            def step(b):
                if b.ago(-1).within(NODE_BLOCKS):
                    load_x(b.ago(-1))
                if b.within(NODE_BLOCKS):
                    load_agg(b)
                if b.ago(4).within(NODE_BLOCKS):
                    store(b.ago(4))

            def load_x(b):
                wait(sp, normed1, b.blk - 3)
                wait(sp, based, b.blk - 3)
                for p in parts:
                    sp.dma_start(x[p, b.slot, :, :], X[p, bass.ds(b.blk * R, R), :]).then_inc(x_in[b.slot], 16)

            def load_agg(b):
                wait(sp, mixed, b.blk - 1)
                for p in parts:
                    sp.dma_start(agg[p, b.par, :, :], AGG[p, bass.ds(b.blk * R, R), :]).then_inc(agg_in[b.par], 16)

            def store(b):
                wait(sp, outs.sem, outs.end(b))
                for p in parts:
                    sp.dma_start(OUT[p, bass.ds(b.blk * R, R), :], result[p, b.par, :, :]).then_inc(stored[b.par], 16)

            load_x(Step(0, 0, 0, 0))
            sweep_by_4(sp, step, NODE_BLOCKS, 4)
            for i in range(2):
                sp.wait_ge(stored[i], 32 * uses(NODE_BLOCKS, i))

        @block.gpsimd
        def _(pool):
            pool.memset(half[:, :], -0.5).then_inc(ready, 1)
            pool.tensor_tensor(offset[:, :], K.vec["L2_gnn_beta"][0:NP, :], K.vec["L3_gnn_bo"][0:NP, :], ALU.add)\
                .then_inc(ready, 1)
            pool.wait_ge(ready, 2)

            def x_stage(b):
                wait(pool, x_in[b.slot], 32 * (b.quad + 1))
                xb = x[:, b.slot, :, :]
                pool.tensor_tensor(xb, xb, middle(K.x2_less_x[0:NP, :], R), ALU.add).then_inc(added, 1)

            def root(b, sums, roots, sm, normed):
                roots.at(b)
                wait(pool, sums.sem, sums.end(b))
                wait(pool, normed, b.blk)
                settle(pool, settled)
                last = roots.done(pool.tensor_scalar(sm["std"], sm["q"], 1.0 / C, EPS, ALU.mult, ALU.add))
                wait(pool, roots.sem, last)
                roots.done(pool.tensor_tensor(sm["rstd"], sm["std"], half[:, :], ALU.pow))

            def step(b):
                after, older = b.ago(-2), b.ago(2)
                if b.within(NODE_BLOCKS):
                    root(b, sums1, roots1, small[0], normed1)
                    wait(pool, outs.sem, outs.end(b.ago(4)))
                    pool.tensor_tensor(base[:, b.slot, :, :], x[:, b.slot, :, :], middle(offset[:, :], R), ALU.add)\
                        .then_inc(based, 1)
                if older.within(NODE_BLOCKS):
                    root(older, sums2, roots2, small[1], normed2)
                if after.within(NODE_BLOCKS):
                    x_stage(after)

            x_stage(Step(0, 0, 0, 0))
            x_stage(Step(0, 1, 0, 1))
            sweep_by_4(pool, step, NODE_BLOCKS, 2)

        @block.scalar
        def _(act):
            def norm(i, source, target, func):
                for u in range(R):
                    last = act.activation(target[:, u, :], source[:, u, :], func,
                                          bias=small[i]["nmr"][:, u:u + 1], scale=small[i]["rstd"][:, u:u + 1])
                return last

            def step(b):
                before, older = b.ago(1), b.ago(2)
                if b.within(NODE_BLOCKS):
                    wait(act, scaled1, b.blk + 1)
                    wait(act, joined, b.blk - 1)
                    wait(act, turned, b.blk - 1)
                    norm(0, x[:, b.slot, :, :], hidden[:, b.par, :, :], ACT.Relu).then_inc(normed1, 1)
                if before.within(NODE_BLOCKS):
                    wait(act, mixed, before.blk + 1)
                    wait(act, outs.sem, outs.base_of(before.ago(2)) + 1)
                    for m, n in banks:
                        last = act.activation(act_out[:, before.par, 4 * m:4 * m + n, :],
                                              mixed_ps[0:NP, m, 0:n * C].rearrange("p (u c) -> p u c", c=C), ACT.Gelu)
                    last.then_inc(gelu, 1)
                if b.within(NODE_BLOCKS):
                    wait(act, turned, b.blk + 1)
                    wait(act, mixed, b.blk)
                    for m, n in banks:
                        last = act.activation(turned_sb[:, m, 0:n * NP], turned_ps[:, m, 0:n * NP], ACT.Copy)
                    last.then_inc(copied, 1)
                if older.within(NODE_BLOCKS):
                    wait(act, scaled2, older.blk + 1)
                    norm(1, act_out[:, older.par, :, :], act_out[:, older.par, :, :], ACT.Identity).then_inc(normed2, 1)

            sweep_by_4(act, step, NODE_BLOCKS, 2)

        @block.tensor
        def _(pe):
            def step(b):
                wait(pe, normed1, b.blk + 1)
                wait(pe, copied, b.blk)
                for u in range(R):
                    last = pe.transpose(turned_ps[:, u // 4, u % 4 * NP:(u % 4 + 1) * NP],
                                        hidden[:, b.par, u, :], K.ident[0:NP, 0:NP])
                last.then_inc(turned, 1)
                wait(pe, gelu, b.blk)
                wait(pe, agg_in[b.par], 32 * (b.k + 1))
                for m, n in banks:
                    pe.matmul(mixed_ps[0:NP, m, 0:n * C], K.ident[0:NP, 0:NP],
                              agg[:, b.par, 4 * m:4 * m + n, :].rearrange("p u c -> p (u c)"), start=True, stop=False)
                wait(pe, copied, b.blk + 1)
                for u in range(R):
                    last = pe.matmul(mixed_ps[0:NP, u // 4, u % 4 * C:(u % 4 + 1) * C],
                                     turned_sb[:, u // 4, u % 4 * NP:(u % 4 + 1) * NP],
                                     K.wself[:, :], start=False, stop=u % 4 == 3 or u == R - 1)
                last.then_inc(mixed, 1)

            sweep_by_4(pe, step, NODE_BLOCKS, 0)

        @block.vector
        def _(dve):
            def sums(b, c, i, rows, scaled):
                c.at(b)
                wait(dve, scaled, b.blk)
                norm_sums(dve, c, rows, R, bn[:, i, :, :], small[i])

            def scales(b, roots, i, normed, scaled):
                wait(dve, roots.sem, roots.end(b))
                wait(dve, normed, b.blk)
                sm = small[i]
                dve.scalar_tensor_tensor(sm["nmr"], sm["sum"], -0.5, sm["rstd"], ALU.mult, ALU.mult)\
                    .then_inc(scaled, 1)

            def step(b):
                older, oldest = b.ago(2), b.ago(3)
                if b.within(NODE_BLOCKS):
                    wait(dve, added, b.blk + 1)
                    sums(b, sums1, 0, x[:, b.slot, :, :], scaled1)
                if older.within(NODE_BLOCKS):
                    wait(dve, gelu, older.blk + 1)
                    a = act_out[:, older.par, :, :]
                    dve.tensor_tensor(a, a, hidden[:, older.par, :, :], ALU.add).then_inc(joined, 1)
                if b.within(NODE_BLOCKS):
                    scales(b, roots1, 0, normed1, scaled1)
                if older.within(NODE_BLOCKS):
                    wait(dve, joined, older.blk + 1)
                    sums(older, sums2, 1, a, scaled2)
                if oldest.within(NODE_BLOCKS):
                    results(oldest)
                if older.within(NODE_BLOCKS):
                    scales(older, roots2, 1, normed2, scaled2)

            def results(b):
                outs.at(b)
                wait(dve, normed2, b.blk + 1)
                wait(dve, stored[b.par], 32 * b.k)
                wait(dve, based, b.blk + 1)
                r = result[:, b.par, :, :]
                last = outs.done(dve.tensor_tensor(r, act_out[:, b.par, :, :],
                                                   middle(K.vec["L2_gnn_gamma"][0:NP, :], R), ALU.mult))
                wait(dve, outs.sem, last)
                outs.done(dve.tensor_tensor(r, r, base[:, b.slot, :, :], ALU.add))

            sweep_by_4(dve, step, NODE_BLOCKS, 3)


def scores(K):
    nc, d = K.nc, K.order["s"]
    with Phase(K, "scores") as ph:
        sides = ("near", "far")
        index = {s: ph.sb(f"index_{s}", [P, 2, U], I32) for s in sides}
        rows = {s: ph.sb(f"rows_{s}", [P, 2, U, C]) for s in sides}
        plain = {s: ph.sb(f"plain_{s}", [P, U, C]) for s in sides}
        hidden = {s: ph.sb(f"hidden_{s}", [P, U, C]) for s in sides}
        row_sums = ph.sb("row_sums", [P, 2, 2, U])
        bn = {s: ph.sb(f"bn_{s}", [P, U, 6]) for s in sides}
        small = {s: small_tiles(ph, f"norm_{s}", U) for s in sides}
        turned_sb = {s: ph.sb(f"turned_{s}", [P, 2, 512]) for s in sides}
        q_sb, k_sb = ph.sb("q_sb", [P, U, C]), ph.sb("k_sb", [P, U, C])
        values = ph.sb("values", [P, 2, U, C])
        turned_ps = ph.ps("turned_ps", [P, 2, 512])
        q_ps = ph.ps("q_ps", [P, 2, 512])
        kv_ps = ph.ps("kv_ps", [P, 4, 512])

        def pair(n):
            return [ph.sem(f"{n}{i}") for i in range(2)]

        index_in, gathered, v_out, row_out = pair("index_in"), pair("gathered"), pair("v_out"), pair("row_out")
        stat, out = ph.sem("stat"), ph.sem("out")
        deviation, normed, turned, copied, mixed, settled, settled_dve = (ph.sem(n) for n in (
            "deviation", "normed", "turned", "copied", "mixed", "settled", "settled_dve"))
        SUMS = 1 + U + 5
        stats = Chain(stat, 2 * SUMS + 4)
        outs = Chain(out, 6)
        block = ph.block()

        @block.sync
        def _(sp):
            def index_blocks(b):
                for s in sides:
                    stage_index(sp, index[s], d[s], b, index_in)

            index_blocks(Step(0, 0))
            index_blocks(Step(0, 1))
            at = lambda table, b: table.rearrange("(p t) d -> p t d", p=P)[:, bass.ds(b.blk * U, U), :]

            def step(b):
                if b.within(NB):
                    wait(sp, gathered[b.par], 2 * 16 * U * (b.k + 1))
                    sp.dma_start(at(K.ROW, b), rows["near"][:, b.par, :, :]).then_inc(row_out[b.par], 16)
                if b.ago(-2).within(NB):
                    index_blocks(b.ago(-2))
                if b.ago(1).within(NB):
                    before = b.ago(1)
                    wait(sp, out, outs.base_of(before) + 3)
                    sp.dma_start(at(K.V, before), values[:, before.par, :, :]).then_inc(v_out[before.par], 16)

            sweep(sp, step, lag=1)
            for i in range(2):
                sp.wait_ge(row_out[i], 16 * uses(NB, i))
                sp.wait_ge(v_out[i], 16 * uses(NB, i))

        @block.gpsimd
        def _(pool):
            def step(b):
                wait(pool, index_in[b.par], 32 * (b.k + 1))
                wait(pool, row_out[b.par], 16 * b.k)
                wait(pool, stat, stats.base_of(b.ago(2)) + SUMS + 1)
                settle(pool, settled)
                for s in sides:
                    gather_rows(pool, K.out, index[s], b.par, rows[s], gathered)

            sweep(pool, step)

        @block.scalar
        def _(act):
            def step(b):
                for n, s in enumerate(sides):
                    wait(act, stat, stats.base_of(b) + (n + 1) * SUMS)
                    act.activation(small[s]["std"], small[s]["q"], ACT.Sqrt, bias=K.eps[:, :], scale=1.0 / C)\
                        .then_inc(deviation, 1)
                wait(act, out, outs.base_of(b.ago(2)) + 4)
                for n, s in enumerate(sides):
                    wait(act, stat, stats.base_of(b) + 2 * SUMS + 2 * (n + 1))
                    wait(act, turned, 2 * (b.blk - 1) + n + 1)
                    for u in range(U):
                        last = act.activation(hidden[s][:, u, :], plain[s][:, u, :], ACT.Relu,
                                              bias=small[s]["nmr"][:, u:u + 1],
                                              scale=small[s]["rstd"][:, u:u + 1],
                                              accum_out=row_sums[:, b.par, n, u:u + 1])
                    last.then_inc(normed, 1)
                for n, s in enumerate(sides):
                    wait(act, turned, 2 * b.blk + n + 1)
                    wait(act, mixed, 2 * (b.blk - 1) + n + 1)
                    for m in range(2):
                        last = act.activation(turned_sb[s][:, m, :], turned_ps[:, m, :], ACT.Copy)
                    last.then_inc(copied, 1)

            sweep(act, step)

        @block.tensor
        def _(pe):
            def step(b):
                before = outs.base_of(b.ago(1))
                for n, s in enumerate(sides):
                    wait(pe, normed, 2 * b.blk + n + 1)
                    wait(pe, copied, 2 * b.blk + n)
                    for u in range(U):
                        last = pe.transpose(turned_ps[:, u // 4, u % 4 * C:(u % 4 + 1) * C],
                                            hidden[s][:, u, :], K.ident[:, :])
                    last.then_inc(turned, 1)
                wait(pe, out, before + 1)
                for u in range(U):
                    at = slice(u % 4 * C, (u % 4 + 1) * C)
                    last = pe.matmul(q_ps[:, u // 4, at], turned_sb["near"][:, u // 4, at], K.wq[:, :],
                                     start=True, stop=True)
                last.then_inc(mixed, 1)
                wait(pe, copied, 2 * (b.blk + 1))
                wait(pe, out, before + 3)
                for u in range(U):
                    last = pe.matmul(kv_ps[:, u // 2, u % 2 * 2 * C:(u % 2 + 1) * 2 * C],
                                     turned_sb["far"][:, u // 4, u % 4 * C:(u % 4 + 1) * C], K.wkv[:, :],
                                     start=True, stop=True)
                last.then_inc(mixed, 1)

            sweep(pe, step)

        @block.vector
        def _(dve):
            def statistics(b):
                stats.at(b)
                wait(dve, gathered[b.par], 2 * 16 * U * (b.k + 1))
                wait(dve, normed, 2 * b.blk)
                for s in sides:
                    last = stats.done(dve.tensor_tensor(plain[s][:, :, :], rows[s][:, b.par, :, :],
                                                        middle(K.vec["L3_gnn_bo"][:, :], U), ALU.subtract))
                    wait(dve, stat, last)
                    norm_sums(dve, stats, plain[s], U, bn[s], small[s])
                for n, s in enumerate(sides):
                    wait(dve, deviation, 2 * b.blk + n + 1)
                    norm_scales(dve, stats, small[s])

            def products(b):
                outs.at(b)
                kv = kv_ps[:, :, :].rearrange("p m (g c) -> p (m g) c", g=2)
                bias = lambda n: middle(K.vec[n][:, :], U)
                wait(dve, mixed, 2 * b.blk + 1)
                wait(dve, out, outs.base)
                outs.done(dve.tensor_tensor(q_sb[:, :, :], q_ps[:, :, :].rearrange("p m (g c) -> p (m g) c", c=C),
                                            bias("L3_gnn_bq"), ALU.add))
                wait(dve, mixed, 2 * b.blk + 2)
                outs.done(dve.tensor_tensor(k_sb[:, :, :], kv[:, :, 0:C], bias("L3_gnn_bk"), ALU.add))
                wait(dve, v_out[b.par], 16 * b.k)
                outs.done(dve.tensor_tensor(values[:, b.par, :, :], kv[:, :, C:2 * C], bias("L3_gnn_bv"), ALU.add))
                wait(dve, normed, 2 * b.blk + 2)
                settle(dve, settled_dve)
                outs.done(dve.tensor_tensor(K.mean_diff[:, bass.ds(b.blk * U, U)], row_sums[:, b.par, 1, :],
                                            row_sums[:, b.par, 0, :], ALU.subtract))
                wait(dve, out, outs.base + 2)
                last = outs.done(dve.tensor_tensor(q_sb[:, :, :], q_sb[:, :, :], k_sb[:, :, :], ALU.mult))
                wait(dve, out, last)
                settle(dve, settled_dve)
                outs.done(dve.tensor_reduce(
                    K.score[:, bass.ds(b.blk * U, U), :].rearrange("p u h -> p (u h)"),
                    q_sb[:, :, :].rearrange("p u (h e) -> p (u h) e", e=HD), AX.X, ALU.add))

            def step(b):
                if b.within(NB):
                    statistics(b)
                if b.ago(1).within(NB):
                    products(b.ago(1))

            sweep(dve, step, lag=1)


def score_softmax(K):
    nc, d = K.nc, K.order["s"]
    with Phase(K, "softmax") as ph:
        t1 = ph.sb("t1", [P, T, HEADS])
        cut = ph.sb("cut", [P, T])
        top = ph.sb("top", [P, HEADS])
        top8 = ph.sb("top8", [HEADS, 1])
        diag = ph.sb("diag", [HEADS, HEADS])
        total = ph.sb("total", [P, HEADS])
        turned_ps = ph.ps("turned_ps", [HEADS, P])
        max_ps = ph.ps("max_ps", [P, HEADS])
        sum_ps = ph.ps("sum_ps", [P, HEADS])
        line_sem, ready, pe_step, act_step = (ph.sem(n) for n in ("line", "ready", "pe_step", "act_step"))
        block = ph.block()
        by_head = lambda t: t.rearrange("p t h -> p h t")

        @block.tensor
        def _(pe):
            pe.wait_ge(ready, 1)
            pe.transpose(turned_ps[:, :], top[:, :], K.ident[:, :]).then_inc(pe_step, 1)
            pe.wait_ge(ready, 2)
            pe.matmul(max_ps[:, :], K.ones[0:HEADS, :], diag[:, :], start=True, stop=True).then_inc(pe_step, 1)
            pe.wait_ge(ready, 4)
            pe.matmul(sum_ps[:, :], K.ones[:, :], total[:, :], start=True, stop=True).then_inc(pe_step, 1)

        @block.scalar
        def _(act):
            act.wait_ge(ready, 3)
            act.activation(K.score[:, :, :], K.score[:, :, :], ACT.Exp).then_inc(act_step, 1)

        @block.vector
        def _(dve):
            line = Line(dve, line_sem)
            sc = K.score[:, :, :]
            line(dve.scalar_tensor_tensor(sc, sc, float(1 / np.sqrt(HD)), inner(d["weight"][:, :], HEADS),
                                          ALU.mult, ALU.add))
            line(dve.tensor_scalar(K.mean_diff[:, :], K.mean_diff[:, :], 1.0 / C, None, ALU.mult))
            line(dve.tensor_tensor(t1[:, :, :], inner(K.mean_diff[:, :], HEADS), middle(K.vec["L3_gnn_Wd"][:, :], T),
                                   ALU.mult))
            line(dve.tensor_tensor(sc, sc, t1[:, :, :], ALU.add))
            line(dve.tensor_tensor(sc, sc, middle(K.vec["L3_gnn_bd"][:, :], T), ALU.add))
            line(dve.tensor_scalar(cut[:, :], d["real"][:, :], BIG, -BIG, ALU.mult, ALU.add))
            line(dve.tensor_tensor(sc, sc, inner(cut[:, :], HEADS), ALU.add))
            dve.tensor_reduce(top[:, :], by_head(sc), AX.X, ALU.max).then_inc(ready, 1)
            dve.wait_ge(pe_step, 1)
            line(dve.tensor_reduce(top8[:, :], turned_ps[:, :], AX.X, ALU.max))
            dve.tensor_scalar(diag[:, :], K.ident[0:HEADS, 0:HEADS], top8[:, :], None, ALU.mult).then_inc(ready, 1)
            dve.wait_ge(pe_step, 2)
            line(dve.tensor_copy(top[:, :], max_ps[:, :]))
            dve.tensor_tensor(sc, sc, middle(top[:, :], T), ALU.subtract).then_inc(ready, 1)
            dve.wait_ge(act_step, 1)
            dve.tensor_reduce(total[:, :], by_head(sc), AX.X, ALU.add).then_inc(ready, 1)
            dve.wait_ge(pe_step, 3)
            line(dve.reciprocal(total[:, :], sum_ps[:, :]))
            line(dve.tensor_tensor(sc, sc, middle(total[:, :], T), ALU.mult))


def layer3(K):
    nc, d = K.nc, K.order["s"]
    with Phase(K, "layer3") as ph:
        put_index = ph.sb("put_index", [P, 2, U], I32)
        messages = ph.sb("messages", [P, 2, U, C])
        own = ph.sb("own", [P, 2, U, C])
        own_first = ph.sb("own_first", [P, C])
        states = ph.sb("states", [P, 2, U, C])
        result = ph.sb("result", [P, 2, U, C])
        head = ph.sb("head", [P, C])
        flags = ph.sb("flags", [P, 2, U, FLAGS])
        turned_sb = ph.sb("turned_sb", [P, 2, 512])
        turned_ps = ph.ps("turned_ps", [P, 2, 512])
        mixed_ps = ph.ps("mixed_ps", [P, 2, 512])
        over_ps = ph.ps("over", [P, C])

        def pair(n):
            return [ph.sem(f"{n}{i}") for i in range(2)]

        put_in, rows_in, flags_in, own_in, sent = (pair(n) for n in ("put_in", "rows_in", "flags_in", "own_in", "sent"))
        weigh, state, post = ph.sem("weigh"), ph.sem("state"), ph.sem("post")
        settled, settled_dve, cleared, over, last_sem, turned, copied, mixed, first_in = (ph.sem(n) for n in (
            "settled", "settled_dve", "cleared", "over", "last", "turned", "copied", "mixed", "first_in"))
        weighed, sums, posts = Chain(weigh, 1), Chain(state, 2 * U), Chain(post, 2)
        block = ph.block()

        @block.sync
        def _(sp):
            at = lambda table, b: table.rearrange("(p t) d -> p t d", p=P)[:, bass.ds(b.blk * U, U), :]
            sp.dma_start(own_first[:, :], K.ROW.rearrange("(p t) d -> p t d", p=P)[:, 0, :]).then_inc(first_in, 16)

            def put_stage(b):
                wait(sp, sent[b.par], 16 * U * b.k)
                stage_index(sp, put_index, d["put"], b, put_in)

            def step(b):
                wait(sp, state, sums.end(b.ago(2)))
                sp.dma_start(messages[:, b.par, :, :], at(K.V, b)).then_inc(rows_in[b.par], 16)
                sp.dma_start(flags[:, b.par, :, :], d["flags"][:, bass.ds(b.blk * U, U), :])\
                    .then_inc(flags_in[b.par], 16)
                wait(sp, post, posts.end(b.ago(2)))
                sp.dma_start(own[:, b.par, :, :], at(K.ROW, b)).then_inc(own_in[b.par], 16)
                if b.ago(1).within(NB):
                    put_stage(b.ago(1))

            sweep(sp, step)
            put_stage(Step(NB // 2, 0))

        @block.gpsimd
        def _(pool):
            def step(b):
                wait(pool, put_in[b.par], 16 * (b.k + 1))
                wait(pool, post, posts.end(b))
                settle(pool, settled)
                scatter_rows(pool, K.out, put_index, b.par, result, sent)

            sweep(pool, step)
            for i in range(2):
                pool.wait_ge(sent[i], 16 * U * uses(NB, i))
            pool.wait_ge(cleared, 4)
            at = bass.IndirectOffsetOnAxis(ap=d["put_first"][:, 0:1], axis=0)
            put_rows(pool, K.out, at, result[:, 1, 0, :], False).then_inc(last_sem, 16)
            pool.wait_ge(last_sem, 16)

        @block.scalar
        def _(act):
            def step(b):
                wait(act, turned, b.blk + 1)
                wait(act, mixed, b.blk)
                for m in range(2):
                    last = act.activation(turned_sb[:, m, :], turned_ps[:, m, :], ACT.Copy)
                last.then_inc(copied, 1)

            sweep(act, step)
            act.wait_ge(turned, NB + 1)
            act.wait_ge(mixed, NB)
            act.activation(turned_sb[:, 0, 0:C], turned_ps[:, 0, 0:C], ACT.Copy).then_inc(copied, 1)

        @block.tensor
        def _(pe):
            tile_at = lambda t, u: t[:, u // 4, u % 4 * C:(u % 4 + 1) * C]

            def step(b):
                wait(pe, state, sums.end(b))
                wait(pe, copied, b.blk)
                for u in range(U):
                    last = pe.transpose(tile_at(turned_ps, u), states[:, b.par, u, :], K.ident[:, :])
                last.then_inc(turned, 1)
                wait(pe, copied, b.blk + 1)
                wait(pe, post, posts.end(b.ago(1)))
                for u in range(U):
                    last = pe.matmul(tile_at(mixed_ps, u), tile_at(turned_sb, u), K.wo[:, :], start=True, stop=True)
                last.then_inc(mixed, 1)

            sweep(pe, step)
            pe.matmul(over_ps[:, :], d["to_later"][:, :], states[:, (NB - 1) % 2, U - 1, :],
                      start=True, stop=True).then_inc(over, 1)
            pe.wait_ge(cleared, 3)
            pe.wait_ge(copied, NB)
            pe.transpose(tile_at(turned_ps, 0), states[:, 1, 0, :], K.ident[:, :]).then_inc(turned, 1)
            pe.wait_ge(copied, NB + 1)
            pe.wait_ge(post, posts.per * NB)
            pe.matmul(tile_at(mixed_ps, 0), tile_at(turned_sb, 0), K.wo[:, :], start=True, stop=True).then_inc(mixed, 1)

        @block.vector
        def _(dve):
            dve.memset(states[:, 1, U - 1, :], 0.0).then_inc(cleared, 1)
            dve.memset(head[:, :], 0.0).then_inc(cleared, 1)

            def message_sums(b):
                weighed.at(b)
                wait(dve, rows_in[b.par], 16 * (b.k + 1))
                wait(dve, flags_in[b.par], 16 * (b.k + 1))
                wait(dve, turned, b.blk - 1)
                dve.wait_ge(cleared, 2)
                settle(dve, settled_dve)
                m = messages[:, b.par, :, :].rearrange("p u (h e) -> p (u h) e", e=HD)
                share = K.score[:, bass.ds(b.blk * U, U), :].rearrange("p u h -> p (u h)")
                weighed.done(dve.tensor_tensor(m, m, inner(share, HD), ALU.mult))
                wait(dve, weigh, weighed.end(b))
                running(dve, sums, b, states, messages, flags, head)

            def finish(b):
                posts.at(b)
                wait(dve, mixed, b.blk + 1)
                wait(dve, own_in[b.par], 16 * (b.k + 1))
                wait(dve, sent[b.par], 16 * U * b.k)
                for m in range(2):
                    part = slice(4 * m, 4 * m + 4)
                    posts.done(dve.tensor_tensor(result[:, b.par, part, :],
                                                 mixed_ps[:, m, :].rearrange("p (u c) -> p u c", c=C),
                                                 own[:, b.par, part, :], ALU.add))

            def step(b):
                if b.within(NB):
                    message_sums(b)
                if b.ago(1).within(NB):
                    finish(b.ago(1))

            sweep(dve, step, lag=1)
            dve.wait_ge(over, 1)
            dve.wait_ge(first_in, 16)
            dve.wait_ge(sent[1], 16 * U * uses(NB, 1))
            dve.wait_ge(state, sums.per * NB)
            dve.tensor_tensor(states[:, 1, 0, :], over_ps[:, :], head[:, :], ALU.add).then_inc(cleared, 1)
            dve.wait_ge(mixed, NB + 1)
            dve.tensor_tensor(result[:, 1, 0, :], mixed_ps[:, 0, 0:C], own_first[:, :], ALU.add).then_inc(cleared, 1)


_OUT = ("out_0", (N, C))


def kernel(**inputs):
    import concourse.bacc as _bacc
    from concourse.bass_utils import run_bass_kernel_spmd as _run

    nc = _bacc.Bacc("TRN2", target_bir_lowering=False, num_devices=1)
    arrays, A = {}, {}
    for name, value in inputs.items():
        a = np.ascontiguousarray(value)
        arrays[f"in_{name}"] = a
        A[name] = nc.dram_tensor(f"in_{name}", a.shape, mybir.dt.from_np(a.dtype), kind="ExternalInput").ap()
    out = nc.dram_tensor(_OUT[0], _OUT[1], F32, kind="ExternalOutput").ap()
    build(nc, A, out)
    r = _run(nc, [arrays], core_ids=[0])
    return r.results[0][_OUT[0]]
```
